# Optimizing a Trainium2 kernel written in Bass

```python
import numpy as np
import jax
import jax.numpy as jnp

def _softmax(x, axis=-1):
    return jax.nn.softmax(x, axis=axis)

def _gelu(x):
    return jax.nn.gelu(x, approximate=True)

def _silu(x):
    return jax.nn.silu(x)

def _sigmoid(x):
    return jax.nn.sigmoid(x)

def _layernorm(x, axis=-1, eps=1e-05):
    m = jnp.mean(x, axis=axis, keepdims=True)
    v = jnp.var(x, axis=axis, keepdims=True)
    return (x - m) / jnp.sqrt(v + eps)

def _scatter_add(tgt, idx, src, axis=0):
    return tgt.at[idx].add(src)

def _segment_sum(src, seg, n):
    return jax.ops.segment_sum(src, seg, n)
kernel_name = 'mk_decoder_preln_d4_seqx_r4_be1b2a'

def setup_inputs(seed: int=0):
    np.random.seed(seed)
    _w = jnp.asarray

    def _rec_inputs():
        import jax
        import jax.numpy as jnp
        _rk = jax.random.key(seed)
        x = -0.0002928 + 1 * jax.random.normal(jax.random.fold_in(_rk, 1), (4, 512, 256), jnp.float32)
        _lenS = 512 - jax.random.randint(jax.random.fold_in(_rk, 7), (4,), 0, max(1, 512 // 4) + 1, jnp.int32)
        _lenS2 = 64 - jax.random.randint(jax.random.fold_in(_rk, 8), (4,), 0, max(1, 64 // 4) + 1, jnp.int32)
        _ctx_1024P = jax.random.normal(jax.random.fold_in(_rk, 11), (4, 16, 256), jnp.float32)
        _ctx_1024c = jax.random.dirichlet(jax.random.fold_in(_rk, 511), 0.3 * jnp.ones((16,), jnp.float32), (4, 64))
        _ctx_1024t = jnp.einsum('bsk,bkd->bsd', _ctx_1024c, _ctx_1024P)
        _ctx_1024t = _ctx_1024t * jax.lax.rsqrt(jnp.mean(jnp.square(_ctx_1024t)) + 1e-12) * 0.953939
        ctx_1024 = -1.39393e-06 + 0.999914 * (_ctx_1024t + 0.3 * jax.random.normal(jax.random.fold_in(_rk, 611), (4, 64, 256), jnp.float32))
        fside_BxS2_0 = jax.random.uniform(jax.random.fold_in(_rk, 12), (4, 64), jnp.float32, 0.0, 0.999833)
        _validS = jnp.arange(512)[None, :] < _lenS[:, None]
        _validS2 = jnp.arange(64)[None, :] < _lenS2[:, None]
        _causal = jnp.tril(jnp.ones((512, 512), dtype=bool))
        mask_BxS2_bf1 = jnp.ones((4, 64), dtype=bool)
        mask_BxS2_bk0 = jnp.logical_not(jnp.broadcast_to(_validS2[:, :], (4, 64)))
        return (x, ctx_1024, fside_BxS2_0, mask_BxS2_bf1, mask_BxS2_bk0)
    x, ctx_1024, fside_BxS2_0, mask_BxS2_bf1, mask_BxS2_bk0 = _rec_inputs()

    def _L0_attn_setup():
        import jax, jax.numpy as jnp
        import numpy as np
        LN_EPS = 1e-05

        def _layernorm(x, g, b):
            m = jnp.mean(x, axis=-1, keepdims=True)
            v = jnp.mean((x - m) ** 2, axis=-1, keepdims=True)
            return (x - m) / jnp.sqrt(v + LN_EPS) * g + b

        def _eigenstate_fft(log_decay, frequency, beta_r, beta_i):
            B, T, K = beta_r.shape
            mag = jax.nn.sigmoid(log_decay)
            n = jnp.arange(T, dtype=beta_r.dtype)
            mag_pow = mag[None, :] ** n[:, None]
            phase = n[:, None] * frequency[None, :]
            kern = mag_pow * (jnp.cos(phase) + 1j * jnp.sin(phase))
            beta = beta_r + 1j * beta_i
            beta_p = jnp.pad(beta, ((0, 0), (0, T), (0, 0)))
            kern_p = jnp.pad(kern, ((0, T), (0, 0)))
            c = jnp.fft.ifft(jnp.fft.fft(beta_p, axis=1) * jnp.fft.fft(kern_p, axis=0)[None], axis=1)[:, :T, :]
            return (c.real.astype(beta_r.dtype), c.imag.astype(beta_r.dtype))

        def _reference_tuple_inner(x, in_proj_w, log_decay, frequency, coupling, out_proj_w, gate_w, gate_b, n1_g, n1_b, n2_g, n2_b, mlp_w1, mlp_b1, mlp_w2, mlp_b2):
            B, T, D = x.shape
            H, Kh, _ = coupling.shape
            K = H * Kh
            xn = _layernorm(x, n1_g, n1_b)
            beta = jnp.einsum('btd,kd->btk', xn, in_proj_w)
            br, bi = (beta[..., :K], beta[..., K:])
            cr, ci = _eigenstate_fft(log_decay, frequency, br, bi)
            cr_h = cr.reshape(B, T, H, Kh)
            ci_h = ci.reshape(B, T, H, Kh)
            cr = jnp.einsum('hjk,bthk->bthj', coupling, cr_h).reshape(B, T, K)
            ci = jnp.einsum('hjk,bthk->bthj', coupling, ci_h).reshape(B, T, K)
            eig = jnp.concatenate([cr, ci], axis=-1)
            out = jnp.einsum('btk,dk->btd', eig, out_proj_w)
            h = jax.nn.sigmoid(jnp.einsum('btd,ed->bte', xn, gate_w) + gate_b) * out
            x = x + h
            x2 = _layernorm(x, n2_g, n2_b)
            hid = jax.nn.silu(jnp.einsum('btd,md->btm', x2, mlp_w1) + mlp_b1)
            x = x + jnp.einsum('btm,dm->btd', hid, mlp_w2) + mlp_b2
            return (x, eig)
        key = jax.random.key(seed)
        ks = jax.random.split(key, 12)
        B, T, D, K, H = (4, 1024, 256, 64, 4)
        Kh = K // H
        M = 4 * D
        f32 = jnp.float32
        inp = {'x': jax.random.normal(ks[0], (B, T, D), f32), 'in_proj_w': jax.random.normal(ks[1], (2 * K, D), f32) / np.sqrt(D), 'log_decay': jax.random.uniform(ks[2], (K,), f32, -3.0, -0.1), 'frequency': jnp.linspace(0.0, 2 * np.pi * (1 - 1.0 / K), K, dtype=f32), 'coupling': jnp.eye(Kh, dtype=f32)[None] + 0.01 * jax.random.normal(ks[3], (H, Kh, Kh), f32) / np.sqrt(Kh), 'out_proj_w': jax.random.normal(ks[4], (D, 2 * K), f32) / np.sqrt(2 * K), 'gate_w': jax.random.normal(ks[5], (D, D), f32) / np.sqrt(D), 'gate_b': jnp.full((D,), -2.0, f32), 'n1_g': jnp.ones((D,), f32), 'n1_b': jnp.zeros((D,), f32), 'n2_g': jnp.ones((D,), f32), 'n2_b': jnp.zeros((D,), f32), 'mlp_w1': jax.random.normal(ks[6], (M, D), f32) / np.sqrt(D), 'mlp_b1': jnp.zeros((M,), f32), 'mlp_w2': jax.random.normal(ks[7], (D, M), f32) / np.sqrt(M), 'mlp_b2': jnp.zeros((D,), f32)}
        return inp
    _L0_attn_all = _L0_attn_setup()
    _L0_attn_in = {k: v for k, v in _L0_attn_all.items() if k in ('in_proj_w', 'log_decay', 'frequency', 'coupling', 'out_proj_w', 'gate_w', 'gate_b', 'n1_g', 'n1_b', 'n2_g', 'n2_b', 'mlp_w1', 'mlp_b1', 'mlp_w2', 'mlp_b2')}
    del _L0_attn_all

    def _L0_xattn_setup():
        import jax, jax.numpy as jnp
        import numpy as np
        D_MODEL = 256
        N_HEADS = 16
        D_K = D_MODEL // N_HEADS

        def _split_heads(x):
            B, S, _ = x.shape
            return x.reshape(B, S, N_HEADS, D_K).transpose(0, 2, 1, 3)
        key = jax.random.key(seed)
        ks = jax.random.split(key, 12)
        B, S = (2, 512)
        scale = 1.0 / np.sqrt(D_MODEL)
        inp = {'query': jax.random.normal(ks[0], (B, S, D_MODEL), jnp.float32), 'key': jax.random.normal(ks[1], (B, S, D_MODEL), jnp.float32), 'value': jax.random.normal(ks[2], (B, S, D_MODEL), jnp.float32), 'weights': jax.random.uniform(ks[3], (B, S), jnp.float32), 'wq': jax.random.normal(ks[4], (D_MODEL, D_MODEL), jnp.float32) * scale, 'bq': jnp.zeros((D_MODEL,), jnp.float32), 'wk': jax.random.normal(ks[5], (D_MODEL, D_MODEL), jnp.float32) * scale, 'bk': jnp.zeros((D_MODEL,), jnp.float32), 'wv': jax.random.normal(ks[6], (D_MODEL, D_MODEL), jnp.float32) * scale, 'bv': jnp.zeros((D_MODEL,), jnp.float32), 'wo': jax.random.normal(ks[7], (D_MODEL, D_MODEL), jnp.float32) * scale, 'bo': jnp.zeros((D_MODEL,), jnp.float32)}
        return inp
    _L0_xattn_all = _L0_xattn_setup()
    _L0_xattn_in = {k: v for k, v in _L0_xattn_all.items() if k in ('wq', 'bq', 'wk', 'bk', 'wv', 'bv', 'wo', 'bo')}
    del _L0_xattn_all

    def _L0_ffn_setup():
        import jax, jax.numpy as jnp
        import numpy as np
        LN_EPS = 1e-05

        def layer_norm(x, g, b):
            mu = jnp.mean(x, axis=-1, keepdims=True)
            var = jnp.mean(jnp.square(x - mu), axis=-1, keepdims=True)
            return (x - mu) * jax.lax.rsqrt(var + LN_EPS) * g + b

        def ternary_quant(w):
            scale = 1.0 / jnp.clip(jnp.mean(jnp.abs(w)), 1e-05)
            wq = jnp.clip(jnp.round(w * scale), -1.0, 1.0) / scale
            return w + jax.lax.stop_gradient(wq - w)
        key = jax.random.key(seed)
        ks = jax.random.split(key, 3)
        dim, hidden = (256, 1024)
        B, S = (8, 256)
        x = jax.random.normal(ks[0], (B, S, dim), dtype=jnp.float32)
        w1 = jax.random.normal(ks[1], (hidden, dim), dtype=jnp.float32) * 0.02
        w2 = jax.random.normal(ks[2], (dim, hidden), dtype=jnp.float32) * 0.02
        return {'x': x, 'ln1_g': jnp.ones((dim,), jnp.float32), 'ln1_b': jnp.zeros((dim,), jnp.float32), 'w1': w1, 'b1': jnp.zeros((hidden,), jnp.float32), 'ln2_g': jnp.ones((hidden,), jnp.float32), 'ln2_b': jnp.zeros((hidden,), jnp.float32), 'w2': w2, 'b2': jnp.zeros((dim,), jnp.float32)}
    _L0_ffn_all = _L0_ffn_setup()
    _L0_ffn_in = {k: v for k, v in _L0_ffn_all.items() if k in ('ln1_g', 'ln1_b', 'w1', 'b1', 'ln2_g', 'ln2_b', 'w2', 'b2')}
    del _L0_ffn_all

    def _L1_attn_setup():
        import jax, jax.numpy as jnp
        import numpy as np
        B, T, D, S = (8, 1024, 256, 128)
        EPS = 1e-05

        def _gla(x, Wq, bq, Wk, bk, Wv, bv, Wg, bg, Wo, bo, gamma, beta):
            q = x @ Wq + bq
            k = x @ Wk + bk
            v = x @ Wv + bv
            g = jax.nn.sigmoid(x @ Wg + bg)

            def step(state, qkvg):
                qt, kt, vt, gt = qkvg
                state = gt[:, :, None] * state + kt[:, :, None] * vt[:, None, :]
                out = jnp.einsum('bs,bst->bt', qt, state)
                return (state, out)
            init = jnp.zeros((x.shape[0], Wq.shape[1], Wq.shape[1]), x.dtype)
            seq = (q.transpose(1, 0, 2), k.transpose(1, 0, 2), v.transpose(1, 0, 2), g.transpose(1, 0, 2))
            _, outs = jax.lax.scan(step, init, seq)
            out = outs.transpose(1, 0, 2)
            y = x + out @ Wo + bo
            mu = jnp.mean(y, axis=-1, keepdims=True)
            var = jnp.mean(jnp.square(y - mu), axis=-1, keepdims=True)
            return (y - mu) * jax.lax.rsqrt(var + EPS) * gamma + beta
        key = jax.random.key(seed)
        ks = jax.random.split(key, 12)
        sD = 1.0 / np.sqrt(D)
        sS = 1.0 / np.sqrt(S)
        return {'x': jax.random.normal(ks[0], (B, T, D), jnp.float32), 'Wq': jax.random.normal(ks[1], (D, S), jnp.float32) * sD, 'bq': jnp.zeros((S,), jnp.float32), 'Wk': jax.random.normal(ks[2], (D, S), jnp.float32) * sD, 'bk': jnp.zeros((S,), jnp.float32), 'Wv': jax.random.normal(ks[3], (D, S), jnp.float32) * sD, 'bv': jnp.zeros((S,), jnp.float32), 'Wg': jax.random.normal(ks[4], (D, S), jnp.float32) * sD, 'bg': jnp.zeros((S,), jnp.float32), 'Wo': jax.random.normal(ks[5], (S, D), jnp.float32) * sS, 'bo': jnp.zeros((D,), jnp.float32), 'gamma': jnp.ones((D,), jnp.float32), 'beta': jnp.zeros((D,), jnp.float32)}
    _L1_attn_all = _L1_attn_setup()
    _L1_attn_in = {k: v for k, v in _L1_attn_all.items() if k in ('Wq', 'bq', 'Wk', 'bk', 'Wv', 'bv', 'Wg', 'bg', 'Wo', 'bo', 'gamma', 'beta')}
    del _L1_attn_all

    def _L1_xattn_setup():
        import jax, jax.numpy as jnp
        import numpy as np
        EPS = 1e-05

        def layer_norm(x, g, b):
            mu = jnp.mean(x, axis=-1, keepdims=True)
            var = jnp.var(x, axis=-1, keepdims=True)
            return (x - mu) * jax.lax.rsqrt(var + EPS) * g + b
        key = jax.random.key(seed)
        ks = jax.random.split(key, 8)
        dim, heads, dim_head = (256, 16, 64)
        inner = heads * dim_head
        b, n, m = (8, 1024, 64)
        s = dim ** (-0.5)
        return {'x': jax.random.normal(ks[0], (b, n, dim), jnp.float32), 'latents': jax.random.normal(ks[1], (b, m, dim), jnp.float32), 'ln_m_g': jnp.ones((dim,), jnp.float32), 'ln_m_b': jnp.zeros((dim,), jnp.float32), 'ln_l_g': jnp.ones((dim,), jnp.float32), 'ln_l_b': jnp.zeros((dim,), jnp.float32), 'Wq': jax.random.normal(ks[2], (dim, inner), jnp.float32) * s, 'Wkv': jax.random.normal(ks[3], (dim, 2 * inner), jnp.float32) * s, 'Wout': jax.random.normal(ks[4], (inner, dim), jnp.float32) * s}
    _L1_xattn_all = _L1_xattn_setup()
    _L1_xattn_in = {k: v for k, v in _L1_xattn_all.items() if k in ('ln_m_g', 'ln_m_b', 'ln_l_g', 'ln_l_b', 'Wq', 'Wkv', 'Wout')}
    del _L1_xattn_all

    def _L1_ffn_setup():
        import jax, jax.numpy as jnp
        import numpy as np
        H = 8
        QD = 64
        HALF = QD // 2
        DIMS = (32, 32)
        TOPK = 16
        DTK = 4
        EPS_BN = 1e-05
        EPS_NORM = 1e-12

        def _l2norm(x):
            n = jnp.linalg.norm(x, axis=-1, keepdims=True)
            return x / jnp.maximum(n, EPS_NORM)
        key = jax.random.key(seed)
        ks = jax.random.split(key, 6)
        B, S, D, O, E = (2, 128, 256, 256, 256)
        hidden_states = jax.random.normal(ks[0], (B, S, D), jnp.float32)
        Wq = jax.random.normal(ks[1], (D, H * QD), jnp.float32) * 0.02
        bq = jnp.zeros((H * QD,), jnp.float32)
        bn_gamma = jnp.ones((QD,), jnp.float32)
        bn_beta = jnp.zeros((QD,), jnp.float32)
        sub_key0 = jax.random.normal(ks[2], (DIMS[0], HALF), jnp.float32) * 0.02
        sub_key1 = jax.random.normal(ks[3], (DIMS[1], HALF), jnp.float32) * 0.02
        expert_down = jax.random.normal(ks[4], (E, D), jnp.float32) * 0.02
        expert_up = jax.random.normal(ks[5], (E, O), jnp.float32) * 0.02
        return {'hidden_states': hidden_states, 'Wq': Wq, 'bq': bq, 'bn_gamma': bn_gamma, 'bn_beta': bn_beta, 'sub_key0': sub_key0, 'sub_key1': sub_key1, 'expert_down': expert_down, 'expert_up': expert_up}
    _L1_ffn_all = _L1_ffn_setup()
    _L1_ffn_in = {k: v for k, v in _L1_ffn_all.items() if k in ('Wq', 'bq', 'bn_gamma', 'bn_beta', 'sub_key0', 'sub_key1', 'expert_down', 'expert_up')}
    del _L1_ffn_all

    def _L2_attn_setup():
        import jax, jax.numpy as jnp
        import numpy as np
        CHUNK = 64
        HEADS = 16

        def _chunk_mask(T, cs):
            idx = jnp.arange(T)
            blk = idx // cs * cs
            qb = blk[:, None]
            kb = blk[None, :]
            masked = (qb >= kb) & (idx[None, :] - idx[:, None] - 2 * (kb - qb) >= 1)
            return masked
        key = jax.random.key(seed)
        ks = jax.random.split(key, 6)
        B, T, C = (2, 512, 256)
        w = 0.02
        return {'x': jax.random.normal(ks[0], (B, T, C), jnp.float32), 'Wq': jax.random.normal(ks[1], (C, C), jnp.float32) * w, 'bq': jnp.zeros((C,), jnp.float32), 'Wk': jax.random.normal(ks[2], (C, C), jnp.float32) * w, 'bk': jnp.zeros((C,), jnp.float32), 'Wv': jax.random.normal(ks[3], (C, C), jnp.float32) * w, 'bv': jnp.zeros((C,), jnp.float32), 'Wo': jax.random.normal(ks[4], (C, C), jnp.float32) * w, 'bo': jnp.zeros((C,), jnp.float32), 'attn_scale': jnp.full((1,), 1.0 / np.sqrt(C // HEADS), jnp.float32)}
    _L2_attn_all = _L2_attn_setup()
    _L2_attn_in = {k: v for k, v in _L2_attn_all.items() if k in ('Wq', 'bq', 'Wk', 'bk', 'Wv', 'bv', 'Wo', 'bo', 'attn_scale')}
    del _L2_attn_all

    def _L2_xattn_setup():
        import jax, jax.numpy as jnp
        import numpy as np
        DIM = 256
        DIM_LATENT = 256
        DIM_HEAD = 64
        HEADS = 16
        INNER = HEADS * DIM_HEAD

        def layernorm(x, g, b, eps=1e-05):
            m = jnp.mean(x, axis=-1, keepdims=True)
            v = jnp.mean((x - m) ** 2, axis=-1, keepdims=True)
            return (x - m) / jnp.sqrt(v + eps) * g + b

        def rmsnorm(x, gamma, eps=1e-08):
            n = jnp.linalg.norm(x, axis=-1, keepdims=True) * x.shape[-1] ** (-0.5)
            return x / jnp.maximum(n, eps) * gamma
        key = jax.random.key(seed)
        ks = jax.random.split(key, 8)
        b, n, m = (4, 1024, 128)
        x = jax.random.normal(ks[0], (b, n, DIM), dtype=jnp.float32)
        latents = jax.random.normal(ks[1], (b, m, DIM_LATENT), dtype=jnp.float32)
        mask = jnp.ones((b, n), dtype=bool)
        s = 0.02
        return {'x': x, 'latents': latents, 'mask': mask, 'ln_x_g': jnp.ones((DIM,), jnp.float32), 'ln_x_b': jnp.zeros((DIM,), jnp.float32), 'ln_l_g': jnp.ones((DIM_LATENT,), jnp.float32), 'ln_l_b': jnp.zeros((DIM_LATENT,), jnp.float32), 'qn_g': jnp.ones((DIM_HEAD,), jnp.float32), 'kn_g': jnp.ones((DIM_HEAD,), jnp.float32), 'Wq': jax.random.normal(ks[2], (DIM_LATENT, INNER), jnp.float32) * s, 'Wkv': jax.random.normal(ks[3], (DIM, 2 * INNER), jnp.float32) * s, 'Wout': jax.random.normal(ks[4], (INNER, DIM_LATENT), jnp.float32) * s, 'bout': jnp.zeros((DIM_LATENT,), jnp.float32)}
    _L2_xattn_all = _L2_xattn_setup()
    _L2_xattn_in = {k: v for k, v in _L2_xattn_all.items() if k in ('ln_x_g', 'ln_x_b', 'ln_l_g', 'ln_l_b', 'qn_g', 'kn_g', 'Wq', 'Wkv', 'Wout', 'bout')}
    del _L2_xattn_all

    def _L2_ffn_setup():
        import jax, jax.numpy as jnp
        import numpy as np
        N_EMBD = 256
        EXPERT_SIZES = [(4, 256), (4, 512)]
        TOP_K = 2
        B, S = (1, 512)
        WIDTHS = []
        for count, size in EXPERT_SIZES:
            WIDTHS += [size] * count
        OFFSETS = np.concatenate([[0], np.cumsum(WIDTHS)]).astype(np.int64)
        E = len(WIDTHS)
        TOTAL_W = int(OFFSETS[-1])
        MAX_W = max(WIDTHS)

        def _stack_experts(w1, w2):
            W1e, W2e = ([], [])
            for e in range(E):
                off, wd = (int(OFFSETS[e]), WIDTHS[e])
                pad = MAX_W - wd
                W1e.append(jnp.pad(w1[:, off:off + wd], ((0, 0), (0, pad))))
                W2e.append(jnp.pad(w2[off:off + wd, :], ((0, pad), (0, 0))))
            return (jnp.stack(W1e), jnp.stack(W2e))
        key = jax.random.key(seed)
        k1, k2, k3, k4 = jax.random.split(key, 4)
        x = jax.random.normal(k1, (B, S, N_EMBD), jnp.float32)
        router_w = jax.random.normal(k2, (E, N_EMBD), jnp.float32) * 0.02
        w1 = jax.random.truncated_normal(k3, -3.0, 3.0, (N_EMBD, TOTAL_W), jnp.float32) * 0.02
        w2 = jax.random.truncated_normal(k4, -3.0, 3.0, (TOTAL_W, N_EMBD), jnp.float32) * 0.02
        return {'x': x, 'router_w': router_w, 'w1': w1, 'w2': w2}
    _L2_ffn_all = _L2_ffn_setup()
    _L2_ffn_in = {k: v for k, v in _L2_ffn_all.items() if k in ('router_w', 'w1', 'w2')}
    del _L2_ffn_all

    def _L3_attn_setup():
        import jax, jax.numpy as jnp
        import numpy as np
        D_MODEL = 256
        N_HEADS = 16
        D_K = D_MODEL // N_HEADS
        MAX_REL = 128
        SEQ = 256
        BATCH = 4

        def _relative_positions(seq_len: int) -> jnp.ndarray:
            pos = jnp.arange(seq_len)
            rel = pos[:, None] - pos[None, :]
            rel = jnp.clip(rel, -MAX_REL, MAX_REL) + MAX_REL
            return rel
        key = jax.random.key(seed)
        ks = jax.random.split(key, 8)
        x = jax.random.normal(ks[0], (SEQ, BATCH, D_MODEL), dtype=jnp.float32)
        w_q = jax.random.normal(ks[1], (D_MODEL, D_MODEL), dtype=jnp.float32) * (1.0 / np.sqrt(D_MODEL))
        w_k = jax.random.normal(ks[2], (D_MODEL, D_MODEL), dtype=jnp.float32) * (1.0 / np.sqrt(D_MODEL))
        w_v = jax.random.normal(ks[3], (D_MODEL, D_MODEL), dtype=jnp.float32) * (1.0 / np.sqrt(D_MODEL))
        w_o = jax.random.normal(ks[4], (D_MODEL, D_MODEL), dtype=jnp.float32) * (1.0 / np.sqrt(D_MODEL))
        b_o = jnp.zeros((D_MODEL,), dtype=jnp.float32)
        rel_k = jax.random.normal(ks[5], (2 * MAX_REL + 1, D_K), dtype=jnp.float32)
        rel_v = jax.random.normal(ks[6], (2 * MAX_REL + 1, D_K), dtype=jnp.float32)
        return {'x': x, 'w_q': w_q, 'w_k': w_k, 'w_v': w_v, 'w_o': w_o, 'b_o': b_o, 'rel_k': rel_k, 'rel_v': rel_v}
    _L3_attn_all = _L3_attn_setup()
    _L3_attn_in = {k: v for k, v in _L3_attn_all.items() if k in ('w_q', 'w_k', 'w_v', 'w_o', 'b_o', 'rel_k', 'rel_v')}
    del _L3_attn_all

    def _L3_xattn_setup():
        import jax, jax.numpy as jnp
        import numpy as np
        DIM, DIM_HEAD, HEADS, SCALE = (256, 64, 8, 8.0)
        INNER = DIM_HEAD * HEADS
        LN_EPS = 1e-05
        L2_EPS = 1e-12

        def layer_norm(x, w, b):
            mu = jnp.mean(x, axis=-1, keepdims=True)
            var = jnp.mean(jnp.square(x - mu), axis=-1, keepdims=True)
            return (x - mu) * jax.lax.rsqrt(var + LN_EPS) * w + b

        def l2norm(t):
            n = jnp.sqrt(jnp.sum(jnp.square(t), axis=-1, keepdims=True))
            return t / jnp.maximum(n, L2_EPS)
        key = jax.random.key(seed)
        ks = jax.random.split(key, 8)
        b, n, m = (8, 2048, 64)
        x = jax.random.normal(ks[0], (b, n, DIM), dtype=jnp.float32)
        latents = jax.random.normal(ks[1], (b, m, DIM), dtype=jnp.float32)
        mask = jax.random.randint(ks[2], (b, n), 0, 2) > 0
        Wq = jax.random.normal(ks[3], (DIM, INNER), dtype=jnp.float32) * DIM ** (-0.5)
        Wkv = jax.random.normal(ks[4], (DIM, 2 * INNER), dtype=jnp.float32) * DIM ** (-0.5)
        Wo = jax.random.normal(ks[5], (INNER, DIM), dtype=jnp.float32) * INNER ** (-0.5)
        return {'x': x, 'latents': latents, 'mask': mask, 'ln_x_w': jnp.ones((DIM,)), 'ln_x_b': jnp.zeros((DIM,)), 'ln_l_w': jnp.ones((DIM,)), 'ln_l_b': jnp.zeros((DIM,)), 'Wq': Wq, 'Wkv': Wkv, 'q_scale': jnp.ones((DIM_HEAD,)), 'k_scale': jnp.ones((DIM_HEAD,)), 'Wo': Wo, 'ln_o_w': jnp.ones((DIM,)), 'ln_o_b': jnp.zeros((DIM,))}
    _L3_xattn_all = _L3_xattn_setup()
    _L3_xattn_in = {k: v for k, v in _L3_xattn_all.items() if k in ('ln_x_w', 'ln_x_b', 'ln_l_w', 'ln_l_b', 'Wq', 'Wkv', 'q_scale', 'k_scale', 'Wo', 'ln_o_w', 'ln_o_b')}
    del _L3_xattn_all

    def _L3_ffn_setup():
        import jax, jax.numpy as jnp
        import numpy as np
        B, S, H, DFF, E, K = (2, 512, 256, 512, 8, 2)

        def _moe(x, Wg, W1, b1, W2, b2, W3, b3):
            Bm, Sm, Hm = x.shape
            xt = x.reshape(-1, Hm)
            gout = xt @ Wg.T
            topv, topi = jax.lax.top_k(gout, K)
            w = jax.nn.softmax(topv, axis=-1)
            comb = jnp.einsum('tke,tk->te', jax.nn.one_hot(topi, E, dtype=x.dtype), w)
            g = jnp.einsum('th,efh->etf', xt, W1) + b1[:, None, :]
            v = jnp.einsum('th,efh->etf', xt, W2) + b2[:, None, :]
            h = jax.nn.silu(g) * v
            eo = jnp.einsum('etf,ehf->eth', h, W3) + b3[:, None, :]
            out = jnp.einsum('eth,te->th', eo, comb)
            return out.reshape(Bm, Sm, Hm)
        key = jax.random.key(seed)
        ks = jax.random.split(key, 8)
        sc_h = 1.0 / np.sqrt(H)
        sc_f = 1.0 / np.sqrt(DFF)
        x = jax.random.normal(ks[0], (B, S, H), dtype=jnp.float32)
        Wg = jax.random.uniform(ks[1], (E, H), jnp.float32, -sc_h, sc_h)
        W1 = jax.random.uniform(ks[2], (E, DFF, H), jnp.float32, -sc_h, sc_h)
        b1 = jax.random.uniform(ks[3], (E, DFF), jnp.float32, -sc_h, sc_h)
        W2 = jax.random.uniform(ks[4], (E, DFF, H), jnp.float32, -sc_h, sc_h)
        b2 = jax.random.uniform(ks[5], (E, DFF), jnp.float32, -sc_h, sc_h)
        W3 = jax.random.uniform(ks[6], (E, H, DFF), jnp.float32, -sc_f, sc_f)
        b3 = jax.random.uniform(ks[7], (E, H), jnp.float32, -sc_f, sc_f)
        return {'x': x, 'Wg': Wg, 'W1': W1, 'b1': b1, 'W2': W2, 'b2': b2, 'W3': W3, 'b3': b3}
    _L3_ffn_all = _L3_ffn_setup()
    _L3_ffn_in = {k: v for k, v in _L3_ffn_all.items() if k in ('Wg', 'W1', 'b1', 'W2', 'b2', 'W3', 'b3')}
    del _L3_ffn_all
    return {'x': x, 'ctx_1024': ctx_1024, 'fside_BxS2_0': fside_BxS2_0, 'mask_BxS2_bf1': mask_BxS2_bf1, 'mask_BxS2_bk0': mask_BxS2_bk0, 'L0_attn_in_proj_w': _L0_attn_in['in_proj_w'], 'L0_attn_log_decay': _L0_attn_in['log_decay'], 'L0_attn_frequency': _L0_attn_in['frequency'], 'L0_attn_coupling': _L0_attn_in['coupling'], 'L0_attn_out_proj_w': _L0_attn_in['out_proj_w'], 'L0_attn_gate_w': _L0_attn_in['gate_w'], 'L0_attn_gate_b': _L0_attn_in['gate_b'], 'L0_attn_n1_g': _L0_attn_in['n1_g'], 'L0_attn_n1_b': _L0_attn_in['n1_b'], 'L0_attn_n2_g': _L0_attn_in['n2_g'], 'L0_attn_n2_b': _L0_attn_in['n2_b'], 'L0_attn_mlp_w1': _L0_attn_in['mlp_w1'], 'L0_attn_mlp_b1': _L0_attn_in['mlp_b1'], 'L0_attn_mlp_w2': _L0_attn_in['mlp_w2'], 'L0_attn_mlp_b2': _L0_attn_in['mlp_b2'], 'L0_xattn_wq': _L0_xattn_in['wq'], 'L0_xattn_bq': _L0_xattn_in['bq'], 'L0_xattn_wk': _L0_xattn_in['wk'], 'L0_xattn_bk': _L0_xattn_in['bk'], 'L0_xattn_wv': _L0_xattn_in['wv'], 'L0_xattn_bv': _L0_xattn_in['bv'], 'L0_xattn_wo': _L0_xattn_in['wo'], 'L0_xattn_bo': _L0_xattn_in['bo'], 'L0_ffn_ln1_g': _L0_ffn_in['ln1_g'], 'L0_ffn_ln1_b': _L0_ffn_in['ln1_b'], 'L0_ffn_w1': _L0_ffn_in['w1'], 'L0_ffn_b1': _L0_ffn_in['b1'], 'L0_ffn_ln2_g': _L0_ffn_in['ln2_g'], 'L0_ffn_ln2_b': _L0_ffn_in['ln2_b'], 'L0_ffn_w2': _L0_ffn_in['w2'], 'L0_ffn_b2': _L0_ffn_in['b2'], 'L1_attn_Wq': _L1_attn_in['Wq'], 'L1_attn_bq': _L1_attn_in['bq'], 'L1_attn_Wk': _L1_attn_in['Wk'], 'L1_attn_bk': _L1_attn_in['bk'], 'L1_attn_Wv': _L1_attn_in['Wv'], 'L1_attn_bv': _L1_attn_in['bv'], 'L1_attn_Wg': _L1_attn_in['Wg'], 'L1_attn_bg': _L1_attn_in['bg'], 'L1_attn_Wo': _L1_attn_in['Wo'], 'L1_attn_bo': _L1_attn_in['bo'], 'L1_attn_gamma': _L1_attn_in['gamma'], 'L1_attn_beta': _L1_attn_in['beta'], 'L1_xattn_ln_m_g': _L1_xattn_in['ln_m_g'], 'L1_xattn_ln_m_b': _L1_xattn_in['ln_m_b'], 'L1_xattn_ln_l_g': _L1_xattn_in['ln_l_g'], 'L1_xattn_ln_l_b': _L1_xattn_in['ln_l_b'], 'L1_xattn_Wq': _L1_xattn_in['Wq'], 'L1_xattn_Wkv': _L1_xattn_in['Wkv'], 'L1_xattn_Wout': _L1_xattn_in['Wout'], 'L1_ffn_Wq': _L1_ffn_in['Wq'], 'L1_ffn_bq': _L1_ffn_in['bq'], 'L1_ffn_bn_gamma': _L1_ffn_in['bn_gamma'], 'L1_ffn_bn_beta': _L1_ffn_in['bn_beta'], 'L1_ffn_sub_key0': _L1_ffn_in['sub_key0'], 'L1_ffn_sub_key1': _L1_ffn_in['sub_key1'], 'L1_ffn_expert_down': _L1_ffn_in['expert_down'], 'L1_ffn_expert_up': _L1_ffn_in['expert_up'], 'L2_attn_Wq': _L2_attn_in['Wq'], 'L2_attn_bq': _L2_attn_in['bq'], 'L2_attn_Wk': _L2_attn_in['Wk'], 'L2_attn_bk': _L2_attn_in['bk'], 'L2_attn_Wv': _L2_attn_in['Wv'], 'L2_attn_bv': _L2_attn_in['bv'], 'L2_attn_Wo': _L2_attn_in['Wo'], 'L2_attn_bo': _L2_attn_in['bo'], 'L2_attn_attn_scale': _L2_attn_in['attn_scale'], 'L2_xattn_ln_x_g': _L2_xattn_in['ln_x_g'], 'L2_xattn_ln_x_b': _L2_xattn_in['ln_x_b'], 'L2_xattn_ln_l_g': _L2_xattn_in['ln_l_g'], 'L2_xattn_ln_l_b': _L2_xattn_in['ln_l_b'], 'L2_xattn_qn_g': _L2_xattn_in['qn_g'], 'L2_xattn_kn_g': _L2_xattn_in['kn_g'], 'L2_xattn_Wq': _L2_xattn_in['Wq'], 'L2_xattn_Wkv': _L2_xattn_in['Wkv'], 'L2_xattn_Wout': _L2_xattn_in['Wout'], 'L2_xattn_bout': _L2_xattn_in['bout'], 'L2_ffn_router_w': _L2_ffn_in['router_w'], 'L2_ffn_w1': _L2_ffn_in['w1'], 'L2_ffn_w2': _L2_ffn_in['w2'], 'L3_attn_w_q': _L3_attn_in['w_q'], 'L3_attn_w_k': _L3_attn_in['w_k'], 'L3_attn_w_v': _L3_attn_in['w_v'], 'L3_attn_w_o': _L3_attn_in['w_o'], 'L3_attn_b_o': _L3_attn_in['b_o'], 'L3_attn_rel_k': _L3_attn_in['rel_k'], 'L3_attn_rel_v': _L3_attn_in['rel_v'], 'L3_xattn_ln_x_w': _L3_xattn_in['ln_x_w'], 'L3_xattn_ln_x_b': _L3_xattn_in['ln_x_b'], 'L3_xattn_ln_l_w': _L3_xattn_in['ln_l_w'], 'L3_xattn_ln_l_b': _L3_xattn_in['ln_l_b'], 'L3_xattn_Wq': _L3_xattn_in['Wq'], 'L3_xattn_Wkv': _L3_xattn_in['Wkv'], 'L3_xattn_q_scale': _L3_xattn_in['q_scale'], 'L3_xattn_k_scale': _L3_xattn_in['k_scale'], 'L3_xattn_Wo': _L3_xattn_in['Wo'], 'L3_xattn_ln_o_w': _L3_xattn_in['ln_o_w'], 'L3_xattn_ln_o_b': _L3_xattn_in['ln_o_b'], 'L3_ffn_Wg': _L3_ffn_in['Wg'], 'L3_ffn_W1': _L3_ffn_in['W1'], 'L3_ffn_b1': _L3_ffn_in['b1'], 'L3_ffn_W2': _L3_ffn_in['W2'], 'L3_ffn_b2': _L3_ffn_in['b2'], 'L3_ffn_W3': _L3_ffn_in['W3'], 'L3_ffn_b3': _L3_ffn_in['b3']}

def reference(x, ctx_1024, fside_BxS2_0, mask_BxS2_bf1, mask_BxS2_bk0, L0_attn_in_proj_w, L0_attn_log_decay, L0_attn_frequency, L0_attn_coupling, L0_attn_out_proj_w, L0_attn_gate_w, L0_attn_gate_b, L0_attn_n1_g, L0_attn_n1_b, L0_attn_n2_g, L0_attn_n2_b, L0_attn_mlp_w1, L0_attn_mlp_b1, L0_attn_mlp_w2, L0_attn_mlp_b2, L0_xattn_wq, L0_xattn_bq, L0_xattn_wk, L0_xattn_bk, L0_xattn_wv, L0_xattn_bv, L0_xattn_wo, L0_xattn_bo, L0_ffn_ln1_g, L0_ffn_ln1_b, L0_ffn_w1, L0_ffn_b1, L0_ffn_ln2_g, L0_ffn_ln2_b, L0_ffn_w2, L0_ffn_b2, L1_attn_Wq, L1_attn_bq, L1_attn_Wk, L1_attn_bk, L1_attn_Wv, L1_attn_bv, L1_attn_Wg, L1_attn_bg, L1_attn_Wo, L1_attn_bo, L1_attn_gamma, L1_attn_beta, L1_xattn_ln_m_g, L1_xattn_ln_m_b, L1_xattn_ln_l_g, L1_xattn_ln_l_b, L1_xattn_Wq, L1_xattn_Wkv, L1_xattn_Wout, L1_ffn_Wq, L1_ffn_bq, L1_ffn_bn_gamma, L1_ffn_bn_beta, L1_ffn_sub_key0, L1_ffn_sub_key1, L1_ffn_expert_down, L1_ffn_expert_up, L2_attn_Wq, L2_attn_bq, L2_attn_Wk, L2_attn_bk, L2_attn_Wv, L2_attn_bv, L2_attn_Wo, L2_attn_bo, L2_attn_attn_scale, L2_xattn_ln_x_g, L2_xattn_ln_x_b, L2_xattn_ln_l_g, L2_xattn_ln_l_b, L2_xattn_qn_g, L2_xattn_kn_g, L2_xattn_Wq, L2_xattn_Wkv, L2_xattn_Wout, L2_xattn_bout, L2_ffn_router_w, L2_ffn_w1, L2_ffn_w2, L3_attn_w_q, L3_attn_w_k, L3_attn_w_v, L3_attn_w_o, L3_attn_b_o, L3_attn_rel_k, L3_attn_rel_v, L3_xattn_ln_x_w, L3_xattn_ln_x_b, L3_xattn_ln_l_w, L3_xattn_ln_l_b, L3_xattn_Wq, L3_xattn_Wkv, L3_xattn_q_scale, L3_xattn_k_scale, L3_xattn_Wo, L3_xattn_ln_o_w, L3_xattn_ln_o_b, L3_ffn_Wg, L3_ffn_W1, L3_ffn_b1, L3_ffn_W2, L3_ffn_b2, L3_ffn_W3, L3_ffn_b3):
    import jax
    import jax.numpy as jnp

    def _L0_attn_ref(x, in_proj_w, log_decay, frequency, coupling, out_proj_w, gate_w, gate_b, n1_g, n1_b, n2_g, n2_b, mlp_w1, mlp_b1, mlp_w2, mlp_b2):
        import jax, jax.numpy as jnp
        import numpy as np
        LN_EPS = 1e-05

        def _layernorm(x, g, b):
            m = jnp.mean(x, axis=-1, keepdims=True)
            v = jnp.mean((x - m) ** 2, axis=-1, keepdims=True)
            return (x - m) / jnp.sqrt(v + LN_EPS) * g + b

        def _eigenstate_fft(log_decay, frequency, beta_r, beta_i):
            B, T, K = beta_r.shape
            mag = jax.nn.sigmoid(log_decay)
            n = jnp.arange(T, dtype=beta_r.dtype)
            mag_pow = mag[None, :] ** n[:, None]
            phase = n[:, None] * frequency[None, :]
            kern = mag_pow * (jnp.cos(phase) + 1j * jnp.sin(phase))
            beta = beta_r + 1j * beta_i
            beta_p = jnp.pad(beta, ((0, 0), (0, T), (0, 0)))
            kern_p = jnp.pad(kern, ((0, T), (0, 0)))
            c = jnp.fft.ifft(jnp.fft.fft(beta_p, axis=1) * jnp.fft.fft(kern_p, axis=0)[None], axis=1)[:, :T, :]
            return (c.real.astype(beta_r.dtype), c.imag.astype(beta_r.dtype))

        def _reference_tuple_inner(x, in_proj_w, log_decay, frequency, coupling, out_proj_w, gate_w, gate_b, n1_g, n1_b, n2_g, n2_b, mlp_w1, mlp_b1, mlp_w2, mlp_b2):
            B, T, D = x.shape
            H, Kh, _ = coupling.shape
            K = H * Kh
            xn = _layernorm(x, n1_g, n1_b)
            beta = jnp.einsum('btd,kd->btk', xn, in_proj_w)
            br, bi = (beta[..., :K], beta[..., K:])
            cr, ci = _eigenstate_fft(log_decay, frequency, br, bi)
            cr_h = cr.reshape(B, T, H, Kh)
            ci_h = ci.reshape(B, T, H, Kh)
            cr = jnp.einsum('hjk,bthk->bthj', coupling, cr_h).reshape(B, T, K)
            ci = jnp.einsum('hjk,bthk->bthj', coupling, ci_h).reshape(B, T, K)
            eig = jnp.concatenate([cr, ci], axis=-1)
            out = jnp.einsum('btk,dk->btd', eig, out_proj_w)
            h = jax.nn.sigmoid(jnp.einsum('btd,ed->bte', xn, gate_w) + gate_b) * out
            x = x + h
            x2 = _layernorm(x, n2_g, n2_b)
            hid = jax.nn.silu(jnp.einsum('btd,md->btm', x2, mlp_w1) + mlp_b1)
            x = x + jnp.einsum('btm,dm->btd', hid, mlp_w2) + mlp_b2
            return (x, eig)
        return _reference_tuple_inner(x, in_proj_w, log_decay, frequency, coupling, out_proj_w, gate_w, gate_b, n1_g, n1_b, n2_g, n2_b, mlp_w1, mlp_b1, mlp_w2, mlp_b2)[0]

    def _L0_xattn_ref(query, key, value, weights, wq, bq, wk, bk, wv, bv, wo, bo):
        import jax, jax.numpy as jnp
        import numpy as np
        D_MODEL = 256
        N_HEADS = 16
        D_K = D_MODEL // N_HEADS

        def _split_heads(x):
            B, S, _ = x.shape
            return x.reshape(B, S, N_HEADS, D_K).transpose(0, 2, 1, 3)
        Q = _split_heads(query @ wq + bq)
        K = _split_heads(key @ wk + bk)
        V = _split_heads(value @ wv + bv)
        scores = jnp.einsum('bhqd,bhkd->bhqk', Q, K) / np.sqrt(D_K)
        log_w = jnp.log(weights + 1e-20)[:, None, None, :]
        attn = jax.nn.softmax(scores + log_w, axis=-1)
        out = jnp.einsum('bhqk,bhkd->bhqd', attn, V)
        B, H, S, Dk = out.shape
        out = out.transpose(0, 2, 1, 3).reshape(B, S, D_MODEL)
        return out @ wo + bo

    def _L0_ffn_ref(x, ln1_g, ln1_b, w1, b1, ln2_g, ln2_b, w2, b2):
        import jax, jax.numpy as jnp
        import numpy as np
        LN_EPS = 1e-05

        def layer_norm(x, g, b):
            mu = jnp.mean(x, axis=-1, keepdims=True)
            var = jnp.mean(jnp.square(x - mu), axis=-1, keepdims=True)
            return (x - mu) * jax.lax.rsqrt(var + LN_EPS) * g + b

        def ternary_quant(w):
            scale = 1.0 / jnp.clip(jnp.mean(jnp.abs(w)), 1e-05)
            wq = jnp.clip(jnp.round(w * scale), -1.0, 1.0) / scale
            return w + jax.lax.stop_gradient(wq - w)
        h = layer_norm(x, ln1_g, ln1_b)
        h = jnp.einsum('bsd,hd->bsh', h, ternary_quant(w1)) + b1
        h = jax.nn.gelu(h, approximate=False)
        h = layer_norm(h, ln2_g, ln2_b)
        out = jnp.einsum('bsh,dh->bsd', h, ternary_quant(w2)) + b2
        return out

    def _L1_attn_ref(x, Wq, bq, Wk, bk, Wv, bv, Wg, bg, Wo, bo, gamma, beta):
        import jax, jax.numpy as jnp
        import numpy as np
        B, T, D, S = (8, 1024, 256, 128)
        EPS = 1e-05

        def _gla(x, Wq, bq, Wk, bk, Wv, bv, Wg, bg, Wo, bo, gamma, beta):
            q = x @ Wq + bq
            k = x @ Wk + bk
            v = x @ Wv + bv
            g = jax.nn.sigmoid(x @ Wg + bg)

            def step(state, qkvg):
                qt, kt, vt, gt = qkvg
                state = gt[:, :, None] * state + kt[:, :, None] * vt[:, None, :]
                out = jnp.einsum('bs,bst->bt', qt, state)
                return (state, out)
            init = jnp.zeros((x.shape[0], Wq.shape[1], Wq.shape[1]), x.dtype)
            seq = (q.transpose(1, 0, 2), k.transpose(1, 0, 2), v.transpose(1, 0, 2), g.transpose(1, 0, 2))
            _, outs = jax.lax.scan(step, init, seq)
            out = outs.transpose(1, 0, 2)
            y = x + out @ Wo + bo
            mu = jnp.mean(y, axis=-1, keepdims=True)
            var = jnp.mean(jnp.square(y - mu), axis=-1, keepdims=True)
            return (y - mu) * jax.lax.rsqrt(var + EPS) * gamma + beta
        return _gla(x, Wq, bq, Wk, bk, Wv, bv, Wg, bg, Wo, bo, gamma, beta)

    def _L1_xattn_ref(x, latents, ln_m_g, ln_m_b, ln_l_g, ln_l_b, Wq, Wkv, Wout):
        import jax, jax.numpy as jnp
        import numpy as np
        EPS = 1e-05

        def layer_norm(x, g, b):
            mu = jnp.mean(x, axis=-1, keepdims=True)
            var = jnp.var(x, axis=-1, keepdims=True)
            return (x - mu) * jax.lax.rsqrt(var + EPS) * g + b
        heads, dim_head = (16, 64)
        scale = dim_head ** (-0.5)
        x = layer_norm(x, ln_m_g, ln_m_b)
        lat = layer_norm(latents, ln_l_g, ln_l_b)
        b, m, _ = lat.shape
        q = lat @ Wq
        kv_input = jnp.concatenate([x, lat], axis=1)
        kv = kv_input @ Wkv
        k, v = jnp.split(kv, 2, axis=-1)

        def split_heads(t):
            return t.reshape(t.shape[0], t.shape[1], heads, dim_head).transpose(0, 2, 1, 3)
        q, k, v = (split_heads(q), split_heads(k), split_heads(v))
        dots = jnp.einsum('bhid,bhjd->bhij', q, k) * scale
        attn = jax.nn.softmax(dots, axis=-1)
        out = jnp.einsum('bhij,bhjd->bhid', attn, v)
        out = out.transpose(0, 2, 1, 3).reshape(b, m, heads * dim_head)
        return out @ Wout

    def _L1_ffn_ref(hidden_states, Wq, bq, bn_gamma, bn_beta, sub_key0, sub_key1, expert_down, expert_up):
        import jax, jax.numpy as jnp
        import numpy as np
        H = 8
        QD = 64
        HALF = QD // 2
        DIMS = (32, 32)
        TOPK = 16
        DTK = 4
        EPS_BN = 1e-05
        EPS_NORM = 1e-12

        def _l2norm(x):
            n = jnp.linalg.norm(x, axis=-1, keepdims=True)
            return x / jnp.maximum(n, EPS_NORM)
        B, S, D = hidden_states.shape
        q = (hidden_states @ Wq + bq).reshape(B, S, H, QD)
        mean = q.mean(axis=(0, 1, 2))
        var = q.var(axis=(0, 1, 2))
        q = (q - mean) / jnp.sqrt(var + EPS_BN) * bn_gamma + bn_beta
        q0 = _l2norm(q[..., :HALF])
        q1 = _l2norm(q[..., HALF:])
        k0 = _l2norm(sub_key0)
        k1 = _l2norm(sub_key1)
        s0 = jnp.einsum('bshq,kq->bshk', q0, k0)
        s1 = jnp.einsum('bshq,kq->bshk', q1, k1)
        ts0, ti0 = jax.lax.top_k(s0, DTK)
        ts1, ti1 = jax.lax.top_k(s1, DTK)
        comb_s = (ts0[..., :, None] + ts1[..., None, :]).reshape(B, S, H, DTK * DTK)
        comb_i = (ti0[..., :, None] * DIMS[1] + ti1[..., None, :]).reshape(B, S, H, DTK * DTK)
        top_s, pos = jax.lax.top_k(comb_s, TOPK)
        idx = jnp.take_along_axis(comb_i, pos, axis=-1)
        w = jax.nn.softmax(top_s, axis=-1)
        down = expert_down[idx]
        up = expert_up[idx]
        eh = jnp.einsum('bshkd,bsd->bshk', down, hidden_states)
        eh = jax.nn.gelu(eh, approximate=False)
        out = jnp.einsum('bshko,bshk->bso', up, eh * w)
        return out

    def _L2_attn_ref(x, Wq, bq, Wk, bk, Wv, bv, Wo, bo, attn_scale):
        import jax, jax.numpy as jnp
        import numpy as np
        CHUNK = 64
        HEADS = 16

        def _chunk_mask(T, cs):
            idx = jnp.arange(T)
            blk = idx // cs * cs
            qb = blk[:, None]
            kb = blk[None, :]
            masked = (qb >= kb) & (idx[None, :] - idx[:, None] - 2 * (kb - qb) >= 1)
            return masked
        B, T, C = x.shape
        H = HEADS
        D = C // H
        q = (x @ Wq.T + bq).reshape(B, T, H, D)
        k = (x @ Wk.T + bk).reshape(B, T, H, D)
        v = (x @ Wv.T + bv).reshape(B, T, H, D)
        scores = jnp.einsum('bqhd,bkhd->bhqk', q, k) * attn_scale[0]
        mask = _chunk_mask(T, CHUNK)
        scores = jnp.where(mask[None, None], -jnp.inf, scores)
        attn = jax.nn.softmax(scores, axis=-1)
        out = jnp.einsum('bhqk,bkhd->bqhd', attn, v).reshape(B, T, C)
        return out @ Wo.T + bo

    def _L2_xattn_ref(x, latents, mask, ln_x_g, ln_x_b, ln_l_g, ln_l_b, qn_g, kn_g, Wq, Wkv, Wout, bout):
        import jax, jax.numpy as jnp
        import numpy as np
        DIM = 256
        DIM_LATENT = 256
        DIM_HEAD = 64
        HEADS = 16
        INNER = HEADS * DIM_HEAD

        def layernorm(x, g, b, eps=1e-05):
            m = jnp.mean(x, axis=-1, keepdims=True)
            v = jnp.mean((x - m) ** 2, axis=-1, keepdims=True)
            return (x - m) / jnp.sqrt(v + eps) * g + b

        def rmsnorm(x, gamma, eps=1e-08):
            n = jnp.linalg.norm(x, axis=-1, keepdims=True) * x.shape[-1] ** (-0.5)
            return x / jnp.maximum(n, eps) * gamma
        b, n, _ = x.shape
        m = latents.shape[1]
        h, d = (HEADS, DIM_HEAD)
        scale = d ** (-0.5)
        xn = layernorm(x, ln_x_g, ln_x_b)
        ln = layernorm(latents, ln_l_g, ln_l_b)
        q = (ln @ Wq).reshape(b, m, h, d).transpose(0, 2, 1, 3)
        kv = jnp.concatenate([xn @ Wkv, ln @ Wkv], axis=1)
        kv = kv.reshape(b, n + m, 2, h, d)
        k = kv[:, :, 0].transpose(0, 2, 1, 3)
        v = kv[:, :, 1].transpose(0, 2, 1, 3)
        qn = rmsnorm(q, qn_g) * scale
        kn = rmsnorm(k, kn_g)
        sim = jnp.einsum('bhid,bhjd->bhij', qn, kn)
        max_neg = -jnp.finfo(sim.dtype).max
        padded_mask = jnp.concatenate([mask, jnp.ones((b, m), bool)], axis=1)
        sim = jnp.where(padded_mask[:, None, None, :], sim, max_neg)
        attn = jax.nn.softmax(sim.astype(jnp.float32), axis=-1).astype(sim.dtype)
        out = jnp.einsum('bhij,bhjd->bhid', attn, v)
        out = out.transpose(0, 2, 1, 3).reshape(b, m, h * d)
        return out @ Wout + bout

    def _L2_ffn_ref(x, router_w, w1, w2):
        import jax, jax.numpy as jnp
        import numpy as np
        N_EMBD = 256
        EXPERT_SIZES = [(4, 256), (4, 512)]
        TOP_K = 2
        B, S = (1, 512)
        WIDTHS = []
        for count, size in EXPERT_SIZES:
            WIDTHS += [size] * count
        OFFSETS = np.concatenate([[0], np.cumsum(WIDTHS)]).astype(np.int64)
        E = len(WIDTHS)
        TOTAL_W = int(OFFSETS[-1])
        MAX_W = max(WIDTHS)

        def _stack_experts(w1, w2):
            W1e, W2e = ([], [])
            for e in range(E):
                off, wd = (int(OFFSETS[e]), WIDTHS[e])
                pad = MAX_W - wd
                W1e.append(jnp.pad(w1[:, off:off + wd], ((0, 0), (0, pad))))
                W2e.append(jnp.pad(w2[off:off + wd, :], ((0, pad), (0, 0))))
            return (jnp.stack(W1e), jnp.stack(W2e))
        b, s, d = x.shape
        xf = x.reshape(-1, d)
        logits = xf @ router_w.T
        probs = jax.nn.sigmoid(logits.astype(jnp.float32))
        topw, sel = jax.lax.top_k(probs, TOP_K)
        topw = topw / (topw.sum(-1, keepdims=True) + 1e-20)
        topw = topw.astype(x.dtype)
        onehot = sel[:, :, None] == jnp.arange(E)[None, None, :]
        combine = jnp.sum(topw[:, :, None] * onehot, axis=1)
        W1e, W2e = _stack_experts(w1, w2)
        h = jnp.einsum('td,edw->tew', xf, W1e)
        h = jnp.square(jax.nn.relu(h))
        y = jnp.einsum('tew,ewd->ted', h, W2e)
        out = jnp.einsum('ted,te->td', y, combine)
        return out.reshape(b, s, d)

    def _L3_attn_ref(x, w_q, w_k, w_v, w_o, b_o, rel_k, rel_v):
        import jax, jax.numpy as jnp
        import numpy as np
        D_MODEL = 256
        N_HEADS = 16
        D_K = D_MODEL // N_HEADS
        MAX_REL = 128
        SEQ = 256
        BATCH = 4

        def _relative_positions(seq_len: int) -> jnp.ndarray:
            pos = jnp.arange(seq_len)
            rel = pos[:, None] - pos[None, :]
            rel = jnp.clip(rel, -MAX_REL, MAX_REL) + MAX_REL
            return rel
        seq_len, batch, _ = x.shape
        scale = 1.0 / np.sqrt(D_K)
        Q = (x @ w_q.T).reshape(seq_len, batch, N_HEADS, D_K)
        K = (x @ w_k.T).reshape(seq_len, batch, N_HEADS, D_K)
        V = (x @ w_v.T).reshape(seq_len, batch, N_HEADS, D_K)
        rel_idx = _relative_positions(seq_len)
        rk = rel_k[rel_idx]
        rv = rel_v[rel_idx]
        scores = jnp.einsum('sbhd,tbhd->sbth', Q, K) * scale
        scores = scores + jnp.einsum('sbhd,std->sbth', Q, rk) * scale
        attn = jax.nn.softmax(scores, axis=-1)
        out = jnp.einsum('sbth,tbhd->sbhd', attn, V)
        out = out + jnp.einsum('sbth,std->sbhd', attn, rv)
        out = out.reshape(seq_len, batch, D_MODEL)
        return out @ w_o.T + b_o

    def _L3_xattn_ref(x, latents, mask, ln_x_w, ln_x_b, ln_l_w, ln_l_b, Wq, Wkv, q_scale, k_scale, Wo, ln_o_w, ln_o_b):
        import jax, jax.numpy as jnp
        import numpy as np
        DIM, DIM_HEAD, HEADS, SCALE = (256, 64, 8, 8.0)
        INNER = DIM_HEAD * HEADS
        LN_EPS = 1e-05
        L2_EPS = 1e-12

        def layer_norm(x, w, b):
            mu = jnp.mean(x, axis=-1, keepdims=True)
            var = jnp.mean(jnp.square(x - mu), axis=-1, keepdims=True)
            return (x - mu) * jax.lax.rsqrt(var + LN_EPS) * w + b

        def l2norm(t):
            n = jnp.sqrt(jnp.sum(jnp.square(t), axis=-1, keepdims=True))
            return t / jnp.maximum(n, L2_EPS)
        b, n, _ = x.shape
        m = latents.shape[1]
        x = layer_norm(x, ln_x_w, ln_x_b)
        latents = layer_norm(latents, ln_l_w, ln_l_b)
        q = latents @ Wq
        kv_input = jnp.concatenate([x, latents], axis=1)
        kv = kv_input @ Wkv
        k, v = jnp.split(kv, 2, axis=-1)

        def to_heads(t):
            return t.reshape(t.shape[0], t.shape[1], HEADS, DIM_HEAD).transpose(0, 2, 1, 3)
        q, k, v = map(to_heads, (q, k, v))
        q = l2norm(q) * q_scale
        k = l2norm(k) * k_scale
        sim = jnp.einsum('bhid,bhjd->bhij', q, k) * SCALE
        full_mask = jnp.concatenate([mask, jnp.ones((b, m), dtype=bool)], axis=1)[:, None, None, :]
        max_neg = -jnp.finfo(sim.dtype).max
        sim = jnp.where(full_mask, sim, max_neg)
        attn = jax.nn.softmax(sim.astype(jnp.float32), axis=-1).astype(sim.dtype)
        out = jnp.einsum('bhij,bhjd->bhid', attn, v)
        out = out.transpose(0, 2, 1, 3).reshape(b, m, INNER)
        return layer_norm(out @ Wo, ln_o_w, ln_o_b)

    def _L3_ffn_ref(x, Wg, W1, b1, W2, b2, W3, b3):
        import jax, jax.numpy as jnp
        import numpy as np
        B, S, H, DFF, E, K = (2, 512, 256, 512, 8, 2)

        def _moe(x, Wg, W1, b1, W2, b2, W3, b3):
            Bm, Sm, Hm = x.shape
            xt = x.reshape(-1, Hm)
            gout = xt @ Wg.T
            topv, topi = jax.lax.top_k(gout, K)
            w = jax.nn.softmax(topv, axis=-1)
            comb = jnp.einsum('tke,tk->te', jax.nn.one_hot(topi, E, dtype=x.dtype), w)
            g = jnp.einsum('th,efh->etf', xt, W1) + b1[:, None, :]
            v = jnp.einsum('th,efh->etf', xt, W2) + b2[:, None, :]
            h = jax.nn.silu(g) * v
            eo = jnp.einsum('etf,ehf->eth', h, W3) + b3[:, None, :]
            out = jnp.einsum('eth,te->th', eo, comb)
            return out.reshape(Bm, Sm, Hm)
        return _moe(x, Wg, W1, b1, W2, b2, W3, b3)
    x = x + _L0_attn_ref(_layernorm(x, axis=-1), L0_attn_in_proj_w, L0_attn_log_decay, L0_attn_frequency, L0_attn_coupling, L0_attn_out_proj_w, L0_attn_gate_w, L0_attn_gate_b, L0_attn_n1_g, L0_attn_n1_b, L0_attn_n2_g, L0_attn_n2_b, L0_attn_mlp_w1, L0_attn_mlp_b1, L0_attn_mlp_w2, L0_attn_mlp_b2)
    x = x + _L0_xattn_ref(_layernorm(x, axis=-1), ctx_1024, ctx_1024, fside_BxS2_0, L0_xattn_wq, L0_xattn_bq, L0_xattn_wk, L0_xattn_bk, L0_xattn_wv, L0_xattn_bv, L0_xattn_wo, L0_xattn_bo)
    x = x + _L0_ffn_ref(_layernorm(x, axis=-1), L0_ffn_ln1_g, L0_ffn_ln1_b, L0_ffn_w1, L0_ffn_b1, L0_ffn_ln2_g, L0_ffn_ln2_b, L0_ffn_w2, L0_ffn_b2)
    x = x + _L1_attn_ref(_layernorm(x, axis=-1), L1_attn_Wq, L1_attn_bq, L1_attn_Wk, L1_attn_bk, L1_attn_Wv, L1_attn_bv, L1_attn_Wg, L1_attn_bg, L1_attn_Wo, L1_attn_bo, L1_attn_gamma, L1_attn_beta)
    x = x + _L1_xattn_ref(ctx_1024, _layernorm(x, axis=-1), L1_xattn_ln_m_g, L1_xattn_ln_m_b, L1_xattn_ln_l_g, L1_xattn_ln_l_b, L1_xattn_Wq, L1_xattn_Wkv, L1_xattn_Wout)
    x = x + _L1_ffn_ref(_layernorm(x, axis=-1), L1_ffn_Wq, L1_ffn_bq, L1_ffn_bn_gamma, L1_ffn_bn_beta, L1_ffn_sub_key0, L1_ffn_sub_key1, L1_ffn_expert_down, L1_ffn_expert_up)
    x = x + _L2_attn_ref(_layernorm(x, axis=-1), L2_attn_Wq, L2_attn_bq, L2_attn_Wk, L2_attn_bk, L2_attn_Wv, L2_attn_bv, L2_attn_Wo, L2_attn_bo, L2_attn_attn_scale)
    x = x + _L2_xattn_ref(ctx_1024, _layernorm(x, axis=-1), mask_BxS2_bf1, L2_xattn_ln_x_g, L2_xattn_ln_x_b, L2_xattn_ln_l_g, L2_xattn_ln_l_b, L2_xattn_qn_g, L2_xattn_kn_g, L2_xattn_Wq, L2_xattn_Wkv, L2_xattn_Wout, L2_xattn_bout)
    x = x + _L2_ffn_ref(_layernorm(x, axis=-1), L2_ffn_router_w, L2_ffn_w1, L2_ffn_w2)
    x = x + _L3_attn_ref(_layernorm(x, axis=-1), L3_attn_w_q, L3_attn_w_k, L3_attn_w_v, L3_attn_w_o, L3_attn_b_o, L3_attn_rel_k, L3_attn_rel_v)
    x = x + _L3_xattn_ref(ctx_1024, _layernorm(x, axis=-1), mask_BxS2_bk0, L3_xattn_ln_x_w, L3_xattn_ln_x_b, L3_xattn_ln_l_w, L3_xattn_ln_l_b, L3_xattn_Wq, L3_xattn_Wkv, L3_xattn_q_scale, L3_xattn_k_scale, L3_xattn_Wo, L3_xattn_ln_o_w, L3_xattn_ln_o_b)
    x = x + _L3_ffn_ref(_layernorm(x, axis=-1), L3_ffn_Wg, L3_ffn_W1, L3_ffn_b1, L3_ffn_W2, L3_ffn_b2, L3_ffn_W3, L3_ffn_b3)
    return x

_drawn_inputs = setup_inputs


def setup_inputs(seed=0):
    import zlib

    import numpy as np

    out = dict(_drawn_inputs(seed))
    spreads = {'L0_attn_gate_b': (-2.0, 0.2),
     'L0_attn_n1_g': (1.0, 0.2),
     'L0_attn_n1_b': (0.0, 0.364),
     'L0_attn_n2_g': (1.0, 0.2),
     'L0_attn_n2_b': (0.0, 0.1),
     'L0_attn_mlp_b1': (0.0, 0.1),
     'L0_attn_mlp_b2': (0.0, 0.1),
     'L0_xattn_bq': (0.0, 0.397),
     'L0_xattn_bk': (0.0, 2.0),
     'L0_xattn_bv': (0.0, 0.1),
     'L0_xattn_bo': (0.0, 0.1),
     'L0_ffn_ln1_g': (1.0, 0.2),
     'L0_ffn_ln1_b': (0.0, 0.1),
     'L0_ffn_b1': (0.0, 0.1),
     'L0_ffn_ln2_g': (1.0, 0.2),
     'L0_ffn_ln2_b': (0.0, 0.1),
     'L0_ffn_b2': (0.0, 0.1),
     'L1_attn_bq': (0.0, 0.1),
     'L1_attn_bk': (0.0, 0.1),
     'L1_attn_bv': (0.0, 0.1),
     'L1_attn_bg': (0.0, 0.381),
     'L1_attn_bo': (0.0, 0.8),
     'L1_attn_gamma': (1.0, 0.2),
     'L1_attn_beta': (0.0, 0.1),
     'L1_xattn_ln_m_g': (1.0, 0.6),
     'L1_xattn_ln_m_b': (0.0, 0.537),
     'L1_xattn_ln_l_g': (1.0, 0.2),
     'L1_xattn_ln_l_b': (0.0, 0.1),
     'L1_ffn_bq': (0.0, 0.8),
     'L1_ffn_bn_gamma': (1.0, 0.6),
     'L1_ffn_bn_beta': (0.0, 0.8),
     'L2_attn_bq': (0.0, 0.8),
     'L2_attn_bk': (0.0, 2.0),
     'L2_attn_bv': (0.0, 0.465),
     'L2_attn_bo': (0.0, 0.1),
     'L2_xattn_ln_x_g': (1.0, 0.6),
     'L2_xattn_ln_x_b': (0.0, 0.8),
     'L2_xattn_ln_l_g': (1.0, 0.6),
     'L2_xattn_ln_l_b': (0.0, 0.8),
     'L2_xattn_qn_g': (1.0, 0.6),
     'L2_xattn_kn_g': (1.0, 0.6),
     'L2_xattn_bout': (0.0, 0.1),
     'L3_attn_b_o': (0.0, 0.333),
     'L3_xattn_ln_x_w': (1.0, 0.6),
     'L3_xattn_ln_x_b': (0.0, 0.8),
     'L3_xattn_ln_l_w': (1.0, 0.2),
     'L3_xattn_ln_l_b': (0.0, 0.1),
     'L3_xattn_q_scale': (1.0, 0.6),
     'L3_xattn_k_scale': (1.0, 0.6),
     'L3_xattn_ln_o_w': (1.0, 0.2),
     'L3_xattn_ln_o_b': (0.0, 0.412)}
    factors = {'L1_ffn_Wq': 8.0,
     'L1_ffn_sub_key0': 8.0,
     'L1_ffn_sub_key1': 8.0,
     'L1_ffn_expert_down': 6.339,
     'L1_ffn_expert_up': 5.466,
     'L2_attn_Wq': 8.0,
     'L2_attn_Wk': 8.0,
     'L2_attn_Wv': 3.321,
     'L2_xattn_Wq': 6.804,
     'L2_ffn_router_w': 5.37,
     'L2_ffn_w1': 5.063,
     'L2_ffn_w2': 4.552,
     'L3_ffn_b1': 52.675,
     'L3_ffn_b2': 50.831,
     'L3_ffn_b3': 24.503,
     'L3_ffn_W1': 3.383,
     'L3_ffn_W2': 3.308,
     'L3_ffn_W3': 2.953}
    for name, (base, spread) in spreads.items():
        noise = np.random.default_rng([zlib.crc32(name.encode()), seed]).standard_normal(out[name].shape)
        drawn = base * np.exp(spread * noise) if base else spread * noise
        out[name] = jnp.asarray(drawn.astype(out[name].dtype))
    for name, factor in factors.items():
        out[name] = (out[name] * factor).astype(out[name].dtype)
    return out
```

```python
from contextlib import ExitStack, contextmanager

import numpy as np

import concourse.bass as bass
from concourse import mybir

F32 = mybir.dt.float32
ALU = mybir.AluOpType
ACT = mybir.ActivationFunctionType
AX = mybir.AxisListType

P = 128
D = 256
KC = D // P
B = 4
T = 512
TT = T // P
NT = B * TT
EPS = 1e-5
FIRST, LAST = 0, 12


@contextmanager
def signals(nc, *names):
    with ExitStack() as st:
        sems = [st.enter_context(nc.semaphore(n)) for n in names]
        yield sems
        for s in sems:
            nc.gpsimd.sem_clear(s)
        nc.all_engine_barrier()


class Order:

    def __init__(self, eng, sem):
        self.eng, self.sem, self.n = eng, sem, 0

    def mark(self, ins):
        self.n += 1
        ins.then_inc(self.sem, 1)
        return self.n

    def wait(self):
        if self.n:
            self.eng.wait_ge(self.sem, self.n)

    def do(self, ins):
        self.mark(ins)
        self.wait()


class Core:

    def __init__(self, nc, ctx, dram):
        self.nc, self.ctx, self.dram = nc, ctx, dram
        self.used = {}
        sb = self.sb
        self.x = sb("x_res", [P, NT, D])
        self.ident = sb("ident", [P, P])
        self.ones = sb("ones", [P, P])
        self.half = sb("neg_half", [P, 64])
        self.xn = sb("x_normed", [P, TT, D])
        self.xnT = sb("x_normed_T", [P, KC, T])
        self.vecs = sb("feature_vectors", [P, dram["vecs"].shape[1]])
        self.rows = sb("row_vectors", [P, dram["rows"].shape[1]])
        self.ps = ctx.enter_context(nc.psum_tensor("psum_banks", [P, 8, 512], F32))

    def vec(self, n):
        return self.vecs[:, self.slots_v[n][0]:self.slots_v[n][1]]

    def row(self, n):
        return self.rows[:, self.slots_r[n][0]:self.slots_r[n][1]]

    def weight(self, name, ctx):
        src = self.dram[name]
        return Loaded(self.sb("w_" + name, list(src.shape), ctx, src.dtype), src)

    const = weight

    def load(self, *what):
        with signals(self.nc, "weights_loaded") as (loaded,), self.nc.Block() as block:
            @block.sync
            def _(sp):
                for w in what:
                    whole = tuple(slice(None) for _ in w.src.shape)
                    sp.dma_start(w.dst[whole], w.src[whole]).then_inc(loaded, 16)
                sp.wait_ge(loaded, 16 * len(what))

    def sb(self, name, shape, ctx=None, dtype=F32):
        self.used[name] = n = self.used.get(name, 0) + 1
        name = name if n == 1 else f"{name}_{n}"
        return (ctx or self.ctx).enter_context(self.nc.sbuf_tensor(name, shape, dtype))


class Loaded:

    def __init__(self, dst, src):
        self.dst, self.src = dst, src

    def __getitem__(self, i):
        return self.dst[i]


class Norm:

    NAMES = ("stats", "aggr", "rstd", "normed", "turned", "ready", "pool_order")

    def __init__(self, k, ctx, sems, name, twice=True, gain=None, offset=None, tiles=TT, rows=P, eps=EPS, eps2=EPS):
        (self.s_stats, self.s_aggr, self.s_rstd, self.s_normed, self.s_turned, self.s_ready, self.s_pool) = sems
        self.k, self.twice, self.gain, self.offset, self.tiles, self.rows = k, twice, gain, offset, tiles, rows
        self.eps, self.eps2 = eps, eps2
        self.stat = k.sb(name + "_stat", [P, tiles, 6], ctx)
        self.mv = k.sb(name + "_mv", [P, tiles, 2], ctx)
        self.rs = k.sb(name + "_rstd", [P, 4, tiles], ctx)

    def dve(self, dve, src, dst):
        r = self.rows
        for t in range(self.tiles):
            dve.bn_stats(self.stat[0:r, t, :], src(t)).then_inc(self.s_stats, 1)
        dve.wait_ge(self.s_stats, self.tiles)
        for t in range(self.tiles):
            dve.bn_aggr(self.mv[0:r, t, :], self.stat[0:r, t, :]).then_inc(self.s_aggr, 1)
        dve.wait_ge(self.s_aggr, self.tiles)
        dve.wait_ge(self.s_rstd, 1)
        for t in range(self.tiles):
            dve.tensor_scalar(dst[0:r, t, :], src(t), self.mv[0:r, t, 0:1], self.rs[0:r, 3, t:t + 1],
                              ALU.subtract, ALU.mult).then_inc(self.s_normed, 1)

    def pool(self, pool):
        k, r, n = self.k, self.rows, self.tiles
        rs, var = self.rs, self.mv[0:r, :, 1]
        o = Order(pool, self.s_pool)
        pool.wait_ge(self.s_aggr, n)
        o.do(pool.tensor_scalar(rs[0:r, 0, :], var, self.eps, 1.0, ALU.add, ALU.mult))
        if not self.twice:
            pool.tensor_tensor(rs[0:r, 3, :], rs[0:r, 0, :], k.half[0:r, 0:n], ALU.pow).then_inc(self.s_rstd, 1)
            return
        o.do(pool.tensor_tensor(rs[0:r, 1, :], rs[0:r, 0, :], k.half[0:r, 0:n], ALU.pow))
        o.do(pool.tensor_tensor(rs[0:r, 2, :], rs[0:r, 1, :], rs[0:r, 1, :], ALU.mult))
        o.do(pool.tensor_tensor(rs[0:r, 2, :], rs[0:r, 2, :], var, ALU.mult))
        o.do(pool.tensor_scalar(rs[0:r, 2, :], rs[0:r, 2, :], self.eps2, 1.0, ALU.add, ALU.mult))
        o.do(pool.tensor_tensor(rs[0:r, 2, :], rs[0:r, 2, :], k.half[0:r, 0:n], ALU.pow))
        pool.tensor_tensor(rs[0:r, 3, :], rs[0:r, 2, :], rs[0:r, 1, :], ALU.mult).then_inc(self.s_rstd, 1)

    def pe(self, pe, src, banks, chunks=KC):
        k, r = self.k, self.rows
        pe.wait_ge(self.s_normed, self.tiles)
        for c in range(chunks):
            for t in range(self.tiles):
                last = pe.transpose(k.ps[:, banks[c], t * r:(t + 1) * r], src[0:r, t, c * P:(c + 1) * P],
                                    k.ident[0:r, 0:r])
            last.then_inc(self.s_turned, 1)

    def act(self, act, dst, banks, chunks=KC):
        k, n = self.k, self.rows * self.tiles
        for c in range(chunks):
            act.wait_ge(self.s_turned, c + 1)
            if self.gain is None:
                act.copy(dst[:, c, 0:n], k.ps[:, banks[c], 0:n]).then_inc(self.s_ready, 1)
            else:
                act.activation(dst[:, c, 0:n], k.ps[:, banks[c], 0:n], ACT.Identity,
                               bias=self.offset[:, c:c + 1], scale=self.gain[:, c:c + 1]).then_inc(self.s_ready, 1)


def norm_names(p):
    return [p + n for n in Norm.NAMES]


def batch_tiles(k, b):
    v = k.x[:, :, :].rearrange("p (b t) d -> p b t d", b=B)
    return lambda t: v[:, bass.ds(b, 1), t, :].rearrange("p o d -> p (o d)")



def l0_ffn(k):
    nc = k.nc
    HID = 1024
    HC = HID // P
    with ExitStack() as st:
        w1 = k.sb("w1_T", [P, KC, HID], st)
        w2 = k.sb("w2_T", [P, HC, D], st)
        h = k.sb("hidden", [P, TT, HID], st)
        hT = k.sb("hidden_T", [P, HC, T], st)
        asum = k.sb("abs_sum", [P, 2], st)
        scal = k.sb("quant_scale", [P, 2, 2], st)
        sems = norm_names("ffn1_") + norm_names("ffn2_")
        with signals(nc, "loaded", "abs_summed", "summed", "scaled", "quantised") as \
                (loaded, abs_summed, summed, scaled, quantised), nc.Block() as block:
            @block.sync
            def _(sp):
                sp.dma_start(w1[:, :, :], k.dram["L0_ffn_w1"][:, :, :]).then_inc(loaded, 16)
                sp.dma_start(w2[:, :, :], k.dram["L0_ffn_w2"][:, :, :]).then_inc(loaded, 16)

            @block.vector
            def _(dve):
                o = Order(dve, quantised)
                dve.wait_ge(loaded, 32)
                for i, w in enumerate((w1, w2)):
                    dve.tensor_reduce(asum[:, i:i + 1], w[:, :, :], AX.XY, ALU.add,
                                      apply_absolute_value=True).then_inc(abs_summed, 1)
                dve.wait_ge(summed, 1)
                o.do(dve.tensor_scalar(scal[:, :, 1], k.ps[:, 0, 0:2], 1.0 / (HID * D), 1e-5, ALU.mult, ALU.max))
                o.do(dve.reciprocal(scal[:, :, 0], scal[:, :, 1]))
                for i, w in enumerate((w1, w2)):
                    o.do(dve.tensor_scalar(w[:, :, :], w[:, :, :], scal[:, i, 0:1], 1.0, ALU.mult, ALU.min))
                    o.do(dve.tensor_scalar(w[:, :, :], w[:, :, :], -1.0, 12582912.0, ALU.max, ALU.add))
                    o.do(dve.tensor_scalar(w[:, :, :], w[:, :, :], -12582912.0, scal[:, i, 1:2], ALU.add, ALU.mult))

            @block.tensor
            def _(pe):
                pe.wait_ge(abs_summed, 2)
                pe.matmul(k.ps[:, 0, 0:2], k.ones[:, :], asum[:, :], start=True, stop=True).then_inc(summed, 1)

        with nc.Fori(0, B) as b, signals(nc, *sems, "up", "biased", "gelued", "down", "added", "freed") as \
                (*ns, up, biased, gelued, down, added, freed), ExitStack() as bs:
            n1 = Norm(k, bs, ns[:7], "n1", gain=k.vec("L0_ffn_ln1_g"), offset=k.vec("L0_ffn_ln1_b"))
            n2s = ns[7:]
            s_stats, s_aggr, s_rstd, s_normed, s_turned, s_ready, s_pool = n2s
            stat = k.sb("hid_stat", [P, TT, 2, 6], bs)
            mv = k.sb("hid_mv", [P, TT, 2], bs)
            rs = k.sb("hid_rstd", [P, 2, TT], bs)
            x = batch_tiles(k, b)
            g2, b2 = k.vec("L0_ffn_ln2_g"), k.vec("L0_ffn_ln2_b")
            b1r, b2r = k.row("L0_ffn_b1"), k.row("L0_ffn_b2")
            with nc.Block() as block:
                @block.vector
                def _(dve):
                    n1.dve(dve, x, k.xn)
                    for t in range(TT):
                        dve.wait_ge(up, t + 1)
                        s0 = 2 * (t % 2)
                        dve.tensor_tensor(h[:, t, :].rearrange("p (a n) -> p a n", a=2), k.ps[:, s0:s0 + 2, :],
                                          b1r.rearrange("p (a n) -> p a n", a=2), ALU.add).then_inc(biased, 1)
                    for t in range(TT):
                        dve.wait_ge(gelued, t + 1)
                        for a in range(2):
                            dve.bn_stats(stat[:, t, a, :], h[:, t, a * 512:(a + 1) * 512]).then_inc(s_stats, 1)
                        dve.wait_ge(s_stats, 2 * (t + 1))
                        dve.bn_aggr(mv[:, t, :], stat[:, t, :, :].rearrange("p a s -> p (a s)")).then_inc(s_aggr, 1)
                    for t in range(TT):
                        dve.wait_ge(s_rstd, t + 1)
                        dve.tensor_scalar(h[:, t, :], h[:, t, :], mv[:, t, 0:1], rs[:, 1, t:t + 1],
                                          ALU.subtract, ALU.mult).then_inc(s_normed, 1)
                    o = Order(dve, freed)
                    for t in range(TT):
                        dve.wait_ge(down, t + 1)
                        o.do(dve.tensor_tensor(k.xn[:, t, :], k.ps[:, 4 + t % 2, 0:D], b2r, ALU.add))
                        dve.tensor_tensor(x(t), x(t), k.xn[:, t, :], ALU.add).then_inc(added, 1)

                @block.gpsimd
                def _(pool):
                    n1.pool(pool)
                    o = Order(pool, s_pool)
                    for t in range(TT):
                        pool.wait_ge(s_aggr, t + 1)
                        o.do(pool.tensor_scalar(rs[:, 0, t:t + 1], mv[:, t, 1:2], EPS, 1.0, ALU.add, ALU.mult))
                        pool.tensor_tensor(rs[:, 1, t:t + 1], rs[:, 0, t:t + 1], k.half[:, 0:1],
                                           ALU.pow).then_inc(s_rstd, 1)

                @block.scalar
                def _(act):
                    n1.act(act, k.xnT, (6, 7))
                    for t in range(TT):
                        act.wait_ge(biased, t + 1)
                        act.activation(h[:, t, :], h[:, t, :], ACT.Gelu).then_inc(gelued, 1)
                    for c in range(HC):
                        act.wait_ge(s_turned, c + 1)
                        act.activation(hT[:, c, :], k.ps[:, c % 4, :], ACT.Identity, bias=b2[:, c:c + 1],
                                       scale=g2[:, c:c + 1]).then_inc(s_ready, 1)

                @block.tensor
                def _(pe):
                    n1.pe(pe, k.xn, (6, 7))
                    pe.wait_ge(n1.s_ready, KC)
                    for t in range(TT):
                        if t >= 2:
                            pe.wait_ge(biased, t - 1)
                        for a in range(2):
                            for c in range(KC):
                                last = pe.matmul(k.ps[:, 2 * (t % 2) + a, :], k.xnT[:, c, t * P:(t + 1) * P],
                                                 w1[:, c, a * 512:(a + 1) * 512], start=c == 0, stop=c == KC - 1)
                        last.then_inc(up, 1)
                    pe.wait_ge(s_normed, TT)
                    for c in range(HC):
                        if c >= 4:
                            pe.wait_ge(s_ready, c - 3)
                        for t in range(TT):
                            last = pe.transpose(k.ps[:, c % 4, t * P:(t + 1) * P], h[:, t, c * P:(c + 1) * P],
                                                k.ident[:, :])
                        last.then_inc(s_turned, 1)
                    pe.wait_ge(s_ready, HC)
                    for t in range(TT):
                        if t >= 2:
                            pe.wait_ge(freed, t - 1)
                        for c in range(HC):
                            last = pe.matmul(k.ps[:, 4 + t % 2, 0:D], hT[:, c, t * P:(t + 1) * P], w2[:, c, :],
                                             start=c == 0, stop=c == HC - 1)
                        last.then_inc(down, 1)


BIG = 3.0e38


def l0_attn(k):
    nc = k.nc
    HC = 1024 // P
    TWO_PI_HI = 6.28125
    TWO_PI_LO = 2 * np.pi - TWO_PI_HI
    MAGIC = 12582912.0
    with ExitStack() as st:
        w_in = k.weight("L0_in", st)
        w_out = k.weight("L0_attn_out_proj_w", st)
        coup = k.weight("L0_coupling", st)
        gate = k.weight("L0_attn_gate_w", st)
        w1 = k.weight("L0_attn_mlp_w1", st)
        w2 = k.weight("L0_attn_mlp_w2", st)
        count = k.const("counting", st)
        k.load(w_in, w_out, coup, gate, w1, w2, count)
        mag = k.sb("magnitude", [P, T], st)
        cos = k.sb("cosine", [P, T], st)
        sin = k.sb("signed_sine", [P, T], st)
        m = k.sb("out_weights", [P, 2, D], st)
        with signals(nc, "rot_order", "reduced", "angles", "magged", "coupled", "out_ready") as \
                (order, reduced, angles, magged, coupled, out_ready), ExitStack() as ts, nc.Block() as block:
            ph = k.sb("phase", [P, T], ts)
            turns = k.sb("turns", [P, T], ts)
            mcol = k.sb("mag_col", [P, 1], ts)

            @block.vector
            def _(dve):
                o = Order(dve, order)
                o.do(dve.tensor_scalar(ph[:, :], count[:, :], k.vec("L0_freq")[:, 0:1], None, ALU.mult))
                o.do(dve.tensor_scalar(turns[:, :], ph[:, :], 1 / (2 * np.pi), MAGIC, ALU.mult, ALU.add))
                o.do(dve.tensor_scalar(turns[:, :], turns[:, :], -MAGIC, None, ALU.add))
                o.do(dve.scalar_tensor_tensor(out=ph[:, :], in0=turns[:, :], scalar=-TWO_PI_HI, in1=ph[:, :],
                                              op0=ALU.mult, op1=ALU.add))
                o.do(dve.scalar_tensor_tensor(out=ph[:, :], in0=turns[:, :], scalar=-TWO_PI_LO, in1=ph[:, :],
                                              op0=ALU.mult, op1=ALU.add))
                dve.tensor_scalar(ph[:, :], ph[:, :], 3.141592, -3.141592, ALU.min, ALU.max).then_inc(reduced, 1)
                dve.wait_ge(magged, 1)
                o.mark(dve.tensor_scalar(mag[:, :], k.ones[:, 0:1].to_broadcast([P, T]), mcol[:, 0:1], None,
                                         ALU.mult))
                dve.wait_ge(angles, 2)
                o.mark(dve.tensor_scalar(sin[:, :], sin[:, :], k.vec("re_im_sign")[:, 0:1], None, ALU.mult))
                for i in range(2):
                    dve.wait_ge(coupled, i + 1)
                    dve.tensor_copy(m[:, i, :], k.ps[:, i, 0:D]).then_inc(out_ready, 1)

            @block.scalar
            def _(act):
                act.activation(mcol[:, :], k.vec("L0_decay")[:, 0:1], ACT.Sigmoid).then_inc(magged, 1)
                act.wait_ge(reduced, 1)
                act.activation(sin[:, :], ph[:, :], ACT.Sin).then_inc(angles, 1)
                act.activation(turns[:, :], ph[:, :], ACT.Abs).then_inc(angles, 1)
                act.wait_ge(angles, 2)
                act.activation(cos[:, :], turns[:, :], ACT.Sin, bias=k.vec("half_pi")[:, 0:1],
                               scale=-1.0).then_inc(angles, 1)

            @block.tensor
            def _(pe):
                for i in range(2):
                    pe.matmul(k.ps[:, i, 0:D], coup[:, 0, i * P:(i + 1) * P], w_out[:, 0, :], start=True,
                              stop=True).then_inc(coupled, 1)

        xin = k.sb("x_in", [P, TT, D], st)
        x2 = k.sb("x_mid_normed", [P, TT, D], st)
        x2T = k.sb("x_mid_T", [P, KC, T], st)
        beta = k.sb("beta_turned", [P, 4, T], st)
        gt = k.sb("gate_value", [P, TT, D], st)
        hT = k.sb("hidden_T", [P, HC, T], st)
        with nc.Fori(0, B) as b, signals(
                nc, *norm_names("a_"), *norm_names("m_"), "once", "beta_made", "rot_order", "scanned", "gate_made",
                "gate_biased", "gate_open", "outed", "midded", "up", "silued", "down", "biased", "added") as (
                *sems, once, beta_made, order, scanned, gate_made, gate_biased, gate_open, outed, midded, up,
                silued, down, biased, added), ExitStack() as bs:
            n1 = Norm(k, bs, sems[:7], "a", gain=k.vec("L0_attn_n1_g"), offset=k.vec("L0_attn_n1_b"))
            n2 = Norm(k, bs, sems[7:], "m", twice=False, gain=k.vec("L0_attn_n2_g"), offset=k.vec("L0_attn_n2_b"))
            b1, b2r, gbr = k.vec("L0_attn_mlp_b1"), k.row("L0_attn_mlp_b2"), k.row("L0_attn_gate_b")
            x = batch_tiles(k, b)
            with nc.Block() as block:
                @block.vector
                def _(dve):
                    n1.dve(dve, x, k.xn)
                    for t in range(TT):
                        dve.tensor_scalar(xin[:, t, :], x(t), n1.mv[:, t, 0:1], n1.rs[:, 1, t:t + 1],
                                          ALU.subtract, ALU.mult).then_inc(once, 1)
                    o = Order(dve, order)
                    dve.wait_ge(beta_made, 2)
                    o.mark(dve.tensor_tensor(beta[:, 0, :], k.ps[:, 0, :], cos[:, :], ALU.mult))
                    o.do(dve.tensor_tensor(beta[:, 1, :], k.ps[:, 1, :], sin[:, :], ALU.mult))
                    o.do(dve.tensor_tensor(beta[:, 0, :], beta[:, 0, :], beta[:, 1, :], ALU.add))
                    o.do(dve.tensor_tensor_scan(beta[:, 1, :], mag[:, :], beta[:, 0, :], 0.0, ALU.mult, ALU.add))
                    dve.tensor_tensor(beta[:, 2, :], beta[:, 1, :], cos[:, :], ALU.mult).then_inc(scanned, 1)
                    dve.tensor_tensor(beta[:, 3, :], beta[:, 1, :], sin[:, :], ALU.mult).then_inc(scanned, 1)
                    for t in range(TT):
                        dve.wait_ge(gate_made, 2 * (t // 2) + 2)
                        dve.tensor_tensor(gt[:, t, :], k.ps[:, 2 + t // 2, (t % 2) * D:(t % 2 + 1) * D], gbr,
                                          ALU.add).then_inc(gate_biased, 1)
                    dve.wait_ge(once, TT)
                    for t in range(TT):
                        dve.wait_ge(gate_open, t + 1)
                        dve.wait_ge(outed, 2 * (t // 2) + 2)
                        o.do(dve.tensor_tensor(gt[:, t, :], gt[:, t, :],
                                               k.ps[:, 4 + t // 2, (t % 2) * D:(t % 2 + 1) * D], ALU.mult))
                        o.mark(dve.tensor_tensor(xin[:, t, :], xin[:, t, :], gt[:, t, :], ALU.add))
                    o.wait()
                    n2.dve(dve, lambda t: xin[:, t, :], x2)
                    for t in range(TT):
                        dve.tensor_tensor(xin[:, t, :], xin[:, t, :], b2r, ALU.add).then_inc(biased, 1)
                    dve.wait_ge(biased, TT)
                    for t in range(TT):
                        dve.tensor_tensor(x(t), x(t), xin[:, t, :], ALU.add).then_inc(biased, 1)
                    for t in range(TT):
                        dve.wait_ge(down, 2 * (t // 2) + 2)
                        dve.wait_ge(biased, TT + t + 1)
                        dve.tensor_tensor(x(t), x(t), k.ps[:, t // 2, (t % 2) * D:(t % 2 + 1) * D],
                                          ALU.add).then_inc(added, 1)

                @block.gpsimd
                def _(pool):
                    n1.pool(pool)
                    n2.pool(pool)

                @block.scalar
                def _(act):
                    n1.act(act, k.xnT, (6, 7))
                    for t in range(TT):
                        act.wait_ge(gate_biased, t + 1)
                        act.activation(gt[:, t, :], gt[:, t, :], ACT.Sigmoid).then_inc(gate_open, 1)
                    n2.act(act, x2T, (6, 7))
                    for c in range(HC):
                        act.wait_ge(up, c + 1)
                        act.activation(hT[:, c, :], k.ps[:, 2 + c % 4, :], ACT.Silu,
                                       bias=b1[:, c:c + 1]).then_inc(silued, 1)

                @block.tensor
                def _(pe):
                    n1.pe(pe, k.xn, (6, 7))
                    pe.wait_ge(n1.s_ready, KC)
                    for i in range(2):
                        for c in range(KC):
                            last = pe.matmul(k.ps[:, i, :], w_in[:, c, i * P:(i + 1) * P], k.xnT[:, c, :],
                                             start=c == 0, stop=c == KC - 1)
                        last.then_inc(beta_made, 1)
                    for t in range(TT):
                        for c in range(KC):
                            last = pe.matmul(k.ps[:, 2 + t // 2, (t % 2) * D:(t % 2 + 1) * D],
                                             k.xnT[:, c, t * P:(t + 1) * P], gate[:, c, :],
                                             start=c == 0, stop=c == KC - 1)
                        last.then_inc(gate_made, 1)
                    pe.wait_ge(scanned, 2)
                    for t in range(TT):
                        for i in range(2):
                            last = pe.matmul(k.ps[:, 4 + t // 2, (t % 2) * D:(t % 2 + 1) * D],
                                             beta[:, 2 + i, t * P:(t + 1) * P], m[:, i, :],
                                             start=i == 0, stop=i == 1)
                        last.then_inc(outed, 1)
                    n2.pe(pe, x2, (6, 7))
                    pe.wait_ge(n2.s_ready, KC)
                    for n in range(HC):
                        if n >= 4:
                            pe.wait_ge(silued, n - 3)
                        for c in range(KC):
                            last = pe.matmul(k.ps[:, 2 + n % 4, :], w1[:, c, n * P:(n + 1) * P], x2T[:, c, :],
                                             start=c == 0, stop=c == KC - 1)
                        last.then_inc(up, 1)
                    pe.wait_ge(silued, HC)
                    for t in range(TT):
                        for n in range(HC):
                            last = pe.matmul(k.ps[:, t // 2, (t % 2) * D:(t % 2 + 1) * D],
                                             hT[:, n, t * P:(t + 1) * P], w2[:, n, :],
                                             start=n == 0, stop=n == HC - 1)
                        last.then_inc(down, 1)



class Product:

    def __init__(self, dst, pairs, rows, n, add=None, mult=None, row=None):
        self.dst, self.pairs, self.rows, self.n = dst, pairs, rows, n
        self.add, self.mult, self.row = add, mult, row


def project(k, products):
    on_act = [i for i, p in enumerate(products) if i % 2 and p.add is None and p.row is None]
    on_dve = [i for i in range(len(products)) if i not in on_act]
    rank = {i: n for lst in (on_act, on_dve) for n, i in enumerate(lst)}
    with signals(k.nc, "made", "act_moved", "dve_moved") as (made, act_moved, dve_moved), k.nc.Block() as block:
        @block.tensor
        def _(pe):
            for i, p in enumerate(products):
                if i >= 8:
                    pe.wait_ge(act_moved if i - 8 in on_act else dve_moved, rank[i - 8] + 1)
                for j, (lhsT, rhs) in enumerate(p.pairs):
                    last = pe.matmul(k.ps[0:p.rows, i % 8, 0:p.n], lhsT, rhs, start=j == 0,
                                     stop=j == len(p.pairs) - 1)
                last.then_inc(made, 1)

        @block.scalar
        def _(act):
            for i in on_act:
                p = products[i]
                act.wait_ge(made, i + 1)
                out = k.ps[0:p.rows, i % 8, 0:p.n]
                if p.mult is None:
                    act.copy(p.dst, out).then_inc(act_moved, 1)
                else:
                    act.mul(p.dst, out, p.mult).then_inc(act_moved, 1)

        @block.vector
        def _(dve):
            for i in on_dve:
                p = products[i]
                dve.wait_ge(made, i + 1)
                out = k.ps[0:p.rows, i % 8, 0:p.n]
                if p.row is not None:
                    dve.tensor_tensor(p.dst, out, p.row, ALU.add).then_inc(dve_moved, 1)
                elif p.add is not None:
                    dve.tensor_scalar(p.dst, out, p.add, p.mult, ALU.add,
                                      ALU.bypass if p.mult is None else ALU.mult).then_inc(dve_moved, 1)
                elif p.mult is not None:
                    dve.tensor_scalar(p.dst, out, p.mult, None, ALU.mult).then_inc(dve_moved, 1)
                else:
                    dve.tensor_copy(p.dst, out).then_inc(dve_moved, 1)


class Item:

    def __init__(self, width, scores, chunks, out, mask=None):
        self.width = width
        self.scores = scores
        self.chunks = chunks
        self.out = out
        self.mask = mask


def attend(k, items, dv):
    nc, N = k.nc, len(items)
    wmax = max(it.width for it in items)
    cmax = (wmax + P - 1) // P
    with ExitStack() as st, signals(nc, "scored", "maxed", "exped", "turned", "copied", "valued", "inverted",
                                    "stored", "mask_order") as (
            scored, maxed, exped, turned, copied, valued, inverted, stored, order):
        prob = k.sb("probs", [P, 2, wmax], st)
        pT = k.sb("probs_T", [P, 2, cmax, P], st)
        nmax = k.sb("neg_max", [P, 4], st)
        tot = k.sb("exp_sum", [P, 4], st)
        inv = k.sb("inv_sum", [P, 4], st)

        def score_bank(i):
            return k.ps[:, 2 * (i % 2):2 * (i % 2) + 2, :].rearrange("p a n -> p (a n)")

        def turned_place(i, c):
            bank = (4 if c < 4 else 6) + i % 2
            return k.ps[:, bank, (c % 4) * P:(c % 4 + 1) * P]

        def out_place(i):
            return k.ps[:, 6 + i % 2, 256:256 + dv]

        with nc.Block() as block:
            @block.tensor
            def _(pe):
                for i in range(N + 2):
                    if i < N:
                        if i >= 2:
                            pe.wait_ge(exped, i - 1)
                        for lhsT, rhs, c0, n in items[i].scores:
                            last = pe.matmul(score_bank(i)[:, c0:c0 + n], lhsT, rhs, start=True, stop=True)
                        last.then_inc(scored, 1)
                    if 1 <= i <= N:
                        j = i - 1
                        pe.wait_ge(exped, j + 1)
                        if j >= 2:
                            pe.wait_ge(copied, j - 1)
                            pe.wait_ge(stored, j - 1)
                        at = 0
                        for c, (n, _) in enumerate(items[j].chunks):
                            last = pe.transpose(turned_place(j, c)[0:n, :], prob[:, j % 2, at:at + n],
                                                k.ident[:, :])
                            at += n
                        last.then_inc(turned, 1)
                    if i >= 2:
                        j = i - 2
                        pe.wait_ge(copied, j + 1)
                        for c, (n, v) in enumerate(items[j].chunks):
                            last = pe.matmul(out_place(j), pT[0:n, j % 2, c, :], v, start=c == 0,
                                             stop=c == len(items[j].chunks) - 1)
                        last.then_inc(valued, 1)

            @block.vector
            def _(dve):
                o = Order(dve, order)
                for i in range(N + 2):
                    if i < N:
                        it = items[i]
                        dve.wait_ge(scored, i + 1)
                        if it.mask is not None:
                            c0, n, m = it.mask
                            o.do(dve.tensor_tensor(score_bank(i)[:, c0:c0 + n], score_bank(i)[:, c0:c0 + n], m,
                                                   ALU.add))
                        dve.tensor_reduce(nmax[:, i % 4:i % 4 + 1], score_bank(i)[:, 0:it.width], AX.X, ALU.max,
                                          negate=True).then_inc(maxed, 1)
                    if 1 <= i <= N:
                        j = i - 1
                        dve.wait_ge(turned, j + 1)
                        if j >= 2:
                            dve.wait_ge(valued, j - 1)
                        chunks = items[j].chunks
                        full = sum(1 for n, _ in chunks[0:4] if n == P)
                        if full:
                            last = dve.tensor_copy(pT[:, j % 2, 0:full, :], k.ps[:, 4 + j % 2, 0:full * P]
                                                   .rearrange("p (c q) -> p c q", c=full))
                        if full < len(chunks):
                            n = chunks[full][0]
                            last = dve.tensor_copy(pT[0:n, j % 2, full, :], turned_place(j, full)[0:n, :])
                        last.then_inc(copied, 1)
                    if i >= 2:
                        j = i - 2
                        dve.wait_ge(exped, j + 1)
                        if j >= 4:
                            dve.wait_ge(stored, j - 3)
                        dve.reciprocal(inv[:, j % 4:j % 4 + 1], tot[:, j % 4:j % 4 + 1]).then_inc(inverted, 1)

            @block.scalar
            def _(act):
                for i in range(N + 2):
                    if i < N:
                        act.wait_ge(maxed, i + 1)
                        if i >= 2:
                            act.wait_ge(turned, i - 1)
                        if i >= 4:
                            act.wait_ge(inverted, i - 3)
                        act.activation(prob[:, i % 2, 0:items[i].width], score_bank(i)[:, 0:items[i].width],
                                       ACT.Exp, bias=nmax[:, i % 4:i % 4 + 1],
                                       accum_out=tot[:, i % 4:i % 4 + 1]).then_inc(exped, 1)
                    if i >= 2:
                        j = i - 2
                        act.wait_ge(valued, j + 1)
                        act.wait_ge(inverted, j + 1)
                        act.mul(items[j].out, out_place(j), inv[:, j % 4:j % 4 + 1]).then_inc(stored, 1)


def normed_batch(k, b, twice=True, gain=None, offset=None, dst=None, banks=(6, 7)):
    nc = k.nc
    dst = k.xnT if dst is None else dst
    with ExitStack() as st, signals(nc, *norm_names("n_")) as sems:
        n = Norm(k, st, sems, "n", twice=twice, gain=gain, offset=offset)
        x = batch_tiles(k, b)
        with nc.Block() as block:
            @block.vector
            def _(dve):
                n.dve(dve, x, k.xn)

            @block.gpsimd
            def _(pool):
                n.pool(pool)

            @block.tensor
            def _(pe):
                n.pe(pe, k.xn, banks)

            @block.scalar
            def _(act):
                n.act(act, dst, banks)
                act.wait_ge(n.s_ready, KC)


def output_projection(k, b, o, wo, width, bias_row=None, gain_row=None, offset_row=None, oT=None, before=None):
    given = oT is not None
    nc, C = k.nc, width // P
    with ExitStack() as st, signals(nc, "turned", "moved", "made", "summed", "stats", "aggr", "shifted", "rstd",
                                    "order") as (turned, moved, made, summed, stats, aggr, shifted, rstd, order):
        oT = oT if given else k.sb("attended_T", [P, C, T], st)
        y = k.sb("projected", [P, TT, D], st)
        stat = k.sb("out_stat", [P, TT, 6], st)
        mv = k.sb("out_mv", [P, TT, 2], st)
        rs = k.sb("out_rstd", [P, 2, TT], st)
        x = batch_tiles(k, b)

        def summand(t):
            return k.ps[:, 4 + t, 0:D] if before is None else y[:, t, :]

        with nc.Block() as block:
            @block.tensor
            def _(pe):
                for c in range(0 if given else C):
                    if c >= 4:
                        pe.wait_ge(moved, c - 3)
                    for t in range(TT):
                        last = pe.transpose(k.ps[:, c % 4, t * P:(t + 1) * P], o[:, t, c * P:(c + 1) * P],
                                            k.ident[:, :])
                    last.then_inc(turned, 1)
                if not given:
                    pe.wait_ge(moved, C)
                for t in range(TT):
                    for c in range(C):
                        last = pe.matmul(k.ps[:, 4 + t, 0:D], oT[:, c, t * P:(t + 1) * P], wo[:, c, :],
                                         start=c == 0, stop=c == C - 1)
                    last.then_inc(made, 1)

            @block.scalar
            def _(act):
                for c in range(0 if given else C):
                    act.wait_ge(turned, c + 1)
                    act.copy(oT[:, c, :], k.ps[:, c % 4, :]).then_inc(moved, 1)

            @block.vector
            def _(dve):
                o_ = Order(dve, order)
                if gain_row is None:
                    for t in range(TT):
                        if bias_row is not None:
                            o_.do(dve.tensor_tensor(x(t), x(t), bias_row, ALU.add))
                        dve.wait_ge(made, t + 1)
                        dve.tensor_tensor(x(t), x(t), k.ps[:, 4 + t, 0:D], ALU.add).then_inc(summed, 1)
                    return
                for t in range(TT):
                    dve.wait_ge(made, t + 1)
                    if before is not None:
                        o_.do(dve.tensor_tensor(y[:, t, :], k.ps[:, 4 + t, 0:D], before[0], ALU.add))
                        o_.do(dve.tensor_tensor(y[:, t, :], y[:, t, :], before[1](t), ALU.add))
                    dve.bn_stats(stat[:, t, :], summand(t)).then_inc(stats, 1)
                    dve.wait_ge(stats, t + 1)
                    dve.bn_aggr(mv[:, t, :], stat[:, t, :]).then_inc(aggr, 1)
                dve.wait_ge(rstd, 1)
                dve.wait_ge(aggr, TT)
                for t in range(TT):
                    o_.do(dve.tensor_scalar(y[:, t, :], summand(t), mv[:, t, 0:1], rs[:, 1, t:t + 1],
                                            ALU.subtract, ALU.mult))
                    o_.do(dve.tensor_tensor(y[:, t, :], y[:, t, :], gain_row, ALU.mult))
                    o_.do(dve.tensor_tensor(y[:, t, :], y[:, t, :], offset_row, ALU.add))
                    dve.tensor_tensor(x(t), x(t), y[:, t, :], ALU.add).then_inc(summed, 1)

            if gain_row is not None:
                @block.gpsimd
                def _(pool):
                    pool.wait_ge(aggr, TT)
                    pool.tensor_scalar(rs[:, 0, :], mv[:, :, 1], EPS, 1.0, ALU.add, ALU.mult).then_inc(shifted, 1)
                    pool.wait_ge(shifted, 1)
                    pool.tensor_tensor(rs[:, 1, :], rs[:, 0, :], k.half[:, 0:TT], ALU.pow).then_inc(rstd, 1)


def head_columns(k, dst, src, mask8, width):
    nc = k.nc
    with signals(nc, "masked") as (masked,), nc.Block() as block:
        @block.vector
        def _(dve):
            for h in range(16):
                dve.tensor_scalar(dst[:, h, 0:width], src[:, h // 8, 0:width], mask8[:, h % 8:h % 8 + 1], None,
                                  ALU.mult).then_inc(masked, 1)


def l0_xattn(k):
    nc = k.nc
    NK = 64
    with ExitStack() as st:
        wq, wk, wv, wo = (k.weight("L0_xattn_" + n, st) for n in ("wq", "wk", "wv", "wo"))
        ctxT = k.weight("ctx_T", st)
        mask8 = k.const("head_mask8", st)
        logw = k.weight("L0_side", st)
        k.load(wq, wk, wv, wo, ctxT, mask8, logw)
        kT = k.sb("keys_T", [P, KC, B, NK], st)
        v = k.sb("values", [NK, B, D], st)
        project(k, [Product(kT[:, c, :, :].rearrange("p b n -> p (b n)"),
                            [(wk[:, i, c * P:(c + 1) * P], ctxT[:, i, :]) for i in range(KC)], P, B * NK,
                            add=k.vec("L0_xattn_bk")[:, c:c + 1]) for c in range(KC)] +
                [Product(v[:, b, :], [(ctxT[:, i, b * NK:(b + 1) * NK], wv[:, i, :]) for i in range(KC)], NK, D,
                         row=k.row("L0_xattn_bv")[0:NK, :]) for b in range(B)])
        with signals(nc, "shifted", "logged") as (shifted, logged), nc.Block() as block:
            @block.vector
            def _(dve):
                dve.tensor_scalar(logw[:, 0, :], logw[:, 0, :], 1e-20, 2.0 ** 20, ALU.add,
                                  ALU.mult).then_inc(shifted, 1)
                dve.wait_ge(logged, 1)
                dve.tensor_scalar(logw[:, 0, :], logw[:, 0, :], -20 * float(np.log(2.0)), None,
                                  ALU.add).then_inc(shifted, 1)

            @block.scalar
            def _(act):
                act.wait_ge(shifted, 1)
                act.activation(logw[:, 0, :], logw[:, 0, :], ACT.Ln).then_inc(logged, 1)

        qT = k.sb("queries_T", [P, KC, T], st)
        km = k.sb("keys_by_head", [P, 16, NK], st)
        lw = k.sb("log_weights", [P, NK], st)
        vb = k.sb("values_batch", [NK, D], st)
        kb = k.sb("keys_batch", [P, KC, NK], st)
        o = k.sb("attended", [P, TT, D], st)
        with nc.Fori(0, B) as b:
            normed_batch(k, b, twice=False)
            with signals(nc, "picked") as (picked,), nc.Block() as block:
                @block.vector
                def _(dve):
                    dve.tensor_copy(kb[:, :, :], kT[:, :, bass.ds(b, 1), :].rearrange("p c o n -> p c (o n)"))\
                        .then_inc(picked, 1)
                    dve.tensor_copy(vb[:, :], v[:, bass.ds(b, 1), :].rearrange("p o n -> p (o n)"))\
                        .then_inc(picked, 1)
                    dve.tensor_copy(lw[:, :], logw[:, 0, bass.ds(b * NK, NK)]).then_inc(picked, 1)
            head_columns(k, km, kb, mask8, NK)
            project(k, [Product(qT[:, c, :], [(wq[:, i, c * P:(c + 1) * P], k.xnT[:, i, :]) for i in range(KC)],
                                P, T, add=k.vec("L0_xattn_bq")[:, c:c + 1], mult=0.25) for c in range(KC)])
            attend(k, [Item(NK, [(qT[:, h // 8, t * P:(t + 1) * P], km[:, h, :], 0, NK)],
                            [(NK, vb[:, h * 16:(h + 1) * 16])], o[:, t, h * 16:(h + 1) * 16],
                            mask=(0, NK, lw[:, :])) for h in range(16) for t in range(TT)], 16)
            output_projection(k, b, o, wo, D, bias_row=k.row("L0_xattn_bo"))


def l2_attn(k):
    nc = k.nc
    with ExitStack() as st:
        wq, wk, wv, wo = (k.weight("L2_attn_" + n, st) for n in ("Wq", "Wk", "Wv", "Wo"))
        mask8 = k.const("head_mask8", st)
        block_mask = k.const("block_mask", st)
        k.load(wq, wk, wv, wo, mask8, block_mask)
        qT = k.sb("queries_T", [P, KC, T], st)
        kT = k.sb("keys_T", [P, KC, T], st)
        km = k.sb("keys_by_head", [P, 16, T], st)
        v = k.sb("values", [P, TT, D], st)
        o = k.sb("attended", [P, TT, D], st)
        with nc.Fori(0, B) as b:
            normed_batch(k, b, twice=False)
            project(k, [Product(qT[:, c, :], [(wq[:, i, c * P:(c + 1) * P], k.xnT[:, i, :]) for i in range(KC)],
                                P, T, add=k.vec("L2_attn_bq")[:, c:c + 1], mult=k.vec("L2_scale")[:, 0:1])
                        for c in range(KC)] +
                    [Product(kT[:, c, :], [(wk[:, i, c * P:(c + 1) * P], k.xnT[:, i, :]) for i in range(KC)],
                             P, T, add=k.vec("L2_attn_bk")[:, c:c + 1]) for c in range(KC)] +
                    [Product(v[:, t, :], [(k.xnT[:, i, t * P:(t + 1) * P], wv[:, i, :]) for i in range(KC)],
                             P, D, row=k.row("L2_attn_bv")) for t in range(TT)])
            head_columns(k, km, kT, mask8, T)
            attend(k, [Item(T - t * P, [(qT[:, h // 8, t * P:(t + 1) * P], km[:, h, t * P:T], 0, T - t * P)],
                            [(P, v[:, c, h * 16:(h + 1) * 16]) for c in range(t, TT)],
                            o[:, t, h * 16:(h + 1) * 16], mask=(0, P, block_mask[:, :]))
                       for h in range(16) for t in range(TT)], 16)
            output_projection(k, b, o, wo, D, bias_row=k.row("L2_attn_bo"))


def unit_heads(k, units, src, w, inv_width, floor, HG):
    nc, N = k.nc, len(units)
    with ExitStack() as st, signals(nc, "made", "squared", "summed", "floored", "inverted", "scaled", "turned",
                                    "moved") as (made, squared, summed, floored, inverted, scaled, turned, moved):
        sq = k.sb("squares", [P, 2, 512], st)
        un = k.sb("unit_rows", [P, 2, 512], st)
        ss = k.sb("square_sum", [P, 2, 3, 8], st)
        with nc.Block() as block:
            @block.tensor
            def _(pe):
                for i in range(N + 1):
                    if i < N:
                        t0, n, c0, _, _ = units[i]
                        if i >= 4:
                            pe.wait_ge(scaled, i - 3)
                        for c in range(KC):
                            last = pe.matmul(k.ps[0:n, i % 4, :], src[:, c, t0:t0 + n], w[:, c, c0:c0 + 512],
                                             start=c == 0, stop=c == KC - 1)
                        last.then_inc(made, 1)
                    if i >= 1:
                        j = i - 1
                        n = units[j][1]
                        pe.wait_ge(scaled, j + 1)
                        if j >= 2:
                            pe.wait_ge(moved, j - 1)
                        for c in range(4):
                            last = pe.transpose(k.ps[:, 4 + j % 2, c * n:(c + 1) * n],
                                                un[0:n, j % 2, c * P:(c + 1) * P], k.ident[0:n, 0:n])
                        last.then_inc(turned, 1)

            @block.scalar
            def _(act):
                for i in range(N + 1):
                    if i < N:
                        n = units[i][1]
                        act.wait_ge(made, i + 1)
                        if i >= 2:
                            act.wait_ge(summed, i - 1)
                        act.activation(sq[0:n, i % 2, :], k.ps[0:n, i % 4, :], ACT.Square).then_inc(squared, 1)
                    if i >= 1:
                        _, n, _, dst, gain = units[i - 1]
                        act.wait_ge(turned, i)
                        act.mul(dst, k.ps[:, 4 + (i - 1) % 2, 0:4 * n].rearrange("p (c n) -> p c n", c=4),
                                gain).then_inc(moved, 1)

            @block.vector
            def _(dve):
                for i in range(N):
                    n = units[i][1]
                    dve.wait_ge(squared, i + 1)
                    if i >= 2:
                        dve.wait_ge(floored, i - 1)
                    dve.reduce_sum(ss[0:n, i % 2, 0, :], sq[0:n, i % 2, :].rearrange("p (h d) -> p h d", h=8),
                                   AX.X).then_inc(summed, 1)
                    dve.wait_ge(inverted, i + 1)
                    if i >= 2:
                        dve.wait_ge(turned, i - 1)
                    dve.tensor_tensor(un[0:n, i % 2, :].rearrange("p (h d) -> p h d", h=8),
                                      k.ps[0:n, i % 4, :].rearrange("p (h d) -> p h d", h=8),
                                      ss[0:n, i % 2, 2, :].unsqueeze(2).to_broadcast([n, 8, 64]),
                                      ALU.mult).then_inc(scaled, 1)

            @block.gpsimd
            def _(pool):
                for i in range(N):
                    n = units[i][1]
                    pool.wait_ge(summed, i + 1)
                    pool.tensor_scalar(ss[0:n, i % 2, 1, :], ss[0:n, i % 2, 0, :], inv_width, floor, ALU.mult,
                                       ALU.max).then_inc(floored, 1)
                    pool.wait_ge(floored, i + 1)
                    if i >= 2:
                        pool.wait_ge(scaled, i - 1)
                    pool.tensor_tensor(ss[0:n, i % 2, 2, :], ss[0:n, i % 2, 1, :], k.half[0:n, 0:8],
                                       ALU.pow).then_inc(inverted, 1)


def latent_attention(k, pre, H, names, unit=None, mask=None, **out_rows):
    nc = k.nc
    NC = 64
    W = H * 64
    NK = T + NC
    PAIRS = W // P
    lg, lb, cg, cb, w_out = names
    with ExitStack() as st:
        wq, wkv, wo = (k.weight(pre + n, st) for n in ("Wq", "Wkv", w_out))
        ctx = k.const("ctx_rows", st)
        kmask = k.weight(mask, st) if mask else None
        k.load(wq, wkv, wo, ctx, *([kmask] if mask else []))
        ctxT = k.sb("context_T", [P, KC, B * NC], st)
        cn = k.sb("context_normed", [P, B, D], st)
        with signals(nc, *norm_names("c_")) as sems, ExitStack() as cs:
            n = Norm(k, cs, sems, "c", twice=False, gain=k.vec(pre + cg), offset=k.vec(pre + cb), tiles=B, rows=NC)
            with nc.Block() as block:
                @block.vector
                def _(dve):
                    n.dve(dve, lambda t: ctx[:, t, :], cn)

                @block.gpsimd
                def _(pool):
                    n.pool(pool)

                @block.tensor
                def _(pe):
                    n.pe(pe, cn, (6, 7))

                @block.scalar
                def _(act):
                    n.act(act, ctxT, (6, 7))
        kvT = k.sb("kv_input_T", [P, KC, NK], st)
        qT = k.sb("queries_T", [P, PAIRS, T], st)
        kT = k.sb("keys_T", [P, PAIRS, NK], st)
        v = k.sb("values", [P, TT + 1, W], st)
        km = k.sb("key_mask", [P, NC], st) if mask else None
        o = k.sb("attended", [P, TT, W], st)
        with nc.Fori(0, B) as b:
            normed_batch(k, b, gain=k.vec(pre + lg), offset=k.vec(pre + lb), dst=kvT)
            with signals(nc, "picked") as (picked,), nc.Block() as block:
                @block.vector
                def _(dve):
                    dve.tensor_copy(kvT[:, :, T:NK], ctxT[:, :, bass.ds(b * NC, NC)]).then_inc(picked, 1)
                    if mask:
                        dve.tensor_scalar(km[:, :], kmask[:, 0, bass.ds(b * NC, NC)], 1.0, -1.0, ALU.min,
                                          ALU.add).then_inc(picked, 1)
                        dve.wait_ge(picked, 2)
                        dve.tensor_scalar(km[:, :], km[:, :], 1e30, None, ALU.mult).then_inc(picked, 1)
            values = [Product(v[0:n, t, a * 512:(a + 1) * 512],
                              [(kvT[:, i, t * P:t * P + n], wkv[:, i, W + a * 512:W + (a + 1) * 512])
                               for i in range(KC)], n, 512)
                      for t, n in enumerate([P] * TT + [NC]) for a in range(W // 512)]
            if unit is None:
                project(k, [Product(qT[:, j, :], [(wq[:, i, j * P:(j + 1) * P], kvT[:, i, 0:T])
                                                  for i in range(KC)], P, T, mult=0.125) for j in range(PAIRS)] +
                        [Product(kT[:, j, c0:c1], [(wkv[:, i, j * P:(j + 1) * P], kvT[:, i, c0:c1])
                                                   for i in range(KC)], P, c1 - c0)
                         for j in range(PAIRS) for c0, c1 in ((0, T), (T, NK))] + values)
            else:
                inv_width, floor, qg, kg = unit
                for w, dst, gain, last in ((wq, qT, qg, TT), (wkv, kT, kg, TT + 1)):
                    unit_heads(k, [(t * P, P if t < TT else NC, a * 512,
                                    dst[:, 4 * a:4 * a + 4, t * P:t * P + (P if t < TT else NC)], gain)
                                   for t in range(last) for a in range(W // 512)], kvT, w, inv_width, floor, 8)
                project(k, values)
            items = []
            for h in range(H):
                r = slice(64 * (h % 2), 64 * (h % 2) + 64)
                for t in range(TT):
                    q = qT[r, h // 2, t * P:(t + 1) * P]
                    items.append(Item(NK, [(q, kT[r, h // 2, 0:T], 0, T), (q, kT[r, h // 2, T:NK], T, NC)],
                                      [(n, v[0:n, c, h * 64:(h + 1) * 64]) for c, n in enumerate([P] * TT + [NC])],
                                      o[:, t, h * 64:(h + 1) * 64],
                                      mask=(T, NC, km[:, :]) if mask else None))
            attend(k, items, 64)
            output_projection(k, b, o, wo, W, **out_rows)


def l1_xattn(k):
    latent_attention(k, "L1_xattn_", 16, ("ln_l_g", "ln_l_b", "ln_m_g", "ln_m_b", "Wout"))


def l2_xattn(k):
    latent_attention(k, "L2_xattn_", 16, ("ln_l_g", "ln_l_b", "ln_x_g", "ln_x_b", "Wout"),
                     unit=(1.0 / 64, 1e-16, k.vec("L2_query_gain")[:, 0:1], k.vec("L2_xattn_kn_g2")[:, 0:1]),
                     mask="mask_bf1", bias_row=k.row("L2_xattn_bout"))


def l3_xattn(k):
    latent_attention(k, "L3_xattn_", 8, ("ln_l_w", "ln_l_b", "ln_x_w", "ln_x_b", "Wo"),
                     unit=(1.0, 1e-24, k.vec("L3_query_gain")[:, 0:1], k.vec("L3_xattn_k_scale2")[:, 0:1]),
                     mask="mask_bk0", gain_row=k.row("L3_xattn_ln_o_w"), offset_row=k.row("L3_xattn_ln_o_b"))



def l1_attn(k):
    nc = k.nc
    C = 16
    NCH = T // C
    PER = P // C
    with ExitStack() as st:
        ws = {n: k.weight("L1_attn_" + n, st) for n in ("Wq", "Wk", "Wv", "Wg", "Wo")}
        mask8 = k.const("head_mask8", st)
        diag = k.const("chunk_diagonal", st)
        k.load(*ws.values(), mask8, diag)
        q = k.sb("queries_decayed", [P, 2, NCH, C], st)
        kT = k.sb("keys_T", [P, NCH, C], st)
        g = k.sb("gates_T", [P, NCH, C], st)
        v = k.sb("values", [P, TT, P], st)
        vj = k.sb("values_by_position", [NCH, C, P], st)
        kd = k.sb("keys_decayed", [P, NCH, C], st)
        kdt = k.sb("keys_decayed_rows", [P, TT, P], st)
        r = k.sb("suffix_gates", [P, NCH], st)
        a = k.sb("scores_diagonal", [NCH, 2, NCH * C], st)
        vm = k.sb("values_by_chunk", [P, TT, PER, P], st)
        state = k.sb("states", [P, NCH + 1, P], st)
        zero = k.sb("zeros", [P, T], st)
        oT = k.sb("attended_T", [P, 1, T], st)
        with signals(nc, "zeroed") as (zeroed,), nc.Block() as block:
            @block.gpsimd
            def _(pool):
                pool.memset(zero[:, :], 0.0).then_inc(zeroed, 1)
                pool.memset(state[:, 0, :], 0.0).then_inc(zeroed, 1)
        with nc.Fori(0, B) as b:
            normed_batch(k, b, twice=False)
            flat = lambda w: w.rearrange("p c j -> p (c j)")
            positions = k.xnT[:, :, :].rearrange("p i (c j) -> p i c j", j=C)
            project(k, [Product(flat(dst), [(ws[n][:, i, :], k.xnT[:, i, :]) for i in range(KC)], P, T,
                                add=k.vec("L1_attn_b" + n[1])[:, 0:1])
                        for n, dst in (("Wg", g[:, :, :]), ("Wq", q[:, 0, :, :]), ("Wq", q[:, 1, :, :]),
                                       ("Wk", kT[:, :, :]))] +
                    [Product(v[:, t, :], [(k.xnT[:, i, t * P:(t + 1) * P], ws["Wv"][:, i, :]) for i in range(KC)],
                             P, P, row=k.row("L1_attn_bv")) for t in range(TT)] +
                    [Product(vj[:, j, :], [(positions[:, i, :, j], ws["Wv"][:, i, :]) for i in range(KC)],
                             NCH, P, row=k.row("L1_attn_bv")[0:NCH, :]) for j in range(C)])
            with signals(nc, "gated", "scored", "scored_diag", "decayed", "order", "within", "spread", "turned",
                         "moved", "kv_made", "carried", "outed") as (
                    gated, scored, scored_diag, decayed, order, within, spread, turned, moved, kv_made, carried,
                    outed), nc.Block() as block:
                @block.scalar
                def _(act):
                    act.activation(g[:, :, :], g[:, :, :], ACT.Sigmoid).then_inc(gated, 1)
                    act.wait_ge(turned, 1)
                    act.copy(kdt[:, :, :], k.ps[:, 3, :].rearrange("p (t s) -> p t s", t=TT)).then_inc(moved, 1)
                    act.wait_ge(outed, 1)
                    act.copy(oT[:, 0, :], k.ps[:, 2, :]).then_inc(moved, 1)

                @block.gpsimd
                def _(pool):
                    for t in range(TT):
                        pool.tensor_tensor(vm[:, t, :, :], v[:, t, :].unsqueeze(1).to_broadcast([P, PER, P]),
                                           mask8[:, :].unsqueeze(2).to_broadcast([P, PER, P]),
                                           ALU.mult).then_inc(spread, 1)

                @block.vector
                def _(dve):
                    o = Order(dve, order)
                    o.mark(dve.memset(r[:, :], 1.0))
                    dve.wait_ge(gated, 1)
                    for n in range(C):
                        j = C - 1 - n
                        w = C - j
                        src, dst = q[:, n % 2, :, j:C], q[:, (n + 1) % 2, :, j:C]
                        o.wait()
                        o.mark(dve.tensor_tensor(kd[:, :, j], kT[:, :, j], r[:, :], ALU.mult))
                        if n >= 1:
                            dve.wait_ge(scored, n)
                            dve.wait_ge(decayed, n)
                        dve.tensor_tensor(dst, src, g[:, :, j:j + 1].to_broadcast([P, NCH, w]),
                                          ALU.mult).then_inc(decayed, 1)
                        o.wait()
                        o.mark(dve.tensor_tensor(r[:, :], r[:, :], g[:, :, j], ALU.mult))
                        dve.wait_ge(scored, n + 1)
                        if n >= 2:
                            dve.wait_ge(within, n - 1)
                        dve.tensor_tensor(a[:, n % 2, 0:NCH * w].rearrange("p (c i) -> p c i", i=w),
                                          k.ps[0:NCH, n % 2, 0:NCH * w].rearrange("p (c i) -> p c i", i=w),
                                          diag[:, :].unsqueeze(2).to_broadcast([NCH, NCH, w]),
                                          ALU.mult).then_inc(scored_diag, 1)
                    o.wait()
                    for c in range(NCH):
                        dve.wait_ge(kv_made, c // 4 + 1)
                        if c:
                            dve.wait_ge(carried, c)
                        dve.scalar_tensor_tensor(out=state[:, c + 1, :], in0=state[:, c, :], scalar=r[:, c:c + 1],
                                                 in1=k.ps[:, 4 + (c // 4) % 4, (c % 4) * P:(c % 4 + 1) * P],
                                                 op0=ALU.mult, op1=ALU.add).then_inc(carried, 1)

                @block.tensor
                def _(pe):
                    pe.matmul(k.ps[:, 2, :], zero[0:1, 0:P], zero[0:1, :], start=True, stop=False,
                              skip_group_check=True)
                    out = k.ps[:, 2, :].rearrange("p (c i) -> p c i", i=C)

                    def add_within(n):
                        j = C - 1 - n
                        w = C - j
                        pe.wait_ge(scored_diag, n + 1)
                        pe.matmul(out[:, :, j:C], vj[:, j, :],
                                  a[:, n % 2, 0:NCH * w].rearrange("p (c i) -> p c i", i=w), start=False,
                                  stop=False, skip_group_check=True).then_inc(within, 1)

                    for n in range(C):
                        j = C - 1 - n
                        w = C - j
                        if n >= 1:
                            pe.wait_ge(decayed, n)
                        if n >= 2:
                            pe.wait_ge(scored_diag, n - 1)
                        pe.matmul(k.ps[0:NCH, n % 2, 0:NCH * w].rearrange("p (c i) -> p c i", i=w), kT[:, :, j],
                                  q[:, n % 2, :, j:C], start=True, stop=True).then_inc(scored, 1)
                        if n >= 1:
                            add_within(n - 1)
                    add_within(C - 1)
                    pe.wait_ge(order, 2 * C)
                    flat_kd = flat(kd[:, :, :])
                    for t in range(TT):
                        last = pe.transpose(k.ps[:, 3, t * P:(t + 1) * P], flat_kd[:, t * P:(t + 1) * P],
                                            k.ident[:, :])
                    last.then_inc(turned, 1)
                    pe.wait_ge(moved, 1)
                    pe.wait_ge(spread, TT)
                    for u in range(2 * TT):
                        if u >= 4:
                            pe.wait_ge(carried, 4 * (u - 3))
                        pe.matmul(k.ps[:, 4 + u % 4, :], kdt[:, u // 2, :],
                                  vm[:, u // 2, 4 * (u % 2):4 * (u % 2) + 4, :].rearrange("p c v -> p (c v)"),
                                  start=True, stop=True).then_inc(kv_made, 1)
                    pe.wait_ge(decayed, C)
                    for c in range(NCH):
                        if c:
                            pe.wait_ge(carried, c)
                        last = pe.matmul(out[:, c, :], state[:, c, :], q[:, C % 2, c, :], start=False,
                                         stop=c == NCH - 1, skip_group_check=True)
                    last.then_inc(outed, 1)
            output_projection(k, b, None, ws["Wo"], P, oT=oT, gain_row=k.row("L1_attn_gamma"),
                              offset_row=k.row("L1_attn_beta"),
                              before=(k.row("L1_attn_bo"), lambda t: k.xn[:, t, :]))



def l1_ffn(k):
    nc = k.nc
    NG = 16
    KEYS = 32
    QC = 4
    with ExitStack() as st:
        wq, down, up = (k.weight(n, st) for n in ("L1_ffn_Wq", "L1_ffn_expert_down", "L1_ffn_expert_up"))
        keys = k.weight("L1_sub_keys", st)
        pair_mean = k.const("pair_mean", st)
        group4 = k.const("group_of_32", st)
        k.load(wq, down, up, keys, pair_mean, group4)
        q = k.sb("queries_T", [P, QC, B * T], st)
        stat = k.sb("query_stat", [P, B * QC, 6], st)
        mv = k.sb("query_mv", [P, 2], st)
        col = k.sb("query_columns", [P, 8], st)
        with signals(nc, "squared", "summed", "floored", "inverted", "unit") as (
                squared, summed, floored, inverted, unit), ExitStack() as ks, nc.Block() as block:
            k2 = k.sb("keys_squared", [P, 3, P], ks)

            @block.vector
            def _(dve):
                dve.tensor_tensor(k2[:, 0, :], keys[:, 0, :], keys[:, 0, :], ALU.mult).then_inc(squared, 1)
                dve.wait_ge(summed, 1)
                dve.tensor_scalar(k2[:, 1, :], k.ps[:, 0, 0:P], 1e-24, None, ALU.max).then_inc(floored, 1)
                dve.wait_ge(inverted, 1)
                dve.tensor_tensor(keys[:, 0, :], keys[:, 0, :], k2[:, 2, :], ALU.mult).then_inc(unit, 1)

            @block.tensor
            def _(pe):
                pe.wait_ge(squared, 1)
                pe.matmul(k.ps[:, 0, 0:P], k.ones[:, :], k2[:, 0, :], start=True, stop=True).then_inc(summed, 1)

            @block.gpsimd
            def _(pool):
                pool.wait_ge(floored, 1)
                pool.tensor_tensor(k2[:, 2, :], k2[:, 1, :], k.half[:, 0:1].to_broadcast([P, P]),
                                   ALU.pow).then_inc(inverted, 1)

        with nc.Fori(0, B) as b:
            normed_batch(k, b, twice=False)
            project(k, [Product(q[:, c, bass.ds(b * T, T)], [(wq[:, i, c * P:(c + 1) * P], k.xnT[:, i, :])
                                                             for i in range(KC)], P, T,
                                add=k.vec("L1_ffn_bq")[:, c:c + 1]) for c in range(QC)])
            with signals(nc, "stats") as (stats,), nc.Block() as block:
                @block.vector
                def _(dve):
                    for c in range(QC):
                        dve.bn_stats(stat[:, bass.ds(b * QC + c, 1), :].rearrange("p o s -> p (o s)"),
                                     q[:, c, bass.ds(b * T, T)]).then_inc(stats, 1)

        with signals(nc, "order", "aggregated", "averaged", "deviated", "spread", "shifted", "inverted") as (
                order, aggregated, averaged, deviated, spread, shifted, inverted), nc.Block() as block:
            @block.vector
            def _(dve):
                o = Order(dve, order)
                dve.bn_aggr(mv[:, :], stat[:, :, :].rearrange("p a s -> p (a s)")).then_inc(aggregated, 1)
                dve.wait_ge(averaged, 1)
                o.do(dve.tensor_copy(col[:, 0:2], k.ps[:, 0, 0:2]))
                dve.wait_ge(aggregated, 1)
                o.do(dve.tensor_tensor(col[:, 2:3], mv[:, 0:1], col[:, 0:1], ALU.subtract))
                o.do(dve.tensor_tensor(col[:, 3:4], col[:, 2:3], col[:, 2:3], ALU.mult))
                dve.tensor_copy(col[:, 2:3], col[:, 3:4]).then_inc(deviated, 1)
                dve.wait_ge(spread, 1)
                dve.tensor_tensor(col[:, 4:5], k.ps[:, 1, 0:1], col[:, 1:2], ALU.add).then_inc(deviated, 1)
                dve.wait_ge(inverted, 1)
                o.do(dve.tensor_tensor(col[:, 6:7], col[:, 5:6], k.vec("L1_bn_gamma2"), ALU.mult))
                o.do(dve.tensor_tensor(col[:, 7:8], col[:, 0:1], col[:, 6:7], ALU.mult))
                o.do(dve.tensor_tensor(col[:, 7:8], k.vec("L1_bn_beta2"), col[:, 7:8], ALU.subtract))

            @block.tensor
            def _(pe):
                pe.wait_ge(aggregated, 1)
                pe.matmul(k.ps[:, 0, 0:2], pair_mean[:, :], mv[:, :], start=True, stop=True).then_inc(averaged, 1)
                pe.wait_ge(deviated, 1)
                pe.matmul(k.ps[:, 1, 0:2], pair_mean[:, :], col[:, 2:4], start=True, stop=True).then_inc(spread, 1)

            @block.gpsimd
            def _(pool):
                pool.wait_ge(deviated, 2)
                pool.tensor_scalar(col[:, 5:6], col[:, 4:5], EPS, 1.0, ALU.add, ALU.mult).then_inc(shifted, 1)
                pool.wait_ge(shifted, 1)
                pool.tensor_tensor(col[:, 5:6], col[:, 5:6], k.half[:, 0:1], ALU.pow).then_inc(inverted, 1)

        qn = k.sb("queries_normed", [P, QC, T], st)
        sq = k.sb("queries_squared", [P, QC, T], st)
        gel = k.sb("expert_hidden", [P, TT, D], st)
        s = k.sb("key_scores", [P, TT, NG, KEYS + 4], st)
        marked = k.sb("key_marked", [P, 2, NG, KEYS + 4], st)
        top = k.sb("key_top", [P, TT, NG, 8], st)
        e = k.sb("key_exp", [P, TT, NG, KEYS], st)
        m = k.sb("key_mask", [P, TT, NG, KEYS], st)
        nrm = k.sb("query_norms", [P, TT, 2, NG], st)
        tot = k.sb("key_sums", [P, TT, 2, NG], st)
        pairs = k.sb("pair_weights", [P, 2, 8, D], st)
        w = k.sb("expert_weights", [P, TT, D], st)
        wt = k.sb("expert_weights_T", [P, KC, T], st)
        far = k.sb("far_weight", [P, TT], st)
        x_ = None
        with signals(nc, "sentinels") as (sentinels,), nc.Block() as block:
            @block.vector
            def _(dve):
                dve.memset(s[:, :, :, KEYS:KEYS + 4], BIG).then_inc(sentinels, 1)
        with nc.Fori(0, B) as b:
            normed_batch(k, b, twice=False)
            x_ = batch_tiles(k, b)
            with signals(nc, "q_normed", "q_squared", "hid_made", "gelued", "scored", "floored", "inverted",
                         "scaled", "topped", "marked", "masked", "below", "exped", "order", "shared", "paired",
                         "summed", "weighted", "turned", "moved", "made", "added") as (
                    q_normed, q_squared, hid_made, gelued, scored, floored, inverted, scaled, topped, marked_s,
                    masked, below, exped, order, shared, paired, summed, weighted, turned, moved, made,
                    added), nc.Block() as block:
                @block.scalar
                def _(act):
                    for c in range(QC):
                        act.activation(qn[:, c, :], q[:, c, bass.ds(b * T, T)], ACT.Identity, bias=col[:, 7:8],
                                       scale=col[:, 6:7]).then_inc(q_normed, 1)
                    act.wait_ge(q_normed, QC)
                    for c in range(QC):
                        act.activation(sq[:, c, :], qn[:, c, :], ACT.Square).then_inc(q_squared, 1)
                    for t in range(TT):
                        act.wait_ge(hid_made, t + 1)
                        act.activation(gel[:, t, :], k.ps[:, 4 + t, 0:D], ACT.Gelu).then_inc(gelued, 1)
                    for t in range(TT):
                        act.wait_ge(below, t + 1)
                        act.activation(e[:, t, :, :], e[:, t, :, :], ACT.Exp).then_inc(exped, 1)
                    for c in range(KC):
                        act.wait_ge(turned, c + 1)
                        act.copy(wt[:, c, :], k.ps[:, c, :]).then_inc(moved, 1)

                @block.tensor
                def _(pe):
                    for t in range(TT):
                        for c in range(KC):
                            last = pe.matmul(k.ps[:, 4 + t, 0:D], k.xnT[:, c, t * P:(t + 1) * P], down[:, c, :],
                                             start=c == 0, stop=c == KC - 1)
                        last.then_inc(hid_made, 1)
                    pe.wait_ge(q_squared, QC)
                    for t in range(TT):
                        if t >= 2:
                            pe.wait_ge(scaled, t - 1)
                        for c in range(QC):
                            pe.matmul(k.ps[:, t % 2, c * P:(c + 1) * P], qn[:, c, t * P:(t + 1) * P],
                                      keys[:, 0, :], start=True, stop=True)
                        for c in range(QC):
                            last = pe.matmul(k.ps[:, 2 + t % 2, 4 * c:4 * c + 4], sq[:, c, t * P:(t + 1) * P],
                                             group4[:, :], start=True, stop=True)
                        last.then_inc(scored, 1)
                    pe.wait_ge(weighted, TT)
                    for c in range(KC):
                        for t in range(TT):
                            last = pe.transpose(k.ps[:, c, t * P:(t + 1) * P], w[:, t, c * P:(c + 1) * P],
                                                k.ident[:, :])
                        last.then_inc(turned, 1)
                    pe.wait_ge(moved, KC)
                    for t in range(TT):
                        for c in range(KC):
                            last = pe.matmul(k.ps[:, 4 + t, 0:D], wt[:, c, t * P:(t + 1) * P], up[:, c, :],
                                             start=c == 0, stop=c == KC - 1)
                        last.then_inc(made, 1)

                @block.gpsimd
                def _(pool):
                    for t in range(TT):
                        pool.wait_ge(floored, t + 1)
                        pool.tensor_tensor(nrm[:, t, 1, :], nrm[:, t, 0, :], k.half[:, 0:NG],
                                           ALU.pow).then_inc(inverted, 1)
                    for t in range(TT):
                        pool.wait_ge(shared, t + 1)
                        if t >= 2:
                            pool.wait_ge(summed, t - 1)
                        halves = e[:, t, :, :].rearrange("p (h s) n -> p h s n", s=2)
                        for h in range(8):
                            last = pool.tensor_tensor(
                                pairs[:, t % 2, h, :].rearrange("p (a c) -> p a c", a=8),
                                halves[:, h, 0, 0:8].unsqueeze(2).to_broadcast([P, 8, KEYS]),
                                halves[:, h, 1, :].unsqueeze(1).to_broadcast([P, 8, KEYS]), ALU.mult)
                            last.then_inc(paired, 1)

                @block.vector
                def _(dve):
                    o = Order(dve, order)
                    for t in range(TT):
                        dve.wait_ge(scored, t + 1)
                        dve.tensor_scalar(nrm[:, t, 0, :], k.ps[:, 2 + t % 2, 0:NG], 1e-24, None,
                                          ALU.max).then_inc(floored, 1)
                        dve.wait_ge(inverted, t + 1)
                        dve.tensor_tensor(s[:, t, :, 0:KEYS],
                                          k.ps[:, t % 2, :].rearrange("p (g n) -> p g n", g=NG),
                                          nrm[:, t, 1, :].unsqueeze(2).to_broadcast([P, NG, KEYS]),
                                          ALU.mult).then_inc(scaled, 1)
                    for t in range(TT):
                        dve.wait_ge(scaled, t + 1)
                        for g in range(NG):
                            dve.max(top[:, t, g, :], s[:, t, g, :]).then_inc(topped, 1)
                        dve.wait_ge(topped, NG * (t + 1))
                        if t >= 2:
                            dve.wait_ge(masked, t - 1)
                        for g in range(NG):
                            dve.match_replace(marked[:, t % 2, g, :], top[:, t, g, :], s[:, t, g, :],
                                              -BIG).then_inc(marked_s, 1)
                        o.do(dve.tensor_tensor(e[:, t, :, :], s[:, t, :, 0:KEYS],
                                               top[:, t, :, 4:5].to_broadcast([P, NG, KEYS]), ALU.subtract))
                        dve.tensor_scalar(e[:, t, :, :], e[:, t, :, :], 0.0, None, ALU.min).then_inc(below, 1)
                        dve.wait_ge(marked_s, NG * (t + 1))
                        dve.tensor_scalar(m[:, t, :, :], marked[:, t % 2, :, 0:KEYS], -BIG, None,
                                          ALU.is_equal).then_inc(masked, 1)
                    for t in range(TT):
                        dve.wait_ge(exped, t + 1)
                        dve.wait_ge(masked, t + 1)
                        o.do(dve.tensor_tensor(e[:, t, :, :], e[:, t, :, :], m[:, t, :, :], ALU.mult))
                        o.do(dve.reduce_sum(tot[:, t, 0, :], e[:, t, :, :], AX.X))
                        o.do(dve.reciprocal(tot[:, t, 1, :], tot[:, t, 0, :]))
                        dve.tensor_tensor(e[:, t, :, :], e[:, t, :, :],
                                          tot[:, t, 1, :].unsqueeze(2).to_broadcast([P, NG, KEYS]),
                                          ALU.mult).then_inc(shared, 1)
                    for t in range(TT):
                        dve.wait_ge(shared, t + 1)
                        o.do(dve.tensor_reduce(far[:, t:t + 1], e[:, t, :, :].rearrange(
                            "p (h s) n -> p h s n", s=2)[:, :, 0, 8:KEYS], AX.XY, ALU.add))
                        dve.wait_ge(paired, 8 * (t + 1))
                        dve.tensor_reduce(w[:, t, :], pairs[:, t % 2, :, :].rearrange("p h n -> p n h"), AX.X,
                                          ALU.add).then_inc(summed, 1)
                        dve.wait_ge(summed, t + 1)
                        o.do(dve.tensor_tensor(w[:, t, D - 1:D], w[:, t, D - 1:D], far[:, t:t + 1], ALU.add))
                        dve.wait_ge(gelued, t + 1)
                        dve.tensor_tensor(w[:, t, :], w[:, t, :], gel[:, t, :], ALU.mult).then_inc(weighted, 1)
                    for t in range(TT):
                        dve.wait_ge(made, t + 1)
                        dve.tensor_tensor(x_(t), x_(t), k.ps[:, 4 + t, 0:D], ALU.add).then_inc(added, 1)



def l3_attn(k):
    nc = k.nc
    S = B
    with ExitStack() as st:
        ws = {n: k.weight("L3_attn_" + n, st) for n in ("w_q", "w_k", "w_v", "w_o")}
        rk, rv = k.const("rel_k_rows", st), k.const("rel_v_rows", st)
        k.load(*ws.values(), rk, rv)
        qkv = [k.sb(n, [P, S, TT, D], st) for n in ("queries", "keys", "values")]
        out = k.sb("attended", [P, S, TT, D], st)
        with nc.Fori(0, B) as b:
            normed_batch(k, b, twice=False)
            project(k, [Product(dst[:, bass.ds(b, 1), t, :].rearrange("p o d -> p (o d)"),
                                [(k.xnT[:, i, t * P:(t + 1) * P], ws[n][:, i, :]) for i in range(KC)], P, D)
                        for n, dst in zip(("w_q", "w_k", "w_v"), qkv) for t in range(TT)])
        qq = k.sb("queries_tile", [P, S, D], st)
        kk = k.sb("keys_relative", [P, 2, S, D], st)
        vv = k.sb("values_relative", [P, 2, S, D], st)
        prod = k.sb("products", [P, 2, S, D], st)
        sc = k.sb("scores", [P, S * S, 16], st)
        red = k.sb("reduced", [P, 3, S * S], st)
        with nc.Fori(0, TT) as j, signals(nc, "keyed", "valued", "multiplied", "weighted", "order", "exped",
                                          "below", "stored") as (
                keyed, valued, multiplied, weighted, order, exped, below, stored), nc.Block() as block:
            q, kt, v = (w[:, :, bass.ds(j, 1), :].rearrange("p s o d -> p s (o d)") for w in qkv)

            @block.gpsimd
            def _(pool):
                for s in range(S):
                    if s >= 2:
                        pool.wait_ge(multiplied, s - 1)
                    pool.tensor_tensor(kk[:, s % 2, :, :], kt, rk[:, S - 1 - s:2 * S - 1 - s, :],
                                       ALU.add).then_inc(keyed, 1)
                for s in range(S):
                    if s >= 2:
                        pool.wait_ge(weighted, s - 1)
                    pool.tensor_tensor(vv[:, s % 2, :, :], v, rv[:, S - 1 - s:2 * S - 1 - s, :],
                                       ALU.add).then_inc(valued, 1)

            @block.scalar
            def _(act):
                act.wait_ge(below, 1)
                act.activation(sc[:, :, :], sc[:, :, :], ACT.Exp, scale=0.25).then_inc(exped, 1)

            @block.vector
            def _(dve):
                o = Order(dve, order)
                o.do(dve.tensor_copy(qq[:, :, :], q))
                for s in range(S):
                    dve.wait_ge(keyed, s + 1)
                    dve.tensor_tensor(prod[:, s % 2, :, :], kk[:, s % 2, :, :],
                                      qq[:, s, :].unsqueeze(1).to_broadcast([P, S, D]),
                                      ALU.mult).then_inc(multiplied, 1)
                    dve.wait_ge(multiplied, s + 1)
                    o.do(dve.reduce_sum(sc[:, S * s:S * s + S, :], prod[:, s % 2, :, :].rearrange(
                        "p t (h d) -> p t h d", d=16), AX.X))
                o.do(dve.tensor_reduce(red[:, 0, :], sc[:, :, :], AX.X, ALU.max))
                dve.tensor_tensor(sc[:, :, :], sc[:, :, :],
                                  red[:, 0, :].unsqueeze(2).to_broadcast([P, S * S, 16]),
                                  ALU.subtract).then_inc(below, 1)
                dve.wait_ge(exped, 1)
                o.do(dve.reduce_sum(red[:, 1, :], sc[:, :, :], AX.X))
                o.do(dve.reciprocal(red[:, 2, :], red[:, 1, :]))
                o.do(dve.tensor_tensor(sc[:, :, :], sc[:, :, :],
                                       red[:, 2, :].unsqueeze(2).to_broadcast([P, S * S, 16]), ALU.mult))
                for s in range(S):
                    dve.wait_ge(valued, s + 1)
                    dve.tensor_tensor(prod[:, s % 2, :, :].rearrange("p t (h d) -> p (t h) d", d=16),
                                      vv[:, s % 2, :, :].rearrange("p t (h d) -> p (t h) d", d=16),
                                      sc[:, S * s:S * s + S, :].rearrange("p t h -> p (t h)").unsqueeze(2)
                                      .to_broadcast([P, S * 16, 16]), ALU.mult).then_inc(weighted, 1)
                    dve.wait_ge(weighted, s + 1)
                    dve.reduce_sum(out[:, s, bass.ds(j, 1), :].rearrange("p o d -> p (o d)"),
                                   prod[:, s % 2, :, :].rearrange("p t d -> p d t"), AX.X).then_inc(stored, 1)
        with nc.Fori(0, B) as b:
            with signals(nc, "picked") as (picked,), nc.Block() as block:
                @block.vector
                def _(dve):
                    dve.tensor_copy(k.xn[:, :, :], out[:, bass.ds(b, 1), :, :].rearrange("p o t d -> p (o t) d"))\
                        .then_inc(picked, 1)
            output_projection(k, b, k.xn, ws["w_o"], D, bias_row=k.row("L3_attn_b_o"))



E = 8


def top_two_gate(k, st, sems, from_sigmoid):
    scored, rowed, picked, exped, combined, turned, ready, order = sems
    row = k.sb("gate_row", [P, TT, 14], st)
    marked = k.sb("gate_marked", [P, TT, 14], st)
    top = k.sb("gate_top", [P, TT, 8], st)
    mask = k.sb("gate_mask", [P, TT, E], st)
    e = k.sb("gate_exp", [P, TT, E], st)
    tot = k.sb("gate_total", [P, TT, 2], st)
    comb = k.sb("gate_combine", [P, TT, E], st)
    combT = k.sb("combine_T", [E, T], st)
    bank = k.ps[:, 7, :]

    def dve_part(dve):
        o = Order(dve, order)
        o.do(dve.memset(row[:, :, E:14], BIG))
        dve.wait_ge(scored, 1)
        if from_sigmoid:
            dve.wait_ge(rowed, 1)
        else:
            dve.tensor_copy(row[:, :, 0:E], bank[:, 0:TT * E].rearrange("p (t e) -> p t e", t=TT)).then_inc(rowed, 1)
            dve.wait_ge(rowed, 1)
        for t in range(TT):
            o.mark(dve.max(top[:, t, :], row[:, t, :]))
        o.wait()
        for t in range(TT):
            o.mark(dve.match_replace(marked[:, t, :], top[:, t, :], row[:, t, :], -BIG))
        o.wait()
        o.do(dve.tensor_scalar(mask[:, :, :], marked[:, :, 0:E], -BIG, None, ALU.is_equal))
        if from_sigmoid:
            o.do(dve.tensor_tensor(e[:, :, :], row[:, :, 0:E], mask[:, :, :], ALU.mult))
        else:
            o.do(dve.tensor_tensor(e[:, :, :], row[:, :, 0:E], top[:, :, 6:7].to_broadcast([P, TT, E]),
                                   ALU.subtract))
            dve.tensor_scalar(e[:, :, :], e[:, :, :], 0.0, None, ALU.min).then_inc(picked, 1)
            dve.wait_ge(exped, 1)
            o.do(dve.tensor_tensor(e[:, :, :], e[:, :, :], mask[:, :, :], ALU.mult))
        o.do(dve.reduce_sum(tot[:, :, 0], e[:, :, :], AX.X))
        if from_sigmoid:
            o.do(dve.tensor_scalar(tot[:, :, 0], tot[:, :, 0], 1e-20, None, ALU.add))
        o.do(dve.reciprocal(tot[:, :, 1], tot[:, :, 0]))
        dve.tensor_tensor(comb[:, :, :], e[:, :, :], tot[:, :, 1:2].to_broadcast([P, TT, E]),
                          ALU.mult).then_inc(combined, 1)

    def act_part(act):
        act.wait_ge(scored, 1)
        if from_sigmoid:
            act.activation(row[:, :, 0:E], bank[:, 0:TT * E].rearrange("p (t e) -> p t e", t=TT),
                           ACT.Sigmoid).then_inc(rowed, 1)
        else:
            act.wait_ge(picked, 1)
            act.activation(e[:, :, :], e[:, :, :], ACT.Exp).then_inc(exped, 1)
        act.wait_ge(turned, 1)
        act.copy(combT[:, :], bank[0:E, :]).then_inc(ready, 1)

    def pe_part(pe, router):
        for t in range(TT):
            for c in range(KC):
                last = pe.matmul(bank[:, t * E:(t + 1) * E], k.xnT[:, c, t * P:(t + 1) * P], router[:, c, :],
                                 start=c == 0, stop=c == KC - 1)
        last.then_inc(scored, 1)
        pe.wait_ge(combined, 1)
        for t in range(TT):
            last = pe.transpose(bank[0:E, t * P:(t + 1) * P], comb[:, t, :], k.ident[:, :])
        last.then_inc(turned, 1)

    return dve_part, act_part, pe_part, combT, comb


GATE = ["g_scored", "g_rowed", "g_picked", "g_exped", "g_combined", "g_turned", "g_ready", "g_order"]


def l2_ffn(k):
    nc = k.nc
    HC = 3072 // P
    expert_of = [n // 2 if n < 8 else 4 + (n - 8) // 4 for n in range(HC)]
    R = 4
    with ExitStack() as st:
        router = k.weight("L2_ffn_router_w", st)
        w1 = k.weight("L2_ffn_w1", st)
        w2 = k.weight("L2_ffn_w2", st)
        sel = k.const("select8", st)
        k.load(router, w1, w2, sel)
        relu = k.sb("relu", [P, R, T], st)
        rw = k.sb("relu_weighted", [P, R, T], st)
        hT = k.sb("hidden_T", [P, R, T], st)
        wb = k.sb("expert_weight", [P, E, T], st)
        with nc.Fori(0, B) as b, signals(
                nc, *norm_names("n_"), *GATE, "spread", "spread_copied", "up", "relued", "weighted", "squared",
                "consumed", "added") as (*sems, spread, spread_copied, up, relued, weighted, squared,
                                                  consumed, added), ExitStack() as bs:
            n1 = Norm(k, bs, sems[:7], "n", twice=False)
            g_dve, g_act, g_pe, combT, _ = top_two_gate(k, bs, sems[7:], True)
            x = batch_tiles(k, b)
            with nc.Block() as block:
                @block.vector
                def _(dve):
                    n1.dve(dve, x, k.xn)
                    g_dve(dve)
                    for n in range(HC):
                        dve.wait_ge(weighted, n + 1)
                        if n >= R:
                            dve.wait_ge(consumed, n - R + 1)
                        dve.tensor_tensor(hT[:, n % R, :], relu[:, n % R, :], rw[:, n % R, :],
                                          ALU.mult).then_inc(squared, 1)
                    dve.wait_ge(consumed, HC)
                    for t in range(TT):
                        dve.tensor_tensor(x(t), x(t), k.ps[:, t, 0:D], ALU.add).then_inc(added, 1)

                @block.gpsimd
                def _(pool):
                    n1.pool(pool)
                    for n in range(HC):
                        pool.wait_ge(relued, n + 1)
                        pool.wait_ge(spread_copied, expert_of[n] + 1)
                        if n >= R:
                            pool.wait_ge(squared, n - R + 1)
                        pool.tensor_tensor(rw[:, n % R, :], relu[:, n % R, :], wb[:, expert_of[n], :],
                                           ALU.mult).then_inc(weighted, 1)

                @block.scalar
                def _(act):
                    n1.act(act, k.xnT, (4, 5))
                    g_act(act)
                    for e in range(E):
                        act.wait_ge(spread, e + 1)
                        act.copy(wb[:, e, :], k.ps[:, 4 + e % 2, :]).then_inc(spread_copied, 1)
                    for n in range(HC):
                        act.wait_ge(up, n + 1)
                        if n >= R:
                            act.wait_ge(squared, n - R + 1)
                        act.activation(relu[:, n % R, :], k.ps[:, 4 + n % 4, :], ACT.Relu).then_inc(relued, 1)

                @block.tensor
                def _(pe):
                    n1.pe(pe, k.xn, (4, 5))
                    pe.wait_ge(n1.s_ready, KC)
                    g_pe(pe, router)
                    pe.wait_ge(sems[7 + 6], 1)
                    for e in range(E):
                        if e >= 2:
                            pe.wait_ge(spread_copied, e - 1)
                        pe.matmul(k.ps[:, 4 + e % 2, :], sel[:, e, :], combT[:, :], start=True,
                                  stop=True).then_inc(spread, 1)
                    pe.wait_ge(spread_copied, E)

                    def product_down(n):
                        pe.wait_ge(squared, n + 1)
                        for t in range(TT):
                            last = pe.matmul(k.ps[:, t, 0:D], hT[:, n % R, t * P:(t + 1) * P], w2[:, n, :],
                                             start=n == 0, stop=n == HC - 1)
                        last.then_inc(consumed, 1)
                        return last

                    for n in range(HC):
                        if n >= 4:
                            pe.wait_ge(relued, n - 3)
                        for c in range(KC):
                            last = pe.matmul(k.ps[:, 4 + n % 4, :], w1[:, c, n * P:(n + 1) * P], k.xnT[:, c, :],
                                             start=c == 0, stop=c == KC - 1)
                        last.then_inc(up, 1)
                        if n >= 2:
                            product_down(n - 2)
                    product_down(HC - 2)
                    product_down(HC - 1)
                    

def l3_ffn(k):
    nc = k.nc
    HC = E * 512 // P
    R = 4
    with ExitStack() as st:
        router = k.weight("L3_ffn_Wg", st)
        w1 = k.weight("L3_ffn_W1", st)
        w2 = k.weight("L3_ffn_W2", st)
        w3 = k.weight("L3_ffn_W3", st)
        b3 = k.const("L3_ffn_b3", st)
        sel = k.const("select8", st)
        k.load(router, w1, w2, w3, b3, sel)
        b1, b2 = k.vec("L3_ffn_b1"), k.vec("L3_ffn_b2")
        silu = k.sb("silu", [P, R, T], st)
        gv = k.sb("gated", [P, R, T], st)
        hT = k.sb("hidden_T", [P, R, T], st)
        wb = k.sb("expert_weight", [P, 2, T], st)
        with nc.Fori(0, B) as b, signals(
                nc, *norm_names("n_"), *GATE, "spread", "spread_copied", "up_g", "up_v", "silued", "gated",
                "weighted", "consumed", "added") as (*sems, spread, spread_copied, up_g, up_v, silued, gated,
                                                      weighted, consumed, added), ExitStack() as bs:
            n1 = Norm(k, bs, sems[:7], "n", twice=False)
            g_dve, g_act, g_pe, combT, _ = top_two_gate(k, bs, sems[7:], False)
            g_ready = sems[7 + 6]
            x = batch_tiles(k, b)
            with nc.Block() as block:
                @block.vector
                def _(dve):
                    n1.dve(dve, x, k.xn)
                    g_dve(dve)
                    for n in range(HC):
                        dve.wait_ge(up_v, n + 1)
                        dve.wait_ge(silued, n + 1)
                        if n >= R:
                            dve.wait_ge(weighted, n - R + 1)
                        dve.scalar_tensor_tensor(out=gv[:, n % R, :], in0=k.ps[:, 5 + 2 * (n % 2), :],
                                                 scalar=b2[:, n:n + 1], in1=silu[:, n % R, :], op0=ALU.add,
                                                 op1=ALU.mult).then_inc(gated, 1)
                    dve.wait_ge(consumed, HC)
                    for t in range(TT):
                        dve.tensor_tensor(x(t), x(t), k.ps[:, t, 0:D], ALU.add).then_inc(added, 1)

                @block.gpsimd
                def _(pool):
                    n1.pool(pool)
                    for n in range(HC):
                        pool.wait_ge(gated, n + 1)
                        pool.wait_ge(spread_copied, n // 4 + 1)
                        if n >= R:
                            pool.wait_ge(consumed, n - R + 1)
                        pool.tensor_tensor(hT[:, n % R, :], gv[:, n % R, :], wb[:, (n // 4) % 2, :],
                                           ALU.mult).then_inc(weighted, 1)

                @block.scalar
                def _(act):
                    n1.act(act, k.xnT, (4, 5))
                    g_act(act)
                    for n in range(HC):
                        if n % 4 == 0:
                            e = n // 4
                            act.wait_ge(spread, e + 1)
                            if e >= 2:
                                act.wait_ge(weighted, 4 * (e - 1))
                            act.copy(wb[:, e % 2, :], k.ps[:, 7, :]).then_inc(spread_copied, 1)
                        act.wait_ge(up_g, n + 1)
                        if n >= R:
                            act.wait_ge(gated, n - R + 1)
                        act.activation(silu[:, n % R, :], k.ps[:, 4 + 2 * (n % 2), :], ACT.Silu,
                                       bias=b1[:, n:n + 1]).then_inc(silued, 1)

                @block.tensor
                def _(pe):
                    n1.pe(pe, k.xn, (4, 5))
                    pe.wait_ge(n1.s_ready, KC)
                    g_pe(pe, router)
                    pe.wait_ge(g_ready, 1)
                    for t in range(TT):
                        pe.matmul(k.ps[:, t, 0:D], combT[:, t * P:(t + 1) * P], b3[:, :], start=True, stop=False)

                    def product_down(n):
                        pe.wait_ge(weighted, n + 1)
                        for t in range(TT):
                            last = pe.matmul(k.ps[:, t, 0:D], hT[:, n % R, t * P:(t + 1) * P], w3[:, n, :],
                                             start=False, stop=n == HC - 1)
                        last.then_inc(consumed, 1)

                    for n in range(HC):
                        if n >= 2:
                            pe.wait_ge(silued, n - 1)
                            pe.wait_ge(gated, n - 1)
                        if n % 4 == 0:
                            if n:
                                pe.wait_ge(gated, n)
                            pe.matmul(k.ps[:, 7, :], sel[:, n // 4, :], combT[:, :], start=True,
                                      stop=True).then_inc(spread, 1)
                        for bank, w, sem in ((4, w1, up_g), (5, w2, up_v)):
                            bank += 2 * (n % 2)
                            if bank == 7:
                                pe.wait_ge(spread_copied, n // 4 + 1)
                            for c in range(KC):
                                last = pe.matmul(k.ps[:, bank, :], w[:, c, n * P:(n + 1) * P], k.xnT[:, c, :],
                                                 start=c == 0, stop=c == KC - 1)
                            last.then_inc(sem, 1)
                        if n >= 2:
                            product_down(n - 2)
                    product_down(HC - 2)
                    product_down(HC - 1)



STAGES = [None] * 12
STAGES[0] = l0_attn
STAGES[1] = l0_xattn
STAGES[2] = l0_ffn
STAGES[3] = l1_attn
STAGES[5] = l1_ffn
STAGES[9] = l3_attn
STAGES[4] = l1_xattn
STAGES[6] = l2_attn
STAGES[7] = l2_xattn
STAGES[10] = l3_xattn
STAGES[8] = l2_ffn
STAGES[11] = l3_ffn

VECS = ["L1_attn_bq", "L1_attn_bk", "L1_attn_bg", "L1_ffn_bq", "L1_bn_gamma2", "L1_bn_beta2", "L0_xattn_bq", "L0_xattn_bk", "L2_attn_bq", "L2_attn_bk", "L2_scale", "L2_query_gain", "L2_xattn_kn_g2",
        "L3_query_gain", "L3_xattn_k_scale2"] + [
    p + n for p, ns in (("L1_xattn_", ("ln_l_g", "ln_l_b", "ln_m_g", "ln_m_b")),
                        ("L2_xattn_", ("ln_l_g", "ln_l_b", "ln_x_g", "ln_x_b")),
                        ("L3_xattn_", ("ln_l_w", "ln_l_b", "ln_x_w", "ln_x_b"))) for n in ns] + [
        "L0_freq", "L0_decay", "re_im_sign", "half_pi", "L0_attn_n1_g", "L0_attn_n1_b", "L0_attn_n2_g",
        "L0_attn_n2_b", "L0_attn_mlp_b1", "L3_ffn_b1", "L3_ffn_b2",
        "L0_ffn_ln1_g", "L0_ffn_ln1_b", "L0_ffn_ln2_g", "L0_ffn_ln2_b"]
ROWS = ["L1_attn_bv", "L1_attn_bo", "L1_attn_gamma", "L1_attn_beta", "L3_attn_b_o", "L0_xattn_bv", "L0_xattn_bo", "L2_attn_bv", "L2_attn_bo", "L2_xattn_bout", "L3_xattn_ln_o_w",
        "L3_xattn_ln_o_b", "L0_attn_gate_b", "L0_attn_mlp_b2", "L0_ffn_b1", "L0_ffn_b2"]
WEIGHTS = {"L0_ffn_w1": "T", "L0_ffn_w2": "T", "L2_ffn_router_w": "T", "L2_ffn_w1": "", "L2_ffn_w2": "",
           "L0_in": "", "L0_attn_out_proj_w": "T", "L0_coupling": "", "L0_attn_gate_w": "T",
           "L0_attn_mlp_w1": "T", "L0_attn_mlp_w2": "T", "L3_ffn_Wg": "T", "L3_ffn_W1": "T", "L3_ffn_W2": "T",
           "L3_ffn_W3": "", "L1_ffn_Wq": "", "L1_ffn_expert_down": "T", "L1_ffn_expert_up": "", "L1_sub_keys": "",
           **{"L1_attn_" + n: "" for n in ("Wq", "Wk", "Wv", "Wg", "Wo")},
           **{"L3_attn_" + n: "T" for n in ("w_q", "w_k", "w_v", "w_o")},
           "ctx_T": "", "L0_side": "", "mask_bf1": "", "mask_bk0": "",
           **{"L0_xattn_" + n: "" for n in ("wq", "wk", "wv", "wo")},
           **{"L2_attn_" + n: "T" for n in ("Wq", "Wk", "Wv", "Wo")},
           **{p + n: "" for p, o in (("L1_xattn_", "Wout"), ("L2_xattn_", "Wout"), ("L3_xattn_", "Wo"))
              for n in ("Wq", "Wkv", o)}}


def program(nc, dram, slots_v, slots_r):
    with ExitStack() as ctx:
        k = Core(nc, ctx, dram)
        k.slots_v, k.slots_r = slots_v, slots_r
        with signals(nc, "in_loaded", "consts_set") as (loaded, consts), nc.Block() as block:
            @block.sync
            def _(sp):
                sp.dma_start(k.x[:, :, :], dram["x"]).then_inc(loaded, 16)
                sp.dma_start(k.vecs[:, :], dram["vecs"]).then_inc(loaded, 16)
                sp.dma_start(k.rows[:, :], dram["rows"]).then_inc(loaded, 16)
                sp.dma_start(k.ident[:, :], dram["ident"]).then_inc(loaded, 16)
                sp.wait_ge(loaded, 64)

            @block.gpsimd
            def _(pool):
                pool.memset(k.ones[:, :], 1.0).then_inc(consts, 1)
                pool.memset(k.half[:, :], -0.5).then_inc(consts, 1)
                pool.wait_ge(consts, 2)

        with signals(nc, "folded") as (folded,), nc.Block() as block:
            @block.vector
            def _(dve):
                for name, c in (("L2_query_gain", 64 ** -0.5), ("L3_query_gain", 8.0)):
                    dve.tensor_scalar(k.vec(name), k.vec(name), c, None, ALU.mult).then_inc(folded, 1)

        for stage in STAGES[FIRST:LAST]:
            stage(k)

        with signals(nc, "out_stored") as (stored,), nc.Block() as block:
            @block.sync
            def _(sp):
                sp.dma_start(dram["out"], k.x[:, :, :]).then_inc(stored, 16)
                sp.wait_ge(stored, 16)


def words_of_bools(m):
    return np.broadcast_to(np.repeat(m.view(np.uint8).reshape(1, -1), 4, axis=1).view(np.int32), (P, m.size))


def lay_out(a, arrays):
    f = np.float32
    w = a["L0_attn_in_proj_w"].T
    a["L0_in"] = np.concatenate([w, w[:, 64:], w[:, :64]], axis=1)
    a["L0_freq"] = np.concatenate([a["L0_attn_frequency"]] * 2)
    a["L0_decay"] = np.concatenate([a["L0_attn_log_decay"]] * 2)
    a["re_im_sign"] = np.repeat(np.array([1, -1], f), 64)
    a["half_pi"] = np.full((P,), np.pi / 2, f)
    cp = np.zeros((P, 2 * P), f)
    for ri in range(2):
        for h in range(4):
            i = 64 * ri + 16 * h
            cp[i:i + 16, i:i + 16] = a["L0_attn_coupling"][h]
            j = P + 64 * (1 - ri) + 16 * h
            cp[i:i + 16, j:j + 16] = a["L0_attn_coupling"][h]
    a["L0_coupling"] = cp
    ctx = a["ctx_1024"]
    a["ctx_T"] = ctx.reshape(-1, D).T
    arrays["ctx_rows"] = np.ascontiguousarray(ctx.transpose(1, 0, 2))
    a["L0_side"] = np.broadcast_to(a["fside_BxS2_0"].reshape(1, -1), (P, B * 64))
    a["mask_bf1"] = words_of_bools(a["mask_BxS2_bf1"])
    a["mask_bk0"] = words_of_bools(a["mask_BxS2_bk0"])
    arrays["head_mask8"] = np.repeat(np.eye(8, dtype=f), 16, axis=0)
    q, c = np.arange(P)[:, None], np.arange(P)[None, :]
    hidden = (q // 64 > c // 64) | ((q // 64 == c // 64) & (c > q))
    arrays["block_mask"] = np.where(hidden, f(-1e30), f(0))
    a["L2_scale"] = np.broadcast_to(a["L2_attn_attn_scale"], (P,))
    a["L2_query_gain"] = np.tile(a["L2_xattn_qn_g"], 2)
    a["L2_xattn_kn_g2"] = np.tile(a["L2_xattn_kn_g"], 2)
    a["L3_query_gain"] = np.tile(a["L3_xattn_q_scale"], 2)
    a["L3_xattn_k_scale2"] = np.tile(a["L3_xattn_k_scale"], 2)
    arrays["chunk_diagonal"] = np.eye(T // 16, dtype=f)
    arrays["pair_mean"] = np.tile(np.eye(64, dtype=f) * f(0.5), (2, 2))
    arrays["group_of_32"] = np.repeat(np.eye(4, dtype=f), 32, axis=0)
    sk = np.zeros((P, P), f)
    for i in range(4):
        sk[32 * i:32 * i + 32, 32 * i:32 * i + 32] = a["L1_ffn_sub_key%d" % (i % 2)].T
    a["L1_sub_keys"] = sk
    a["L1_bn_gamma2"] = np.tile(a["L1_ffn_bn_gamma"], 2)
    a["L1_bn_beta2"] = np.tile(a["L1_ffn_bn_beta"], 2)
    for n in ("rel_k", "rel_v"):
        rel = np.tile(a["L3_attn_" + n][128 - 3:128 + 4][::-1], (1, 16))
        arrays[n + "_rows"] = np.ascontiguousarray(np.broadcast_to(rel[None], (P, 7, D)))
    arrays["counting"] = np.ascontiguousarray(np.broadcast_to(np.arange(T, dtype=f)[None], (P, T)))
    arrays["select8"] = np.ascontiguousarray(np.repeat(np.eye(E, dtype=f)[:, :, None], P, axis=2))
    for n in ("L3_ffn_W1", "L3_ffn_W2"):
        a[n] = a[n].reshape(-1, D)
    a["L3_ffn_W3"] = a["L3_ffn_W3"].transpose(0, 2, 1).reshape(-1, D)
    arrays["L3_ffn_b3"] = a["L3_ffn_b3"]


def kernel(**inputs):
    import concourse.bacc as _bacc
    from concourse.bass_utils import run_bass_kernel_spmd as _run

    nc = _bacc.Bacc("TRN2", target_bir_lowering=False, num_devices=1)
    a = {n: np.asarray(v) for n, v in inputs.items()}
    arrays = {"x": np.ascontiguousarray(a["x"].reshape(NT, P, D).transpose(1, 0, 2))}
    lay_out(a, arrays)
    slots_v, slots_r, at = {}, {}, 0
    for n in VECS:
        slots_v[n] = (at, at + a[n].size // P)
        at += a[n].size // P
    arrays["vecs"] = np.ascontiguousarray(np.concatenate([a[n].reshape(-1, P).T for n in VECS], axis=1))
    at = 0
    for n in ROWS:
        slots_r[n] = (at, at + a[n].size)
        at += a[n].size
    arrays["rows"] = np.ascontiguousarray(
        np.broadcast_to(np.concatenate([a[n].reshape(-1) for n in ROWS])[None, :], (P, at)))
    arrays["ident"] = np.eye(P, dtype=np.float32)
    for n, how in WEIGHTS.items():
        w = a[n].T if how == "T" else a[n]
        arrays[n] = np.ascontiguousarray(w.reshape(w.shape[0] // P, P, w.shape[1]).transpose(1, 0, 2))
    dram = {n: nc.dram_tensor("in_" + n, v.shape, mybir.dt.from_np(v.dtype), kind="ExternalInput").ap()
            for n, v in arrays.items()}
    dram["out"] = nc.dram_tensor("out_x", (P, NT, D), F32, kind="ExternalOutput").ap()
    program(nc, dram, slots_v, slots_r)
    r = _run(nc, [{"in_" + n: v for n, v in arrays.items()}], core_ids=[0])
    out = np.asarray(r.results[0]["out_x"])
    return out.transpose(1, 0, 2).reshape(B, T, D)
```

```python
from contextlib import ExitStack, contextmanager

import numpy as np

import concourse.bass as bass
from concourse import mybir

F32 = mybir.dt.float32
ALU = mybir.AluOpType
ACT = mybir.ActivationFunctionType
AX = mybir.AxisListType

P = 128
D = 256
KC = D // P
B = 4
T = 512
TT = T // P
NT = B * TT
EPS = 1e-5
FIRST, LAST = 0, 12


@contextmanager
def signals(nc, *names):
    with ExitStack() as st:
        sems = [st.enter_context(nc.semaphore(n)) for n in names]
        yield sems
        for s in sems:
            nc.gpsimd.sem_clear(s)
        nc.all_engine_barrier()


class Order:

    def __init__(self, eng, sem):
        self.eng, self.sem, self.n = eng, sem, 0

    def mark(self, ins):
        self.n += 1
        ins.then_inc(self.sem, 1)
        return self.n

    def wait(self):
        if self.n:
            self.eng.wait_ge(self.sem, self.n)

    def do(self, ins):
        self.mark(ins)
        self.wait()


class Core:

    def __init__(self, nc, ctx, dram):
        self.nc, self.ctx, self.dram = nc, ctx, dram
        self.used = {}
        sb = self.sb
        self.x = sb("x_res", [P, NT, D])
        self.ident = sb("ident", [P, P])
        self.ones = sb("ones", [P, P])
        self.half = sb("neg_half", [P, 64])
        self.xn = sb("x_normed", [P, TT, D])
        self.xnT = sb("x_normed_T", [P, KC, T])
        self.vecs = sb("feature_vectors", [P, dram["vecs"].shape[1]])
        self.rows = sb("row_vectors", [P, dram["rows"].shape[1]])
        self.ps = ctx.enter_context(nc.psum_tensor("psum_banks", [P, 8, 512], F32))

    def vec(self, n):
        return self.vecs[:, self.slots_v[n][0]:self.slots_v[n][1]]

    def row(self, n):
        return self.rows[:, self.slots_r[n][0]:self.slots_r[n][1]]

    def weight(self, name, ctx):
        src = self.dram[name]
        return Loaded(self.sb("w_" + name, list(src.shape), ctx, src.dtype), src)

    const = weight

    def load(self, *what):
        with signals(self.nc, "weights_loaded") as (loaded,), self.nc.Block() as block:
            @block.sync
            def _(sp):
                for w in what:
                    whole = tuple(slice(None) for _ in w.src.shape)
                    sp.dma_start(w.dst[whole], w.src[whole]).then_inc(loaded, 16)
                sp.wait_ge(loaded, 16 * len(what))

    def sb(self, name, shape, ctx=None, dtype=F32):
        self.used[name] = n = self.used.get(name, 0) + 1
        name = name if n == 1 else f"{name}_{n}"
        return (ctx or self.ctx).enter_context(self.nc.sbuf_tensor(name, shape, dtype))


class Loaded:

    def __init__(self, dst, src):
        self.dst, self.src = dst, src

    def __getitem__(self, i):
        return self.dst[i]


class Norm:

    NAMES = ("stats", "aggr", "rstd", "normed", "turned", "ready", "pool_order")

    def __init__(self, k, ctx, sems, name, twice=True, gain=None, offset=None, tiles=TT, rows=P, eps=EPS, eps2=EPS):
        (self.s_stats, self.s_aggr, self.s_rstd, self.s_normed, self.s_turned, self.s_ready, self.s_pool) = sems
        self.k, self.twice, self.gain, self.offset, self.tiles, self.rows = k, twice, gain, offset, tiles, rows
        self.eps, self.eps2 = eps, eps2
        self.stat = k.sb(name + "_stat", [P, tiles, 6], ctx)
        self.mv = k.sb(name + "_mv", [P, tiles, 2], ctx)
        self.rs = k.sb(name + "_rstd", [P, 4, tiles], ctx)

    def dve(self, dve, src, dst):
        r = self.rows
        for t in range(self.tiles):
            dve.bn_stats(self.stat[0:r, t, :], src(t)).then_inc(self.s_stats, 1)
        dve.wait_ge(self.s_stats, self.tiles)
        for t in range(self.tiles):
            dve.bn_aggr(self.mv[0:r, t, :], self.stat[0:r, t, :]).then_inc(self.s_aggr, 1)
        dve.wait_ge(self.s_aggr, self.tiles)
        dve.wait_ge(self.s_rstd, 1)
        for t in range(self.tiles):
            dve.tensor_scalar(dst[0:r, t, :], src(t), self.mv[0:r, t, 0:1], self.rs[0:r, 3, t:t + 1],
                              ALU.subtract, ALU.mult).then_inc(self.s_normed, 1)

    def pool(self, pool):
        k, r, n = self.k, self.rows, self.tiles
        rs, var = self.rs, self.mv[0:r, :, 1]
        o = Order(pool, self.s_pool)
        pool.wait_ge(self.s_aggr, n)
        o.do(pool.tensor_scalar(rs[0:r, 0, :], var, self.eps, 1.0, ALU.add, ALU.mult))
        if not self.twice:
            pool.tensor_tensor(rs[0:r, 3, :], rs[0:r, 0, :], k.half[0:r, 0:n], ALU.pow).then_inc(self.s_rstd, 1)
            return
        o.do(pool.tensor_tensor(rs[0:r, 1, :], rs[0:r, 0, :], k.half[0:r, 0:n], ALU.pow))
        o.do(pool.tensor_tensor(rs[0:r, 2, :], rs[0:r, 1, :], rs[0:r, 1, :], ALU.mult))
        o.do(pool.tensor_tensor(rs[0:r, 2, :], rs[0:r, 2, :], var, ALU.mult))
        o.do(pool.tensor_scalar(rs[0:r, 2, :], rs[0:r, 2, :], self.eps2, 1.0, ALU.add, ALU.mult))
        o.do(pool.tensor_tensor(rs[0:r, 2, :], rs[0:r, 2, :], k.half[0:r, 0:n], ALU.pow))
        pool.tensor_tensor(rs[0:r, 3, :], rs[0:r, 2, :], rs[0:r, 1, :], ALU.mult).then_inc(self.s_rstd, 1)

    def pe(self, pe, src, banks, chunks=KC):
        k, r = self.k, self.rows
        pe.wait_ge(self.s_normed, self.tiles)
        for c in range(chunks):
            for t in range(self.tiles):
                last = pe.transpose(k.ps[:, banks[c], t * r:(t + 1) * r], src[0:r, t, c * P:(c + 1) * P],
                                    k.ident[0:r, 0:r])
            last.then_inc(self.s_turned, 1)

    def act(self, act, dst, banks, chunks=KC):
        k, n = self.k, self.rows * self.tiles
        for c in range(chunks):
            act.wait_ge(self.s_turned, c + 1)
            if self.gain is None:
                act.copy(dst[:, c, 0:n], k.ps[:, banks[c], 0:n]).then_inc(self.s_ready, 1)
            else:
                act.activation(dst[:, c, 0:n], k.ps[:, banks[c], 0:n], ACT.Identity,
                               bias=self.offset[:, c:c + 1], scale=self.gain[:, c:c + 1]).then_inc(self.s_ready, 1)


def norm_names(p):
    return [p + n for n in Norm.NAMES]


def batch_tiles(k, b):
    v = k.x[:, :, :].rearrange("p (b t) d -> p b t d", b=B)
    return lambda t: v[:, bass.ds(b, 1), t, :].rearrange("p o d -> p (o d)")



def l0_ffn(k):
    nc = k.nc
    HID = 1024
    HC = HID // P
    with ExitStack() as st:
        w1 = k.sb("w1_T", [P, KC, HID], st)
        w2 = k.sb("w2_T", [P, HC, D], st)
        h = k.sb("hidden", [P, TT, HID], st)
        hT = k.sb("hidden_T", [P, HC, T], st)
        asum = k.sb("abs_sum", [P, 2], st)
        scal = k.sb("quant_scale", [P, 2, 2], st)
        sems = norm_names("ffn1_") + norm_names("ffn2_")
        with signals(nc, "loaded", "abs_summed", "summed", "scaled", "quantised") as \
                (loaded, abs_summed, summed, scaled, quantised), nc.Block() as block:
            @block.sync
            def _(sp):
                sp.dma_start(w1[:, :, :], k.dram["L0_ffn_w1"][:, :, :]).then_inc(loaded, 16)
                sp.dma_start(w2[:, :, :], k.dram["L0_ffn_w2"][:, :, :]).then_inc(loaded, 16)

            @block.vector
            def _(dve):
                o = Order(dve, quantised)
                dve.wait_ge(loaded, 32)
                for i, w in enumerate((w1, w2)):
                    dve.tensor_reduce(asum[:, i:i + 1], w[:, :, :], AX.XY, ALU.add,
                                      apply_absolute_value=True).then_inc(abs_summed, 1)
                dve.wait_ge(summed, 1)
                o.do(dve.tensor_scalar(scal[:, :, 1], k.ps[:, 0, 0:2], 1.0 / (HID * D), 1e-5, ALU.mult, ALU.max))
                o.do(dve.reciprocal(scal[:, :, 0], scal[:, :, 1]))
                for i, w in enumerate((w1, w2)):
                    o.do(dve.tensor_scalar(w[:, :, :], w[:, :, :], scal[:, i, 0:1], 1.0, ALU.mult, ALU.min))
                    o.do(dve.tensor_scalar(w[:, :, :], w[:, :, :], -1.0, 12582912.0, ALU.max, ALU.add))
                    o.do(dve.tensor_scalar(w[:, :, :], w[:, :, :], -12582912.0, scal[:, i, 1:2], ALU.add, ALU.mult))

            @block.tensor
            def _(pe):
                pe.wait_ge(abs_summed, 2)
                pe.matmul(k.ps[:, 0, 0:2], k.ones[:, :], asum[:, :], start=True, stop=True).then_inc(summed, 1)

        with nc.Fori(0, B) as b, signals(nc, *sems, "up", "biased", "gelued", "down", "added", "freed") as \
                (*ns, up, biased, gelued, down, added, freed), ExitStack() as bs:
            n1 = Norm(k, bs, ns[:7], "n1", gain=k.vec("L0_ffn_ln1_g"), offset=k.vec("L0_ffn_ln1_b"))
            n2s = ns[7:]
            s_stats, s_aggr, s_rstd, s_normed, s_turned, s_ready, s_pool = n2s
            stat = k.sb("hid_stat", [P, TT, 2, 6], bs)
            mv = k.sb("hid_mv", [P, TT, 2], bs)
            rs = k.sb("hid_rstd", [P, 2, TT], bs)
            x = batch_tiles(k, b)
            g2, b2 = k.vec("L0_ffn_ln2_g"), k.vec("L0_ffn_ln2_b")
            b1r, b2r = k.row("L0_ffn_b1"), k.row("L0_ffn_b2")
            with nc.Block() as block:
                @block.vector
                def _(dve):
                    n1.dve(dve, x, k.xn)
                    for t in range(TT):
                        dve.wait_ge(up, t + 1)
                        s0 = 2 * (t % 2)
                        dve.tensor_tensor(h[:, t, :].rearrange("p (a n) -> p a n", a=2), k.ps[:, s0:s0 + 2, :],
                                          b1r.rearrange("p (a n) -> p a n", a=2), ALU.add).then_inc(biased, 1)
                    for t in range(TT):
                        dve.wait_ge(gelued, t + 1)
                        for a in range(2):
                            dve.bn_stats(stat[:, t, a, :], h[:, t, a * 512:(a + 1) * 512]).then_inc(s_stats, 1)
                        dve.wait_ge(s_stats, 2 * (t + 1))
                        dve.bn_aggr(mv[:, t, :], stat[:, t, :, :].rearrange("p a s -> p (a s)")).then_inc(s_aggr, 1)
                    for t in range(TT):
                        dve.wait_ge(s_rstd, t + 1)
                        dve.tensor_scalar(h[:, t, :], h[:, t, :], mv[:, t, 0:1], rs[:, 1, t:t + 1],
                                          ALU.subtract, ALU.mult).then_inc(s_normed, 1)
                    o = Order(dve, freed)
                    for t in range(TT):
                        dve.wait_ge(down, t + 1)
                        o.do(dve.tensor_tensor(k.xn[:, t, :], k.ps[:, 4 + t % 2, 0:D], b2r, ALU.add))
                        dve.tensor_tensor(x(t), x(t), k.xn[:, t, :], ALU.add).then_inc(added, 1)

                @block.gpsimd
                def _(pool):
                    n1.pool(pool)
                    o = Order(pool, s_pool)
                    for t in range(TT):
                        pool.wait_ge(s_aggr, t + 1)
                        o.do(pool.tensor_scalar(rs[:, 0, t:t + 1], mv[:, t, 1:2], EPS, 1.0, ALU.add, ALU.mult))
                        pool.tensor_tensor(rs[:, 1, t:t + 1], rs[:, 0, t:t + 1], k.half[:, 0:1],
                                           ALU.pow).then_inc(s_rstd, 1)

                @block.scalar
                def _(act):
                    n1.act(act, k.xnT, (6, 7))
                    for t in range(TT):
                        act.wait_ge(biased, t + 1)
                        act.activation(h[:, t, :], h[:, t, :], ACT.Gelu).then_inc(gelued, 1)
                    for c in range(HC):
                        act.wait_ge(s_turned, c + 1)
                        act.activation(hT[:, c, :], k.ps[:, c % 4, :], ACT.Identity, bias=b2[:, c:c + 1],
                                       scale=g2[:, c:c + 1]).then_inc(s_ready, 1)

                @block.tensor
                def _(pe):
                    n1.pe(pe, k.xn, (6, 7))
                    pe.wait_ge(n1.s_ready, KC)
                    for t in range(TT):
                        if t >= 2:
                            pe.wait_ge(biased, t - 1)
                        for a in range(2):
                            for c in range(KC):
                                last = pe.matmul(k.ps[:, 2 * (t % 2) + a, :], k.xnT[:, c, t * P:(t + 1) * P],
                                                 w1[:, c, a * 512:(a + 1) * 512], start=c == 0, stop=c == KC - 1)
                        last.then_inc(up, 1)
                    pe.wait_ge(s_normed, TT)
                    for c in range(HC):
                        if c >= 4:
                            pe.wait_ge(s_ready, c - 3)
                        for t in range(TT):
                            last = pe.transpose(k.ps[:, c % 4, t * P:(t + 1) * P], h[:, t, c * P:(c + 1) * P],
                                                k.ident[:, :])
                        last.then_inc(s_turned, 1)
                    pe.wait_ge(s_ready, HC)
                    for t in range(TT):
                        if t >= 2:
                            pe.wait_ge(freed, t - 1)
                        for c in range(HC):
                            last = pe.matmul(k.ps[:, 4 + t % 2, 0:D], hT[:, c, t * P:(t + 1) * P], w2[:, c, :],
                                             start=c == 0, stop=c == HC - 1)
                        last.then_inc(down, 1)


BIG = 3.0e38


def l0_attn(k):
    nc = k.nc
    HC = 1024 // P
    TWO_PI_HI = 6.28125
    TWO_PI_LO = 2 * np.pi - TWO_PI_HI
    MAGIC = 12582912.0
    with ExitStack() as st:
        w_in = k.weight("L0_in", st)
        w_out = k.weight("L0_attn_out_proj_w", st)
        coup = k.weight("L0_coupling", st)
        gate = k.weight("L0_attn_gate_w", st)
        w1 = k.weight("L0_attn_mlp_w1", st)
        w2 = k.weight("L0_attn_mlp_w2", st)
        count = k.const("counting", st)
        k.load(w_in, w_out, coup, gate, w1, w2, count)
        mag = k.sb("magnitude", [P, T], st)
        cos = k.sb("cosine", [P, T], st)
        sin = k.sb("signed_sine", [P, T], st)
        m = k.sb("out_weights", [P, 2, D], st)
        with signals(nc, "rot_order", "reduced", "angles", "magged", "coupled", "out_ready") as \
                (order, reduced, angles, magged, coupled, out_ready), ExitStack() as ts, nc.Block() as block:
            ph = k.sb("phase", [P, T], ts)
            turns = k.sb("turns", [P, T], ts)
            mcol = k.sb("mag_col", [P, 1], ts)

            @block.vector
            def _(dve):
                o = Order(dve, order)
                o.do(dve.tensor_scalar(ph[:, :], count[:, :], k.vec("L0_freq")[:, 0:1], None, ALU.mult))
                o.do(dve.tensor_scalar(turns[:, :], ph[:, :], 1 / (2 * np.pi), MAGIC, ALU.mult, ALU.add))
                o.do(dve.tensor_scalar(turns[:, :], turns[:, :], -MAGIC, None, ALU.add))
                o.do(dve.scalar_tensor_tensor(out=ph[:, :], in0=turns[:, :], scalar=-TWO_PI_HI, in1=ph[:, :],
                                              op0=ALU.mult, op1=ALU.add))
                o.do(dve.scalar_tensor_tensor(out=ph[:, :], in0=turns[:, :], scalar=-TWO_PI_LO, in1=ph[:, :],
                                              op0=ALU.mult, op1=ALU.add))
                dve.tensor_scalar(ph[:, :], ph[:, :], 3.141592, -3.141592, ALU.min, ALU.max).then_inc(reduced, 1)
                dve.wait_ge(magged, 1)
                o.mark(dve.tensor_scalar(mag[:, :], k.ones[:, 0:1].to_broadcast([P, T]), mcol[:, 0:1], None,
                                         ALU.mult))
                dve.wait_ge(angles, 2)
                o.mark(dve.tensor_scalar(sin[:, :], sin[:, :], k.vec("re_im_sign")[:, 0:1], None, ALU.mult))
                for i in range(2):
                    dve.wait_ge(coupled, i + 1)
                    dve.tensor_copy(m[:, i, :], k.ps[:, i, 0:D]).then_inc(out_ready, 1)

            @block.scalar
            def _(act):
                act.activation(mcol[:, :], k.vec("L0_decay")[:, 0:1], ACT.Sigmoid).then_inc(magged, 1)
                act.wait_ge(reduced, 1)
                act.activation(sin[:, :], ph[:, :], ACT.Sin).then_inc(angles, 1)
                act.activation(turns[:, :], ph[:, :], ACT.Abs).then_inc(angles, 1)
                act.wait_ge(angles, 2)
                act.activation(cos[:, :], turns[:, :], ACT.Sin, bias=k.vec("half_pi")[:, 0:1],
                               scale=-1.0).then_inc(angles, 1)

            @block.tensor
            def _(pe):
                for i in range(2):
                    pe.matmul(k.ps[:, i, 0:D], coup[:, 0, i * P:(i + 1) * P], w_out[:, 0, :], start=True,
                              stop=True).then_inc(coupled, 1)

        xin = k.sb("x_in", [P, TT, D], st)
        x2 = k.sb("x_mid_normed", [P, TT, D], st)
        x2T = k.sb("x_mid_T", [P, KC, T], st)
        beta = k.sb("beta_turned", [P, 4, T], st)
        gt = k.sb("gate_value", [P, TT, D], st)
        hT = k.sb("hidden_T", [P, HC, T], st)
        with nc.Fori(0, B) as b, signals(
                nc, *norm_names("a_"), *norm_names("m_"), "once", "beta_made", "rot_order", "scanned", "gate_made",
                "gate_biased", "gate_open", "outed", "midded", "up", "silued", "down", "biased", "added") as (
                *sems, once, beta_made, order, scanned, gate_made, gate_biased, gate_open, outed, midded, up,
                silued, down, biased, added), ExitStack() as bs:
            n1 = Norm(k, bs, sems[:7], "a", gain=k.vec("L0_attn_n1_g"), offset=k.vec("L0_attn_n1_b"))
            n2 = Norm(k, bs, sems[7:], "m", twice=False, gain=k.vec("L0_attn_n2_g"), offset=k.vec("L0_attn_n2_b"))
            b1, b2r, gbr = k.vec("L0_attn_mlp_b1"), k.row("L0_attn_mlp_b2"), k.row("L0_attn_gate_b")
            x = batch_tiles(k, b)
            with nc.Block() as block:
                @block.vector
                def _(dve):
                    n1.dve(dve, x, k.xn)
                    for t in range(TT):
                        dve.tensor_scalar(xin[:, t, :], x(t), n1.mv[:, t, 0:1], n1.rs[:, 1, t:t + 1],
                                          ALU.subtract, ALU.mult).then_inc(once, 1)
                    o = Order(dve, order)
                    dve.wait_ge(beta_made, 2)
                    o.mark(dve.tensor_tensor(beta[:, 0, :], k.ps[:, 0, :], cos[:, :], ALU.mult))
                    o.do(dve.tensor_tensor(beta[:, 1, :], k.ps[:, 1, :], sin[:, :], ALU.mult))
                    o.do(dve.tensor_tensor(beta[:, 0, :], beta[:, 0, :], beta[:, 1, :], ALU.add))
                    o.do(dve.tensor_tensor_scan(beta[:, 1, :], mag[:, :], beta[:, 0, :], 0.0, ALU.mult, ALU.add))
                    dve.tensor_tensor(beta[:, 2, :], beta[:, 1, :], cos[:, :], ALU.mult).then_inc(scanned, 1)
                    dve.tensor_tensor(beta[:, 3, :], beta[:, 1, :], sin[:, :], ALU.mult).then_inc(scanned, 1)
                    for t in range(TT):
                        dve.wait_ge(gate_made, 2 * (t // 2) + 2)
                        dve.tensor_tensor(gt[:, t, :], k.ps[:, 2 + t // 2, (t % 2) * D:(t % 2 + 1) * D], gbr,
                                          ALU.add).then_inc(gate_biased, 1)
                    dve.wait_ge(once, TT)
                    for t in range(TT):
                        dve.wait_ge(gate_open, t + 1)
                        dve.wait_ge(outed, 2 * (t // 2) + 2)
                        o.do(dve.tensor_tensor(gt[:, t, :], gt[:, t, :],
                                               k.ps[:, 4 + t // 2, (t % 2) * D:(t % 2 + 1) * D], ALU.mult))
                        o.mark(dve.tensor_tensor(xin[:, t, :], xin[:, t, :], gt[:, t, :], ALU.add))
                    o.wait()
                    n2.dve(dve, lambda t: xin[:, t, :], x2)
                    for t in range(TT):
                        dve.tensor_tensor(xin[:, t, :], xin[:, t, :], b2r, ALU.add).then_inc(biased, 1)
                    dve.wait_ge(biased, TT)
                    for t in range(TT):
                        dve.tensor_tensor(x(t), x(t), xin[:, t, :], ALU.add).then_inc(biased, 1)
                    for t in range(TT):
                        dve.wait_ge(down, 2 * (t // 2) + 2)
                        dve.wait_ge(biased, TT + t + 1)
                        dve.tensor_tensor(x(t), x(t), k.ps[:, t // 2, (t % 2) * D:(t % 2 + 1) * D],
                                          ALU.add).then_inc(added, 1)

                @block.gpsimd
                def _(pool):
                    n1.pool(pool)
                    n2.pool(pool)

                @block.scalar
                def _(act):
                    n1.act(act, k.xnT, (6, 7))
                    for t in range(TT):
                        act.wait_ge(gate_biased, t + 1)
                        act.activation(gt[:, t, :], gt[:, t, :], ACT.Sigmoid).then_inc(gate_open, 1)
                    n2.act(act, x2T, (6, 7))
                    for c in range(HC):
                        act.wait_ge(up, c + 1)
                        act.activation(hT[:, c, :], k.ps[:, 2 + c % 4, :], ACT.Silu,
                                       bias=b1[:, c:c + 1]).then_inc(silued, 1)

                @block.tensor
                def _(pe):
                    n1.pe(pe, k.xn, (6, 7))
                    pe.wait_ge(n1.s_ready, KC)
                    for i in range(2):
                        for c in range(KC):
                            last = pe.matmul(k.ps[:, i, :], w_in[:, c, i * P:(i + 1) * P], k.xnT[:, c, :],
                                             start=c == 0, stop=c == KC - 1)
                        last.then_inc(beta_made, 1)
                    for t in range(TT):
                        for c in range(KC):
                            last = pe.matmul(k.ps[:, 2 + t // 2, (t % 2) * D:(t % 2 + 1) * D],
                                             k.xnT[:, c, t * P:(t + 1) * P], gate[:, c, :],
                                             start=c == 0, stop=c == KC - 1)
                        last.then_inc(gate_made, 1)
                    pe.wait_ge(scanned, 2)
                    for t in range(TT):
                        for i in range(2):
                            last = pe.matmul(k.ps[:, 4 + t // 2, (t % 2) * D:(t % 2 + 1) * D],
                                             beta[:, 2 + i, t * P:(t + 1) * P], m[:, i, :],
                                             start=i == 0, stop=i == 1)
                        last.then_inc(outed, 1)
                    n2.pe(pe, x2, (6, 7))
                    pe.wait_ge(n2.s_ready, KC)
                    for n in range(HC):
                        if n >= 4:
                            pe.wait_ge(silued, n - 3)
                        for c in range(KC):
                            last = pe.matmul(k.ps[:, 2 + n % 4, :], w1[:, c, n * P:(n + 1) * P], x2T[:, c, :],
                                             start=c == 0, stop=c == KC - 1)
                        last.then_inc(up, 1)
                    pe.wait_ge(silued, HC)
                    for t in range(TT):
                        for n in range(HC):
                            last = pe.matmul(k.ps[:, t // 2, (t % 2) * D:(t % 2 + 1) * D],
                                             hT[:, n, t * P:(t + 1) * P], w2[:, n, :],
                                             start=n == 0, stop=n == HC - 1)
                        last.then_inc(down, 1)



class Product:

    def __init__(self, dst, pairs, rows, n, add=None, mult=None, row=None):
        self.dst, self.pairs, self.rows, self.n = dst, pairs, rows, n
        self.add, self.mult, self.row = add, mult, row


def project(k, products):
    on_act = [i for i, p in enumerate(products) if i % 2 and p.add is None and p.row is None]
    on_dve = [i for i in range(len(products)) if i not in on_act]
    rank = {i: n for lst in (on_act, on_dve) for n, i in enumerate(lst)}
    with signals(k.nc, "made", "act_moved", "dve_moved") as (made, act_moved, dve_moved), k.nc.Block() as block:
        @block.tensor
        def _(pe):
            for i, p in enumerate(products):
                if i >= 8:
                    pe.wait_ge(act_moved if i - 8 in on_act else dve_moved, rank[i - 8] + 1)
                for j, (lhsT, rhs) in enumerate(p.pairs):
                    last = pe.matmul(k.ps[0:p.rows, i % 8, 0:p.n], lhsT, rhs, start=j == 0,
                                     stop=j == len(p.pairs) - 1)
                last.then_inc(made, 1)

        @block.scalar
        def _(act):
            for i in on_act:
                p = products[i]
                act.wait_ge(made, i + 1)
                out = k.ps[0:p.rows, i % 8, 0:p.n]
                if p.mult is None:
                    act.copy(p.dst, out).then_inc(act_moved, 1)
                else:
                    act.mul(p.dst, out, p.mult).then_inc(act_moved, 1)

        @block.vector
        def _(dve):
            for i in on_dve:
                p = products[i]
                dve.wait_ge(made, i + 1)
                out = k.ps[0:p.rows, i % 8, 0:p.n]
                if p.row is not None:
                    dve.tensor_tensor(p.dst, out, p.row, ALU.add).then_inc(dve_moved, 1)
                elif p.add is not None:
                    dve.tensor_scalar(p.dst, out, p.add, p.mult, ALU.add,
                                      ALU.bypass if p.mult is None else ALU.mult).then_inc(dve_moved, 1)
                elif p.mult is not None:
                    dve.tensor_scalar(p.dst, out, p.mult, None, ALU.mult).then_inc(dve_moved, 1)
                else:
                    dve.tensor_copy(p.dst, out).then_inc(dve_moved, 1)


class Item:

    def __init__(self, halves, scores, chunks, mask=None):
        self.halves = halves
        self.scores = scores
        self.chunks = chunks
        self.mask = mask


class Head:

    def __init__(self, rows, parts, store=None):
        self.rows, self.parts = rows, parts
        self.store = store


def attend(k, items, heads):
    nc, N = k.nc, len(items)
    wide = len(items[0].halves) == 2
    wmax = max(sum(it.halves) for it in items)
    cmax = (wmax + P - 1) // P
    SB = 2 if wide else 3
    stores = [h for h in range(len(heads)) if heads[h].store is not None]
    with ExitStack() as st, signals(nc, "scored", "maxed", "exped", "inverted", "shared", "turned", "copied",
                                    "copied_fifth", "valued", "stored", "mask_order") as (
            scored, maxed, exped, inverted, shared, turned, copied, copied_fifth, valued, stored, order):
        prob = k.sb("probs", [P, 3, wmax], st)
        pT = k.sb("probs_T", [P, 2, cmax, T], st)
        nmax = k.sb("neg_max", [P, 4], st)
        tot = k.sb("exp_sum", [P, 4], st)
        inv = k.sb("inv_sum", [P, 4], st)

        def score_banks(i):
            h = items[i].halves
            if wide:
                return k.ps[:, 2 * (i % 2):2 * (i % 2) + 2, 0:h[0]]
            return k.ps[:, i % 3, 0:h[0]]

        def probs(i):
            w = prob[:, i % 3, 0:sum(items[i].halves)]
            return w.rearrange("p (a n) -> p a n", a=2) if wide else w

        def turned_place(i, c):
            return k.ps[:, 4 + i % 2, c * P:(c + 1) * P] if c < 4 else k.ps[:, 7, 0:P]

        with nc.Block() as block:
            @block.tensor
            def _(pe):
                for i in range(N + 6):
                    if i < N:
                        if i >= SB:
                            pe.wait_ge(exped, i - SB + 1)
                        for lhsT, rhs, bank in items[i].scores:
                            out = score_banks(i)
                            last = pe.matmul(out[:, bank, :] if wide else out, lhsT, rhs, start=True, stop=True)
                        last.then_inc(scored, 1)
                    if 2 <= i < N + 2:
                        j = i - 2
                        pe.wait_ge(shared, j + 1)
                        if j >= 2:
                            pe.wait_ge(copied, j - 1)
                        if wide and j >= 1:
                            pe.wait_ge(copied_fifth, j)
                        at = 0
                        for c, n in items[j].chunks:
                            last = pe.transpose(turned_place(j, c)[0:n, :], prob[:, j % 3, at:at + n],
                                                k.ident[:, :])
                            at += n
                        last.then_inc(turned, 1)
                    if i >= 6:
                        h, part = (i - 6) // 4, (i - 6) % 4
                        if part == 0:
                            pe.wait_ge(copied, 4 * h + 4)
                            if wide:
                                pe.wait_ge(copied_fifth, 4 * h + 4)
                            before = sum(1 for x in stores if x < h)
                            if before:
                                pe.wait_ge(stored, before)
                        for c, n, v, cols, start, stop in heads[h].parts[part]:
                            last = pe.matmul(k.ps[heads[h].rows, 6, 0:cols], v, pT[0:n, h % 2, c, 0:cols],
                                             start=start, stop=stop)
                        if part == 3:
                            last.then_inc(valued, 1)

            @block.vector
            def _(dve):
                o = Order(dve, order)
                for i in range(N + 2):
                    if i < N:
                        it = items[i]
                        dve.wait_ge(scored, i + 1)
                        if it.mask is not None:
                            bank, c0, n, m = it.mask
                            place = (score_banks(i)[:, bank, :] if wide else score_banks(i))[:, c0:c0 + n]
                            o.do(dve.tensor_tensor(place, place, m, ALU.add))
                        dve.tensor_reduce(nmax[:, i % 4:i % 4 + 1], score_banks(i), AX.XY if wide else AX.X,
                                          ALU.max, negate=True).then_inc(maxed, 1)
                    if i >= 2:
                        j = i - 2
                        h, t = j // TT, j % TT
                        dve.wait_ge(turned, j + 1)
                        if h >= 2 and t == 0:
                            dve.wait_ge(valued, h - 1)
                        c0 = items[j].chunks[0][0]
                        c1 = min(4, items[j].chunks[-1][0] + 1)
                        dve.tensor_copy(pT[:, h % 2, c0:c1, t * P:(t + 1) * P],
                                        k.ps[:, 4 + j % 2, c0 * P:c1 * P]
                                        .rearrange("p (c q) -> p c q", q=P)).then_inc(copied, 1)
                    if 1 <= i < N + 1:
                        j = i - 1
                        dve.wait_ge(exped, j + 1)
                        dve.reciprocal(inv[:, j % 4:j % 4 + 1], tot[:, j % 4:j % 4 + 1]).then_inc(inverted, 1)
                        dve.wait_ge(inverted, j + 1)
                        w = prob[:, j % 3, 0:sum(items[j].halves)]
                        dve.tensor_scalar(w, w, inv[:, j % 4:j % 4 + 1], None, ALU.mult).then_inc(shared, 1)

            @block.scalar
            def _(act):
                for i in range(1, N + 6):
                    if i <= N:
                        j = i - 1
                        act.wait_ge(maxed, j + 1)
                        if j >= 3:
                            act.wait_ge(turned, j - 2)
                        if j >= 4:
                            act.wait_ge(inverted, j - 3)
                        act.activation(probs(j), score_banks(j), ACT.Exp, bias=nmax[:, j % 4:j % 4 + 1],
                                       accum_out=tot[:, j % 4:j % 4 + 1]).then_inc(exped, 1)
                    if wide and 2 <= i < N + 2:
                        j = i - 2
                        h, t = j // TT, j % TT
                        n = items[j].chunks[4][1]
                        act.wait_ge(turned, j + 1)
                        if h >= 2 and t == 0:
                            act.wait_ge(valued, h - 1)
                        act.copy(pT[0:n, h % 2, 4, t * P:(t + 1) * P],
                                 turned_place(j, 4)[0:n, :]).then_inc(copied_fifth, 1)
                    if i >= 9 and (i - 6) % 4 == 3:
                        h = (i - 6) // 4
                        if heads[h].store is not None:
                            rows, dst = heads[h].store
                            act.wait_ge(valued, h + 1)
                            act.copy(dst, k.ps[rows, 6, :]).then_inc(stored, 1)


def normed_batch(k, b, twice=True, gain=None, offset=None, dst=None, banks=(6, 7)):
    nc = k.nc
    dst = k.xnT if dst is None else dst
    with ExitStack() as st, signals(nc, *norm_names("n_")) as sems:
        n = Norm(k, st, sems, "n", twice=twice, gain=gain, offset=offset)
        x = batch_tiles(k, b)
        with nc.Block() as block:
            @block.vector
            def _(dve):
                n.dve(dve, x, k.xn)

            @block.gpsimd
            def _(pool):
                n.pool(pool)

            @block.tensor
            def _(pe):
                n.pe(pe, k.xn, banks)

            @block.scalar
            def _(act):
                n.act(act, dst, banks)
                act.wait_ge(n.s_ready, KC)


def output_projection(k, b, o, wo, width, bias_row=None, gain_row=None, offset_row=None, oT=None, before=None):
    given = oT is not None
    nc, C = k.nc, width // P
    with ExitStack() as st, signals(nc, "turned", "moved", "made", "summed", "stats", "aggr", "shifted", "rstd",
                                    "order") as (turned, moved, made, summed, stats, aggr, shifted, rstd, order):
        oT = oT if given else k.sb("attended_T", [P, C, T], st)
        y = k.sb("projected", [P, TT, D], st)
        stat = k.sb("out_stat", [P, TT, 6], st)
        mv = k.sb("out_mv", [P, TT, 2], st)
        rs = k.sb("out_rstd", [P, 2, TT], st)
        x = batch_tiles(k, b)

        def summand(t):
            return k.ps[:, 4 + t, 0:D] if before is None else y[:, t, :]

        with nc.Block() as block:
            @block.tensor
            def _(pe):
                for c in range(0 if given else C):
                    if c >= 4:
                        pe.wait_ge(moved, c - 3)
                    for t in range(TT):
                        last = pe.transpose(k.ps[:, c % 4, t * P:(t + 1) * P], o[:, t, c * P:(c + 1) * P],
                                            k.ident[:, :])
                    last.then_inc(turned, 1)
                if not given:
                    pe.wait_ge(moved, C)
                for t in range(TT):
                    for c in range(C):
                        last = pe.matmul(k.ps[:, 4 + t, 0:D], oT[:, c, t * P:(t + 1) * P], wo[:, c, :],
                                         start=c == 0, stop=c == C - 1)
                    last.then_inc(made, 1)

            @block.scalar
            def _(act):
                for c in range(0 if given else C):
                    act.wait_ge(turned, c + 1)
                    act.copy(oT[:, c, :], k.ps[:, c % 4, :]).then_inc(moved, 1)

            @block.vector
            def _(dve):
                o_ = Order(dve, order)
                if gain_row is None:
                    for t in range(TT):
                        if bias_row is not None:
                            o_.do(dve.tensor_tensor(x(t), x(t), bias_row, ALU.add))
                        dve.wait_ge(made, t + 1)
                        dve.tensor_tensor(x(t), x(t), k.ps[:, 4 + t, 0:D], ALU.add).then_inc(summed, 1)
                    return
                for t in range(TT):
                    dve.wait_ge(made, t + 1)
                    if before is not None:
                        o_.do(dve.tensor_tensor(y[:, t, :], k.ps[:, 4 + t, 0:D], before[0], ALU.add))
                        o_.do(dve.tensor_tensor(y[:, t, :], y[:, t, :], before[1](t), ALU.add))
                    dve.bn_stats(stat[:, t, :], summand(t)).then_inc(stats, 1)
                    dve.wait_ge(stats, t + 1)
                    dve.bn_aggr(mv[:, t, :], stat[:, t, :]).then_inc(aggr, 1)
                dve.wait_ge(rstd, 1)
                dve.wait_ge(aggr, TT)
                for t in range(TT):
                    o_.do(dve.tensor_scalar(y[:, t, :], summand(t), mv[:, t, 0:1], rs[:, 1, t:t + 1],
                                            ALU.subtract, ALU.mult))
                    o_.do(dve.tensor_tensor(y[:, t, :], y[:, t, :], gain_row, ALU.mult))
                    o_.do(dve.tensor_tensor(y[:, t, :], y[:, t, :], offset_row, ALU.add))
                    dve.tensor_tensor(x(t), x(t), y[:, t, :], ALU.add).then_inc(summed, 1)

            if gain_row is not None:
                @block.gpsimd
                def _(pool):
                    pool.wait_ge(aggr, TT)
                    pool.tensor_scalar(rs[:, 0, :], mv[:, :, 1], EPS, 1.0, ALU.add, ALU.mult).then_inc(shifted, 1)
                    pool.wait_ge(shifted, 1)
                    pool.tensor_tensor(rs[:, 1, :], rs[:, 0, :], k.half[:, 0:TT], ALU.pow).then_inc(rstd, 1)


def head_columns(k, dst, src, mask8, width):
    nc = k.nc
    with signals(nc, "masked") as (masked,), nc.Block() as block:
        @block.vector
        def _(dve):
            for h in range(16):
                dve.tensor_scalar(dst[:, h, 0:width], src[:, h // 8, 0:width], mask8[:, h % 8:h % 8 + 1], None,
                                  ALU.mult).then_inc(masked, 1)


def l0_xattn(k):
    nc = k.nc
    NK = 64
    with ExitStack() as st:
        wq, wk, wv, wo = (k.weight("L0_xattn_" + n, st) for n in ("wq", "wk", "wv", "wo"))
        ctxT = k.weight("ctx_T", st)
        mask8 = k.const("head_mask8", st)
        logw = k.weight("L0_side", st)
        k.load(wq, wk, wv, wo, ctxT, mask8, logw)
        kT = k.sb("keys_T", [P, KC, B, NK], st)
        ctx2 = k.sb("ctx_T_twice", [P, KC, B, 2, NK], st)
        with signals(nc, "doubled") as (doubled,), nc.Block() as block:
            @block.vector
            def _(dve):
                for i in range(2):
                    dve.tensor_copy(ctx2[:, :, :, i, :], ctxT[:, :, :].rearrange("p c (b n) -> p c b n", b=B))\
                        .then_inc(doubled, 1)

        v = k.sb("values", [2 * NK, B, D], st)
        project(k, [Product(kT[:, c, :, :].rearrange("p b n -> p (b n)"),
                            [(wk[:, i, c * P:(c + 1) * P], ctxT[:, i, :]) for i in range(KC)], P, B * NK,
                            add=k.vec("L0_xattn_bk")[:, c:c + 1]) for c in range(KC)] +
                [Product(v[:, b, :], [(ctx2[:, i, b, :, :].rearrange("p s n -> p (s n)"), wv[:, i, :])
                                      for i in range(KC)], 2 * NK, D, row=k.row("L0_xattn_bv")) for b in range(B)])
        with signals(nc, "shifted", "logged") as (shifted, logged), nc.Block() as block:
            @block.vector
            def _(dve):
                dve.tensor_scalar(logw[:, 0, :], logw[:, 0, :], 1e-20, 2.0 ** 20, ALU.add,
                                  ALU.mult).then_inc(shifted, 1)
                dve.wait_ge(logged, 1)
                dve.tensor_scalar(logw[:, 0, :], logw[:, 0, :], -20 * float(np.log(2.0)), None,
                                  ALU.add).then_inc(shifted, 1)

            @block.scalar
            def _(act):
                act.wait_ge(shifted, 1)
                act.activation(logw[:, 0, :], logw[:, 0, :], ACT.Ln).then_inc(logged, 1)

        qT = k.sb("queries_T", [P, KC, T], st)
        km = k.sb("keys_by_head", [P, 16, NK], st)
        lw = k.sb("log_weights", [P, 8, NK], st)
        vb = k.sb("values_batch", [P, 8, 32], st)
        kb = k.sb("keys_batch", [P, KC, NK], st)
        o = k.sb("attended", [P, TT, D], st)
        prob = k.sb("probs", [P, 3, 8, NK], st)
        pT = k.sb("probs_T", [P, 2, 4, P], st)
        mx = k.sb("max", [P, 4, 8], st)
        tot = k.sb("exp_sum", [P, 4, 8], st)
        inv = k.sb("inv_sum", [P, 4, 8], st)
        with signals(nc, "zeroed") as (zeroed,), nc.Block() as block:
            @block.vector
            def _(dve):
                dve.memset(vb[:, :, :], 0.0).then_inc(zeroed, 1)
        with nc.Fori(0, B) as b:
            normed_batch(k, b, twice=False)
            with signals(nc, "picked") as (picked,), nc.Block() as block:
                @block.vector
                def _(dve):
                    dve.tensor_copy(kb[:, :, :], kT[:, :, bass.ds(b, 1), :].rearrange("p c o n -> p c (o n)"))\
                        .then_inc(picked, 1)
                    for half in range(2):
                        r = slice(NK * half, NK * (half + 1))
                        dve.tensor_copy(vb[r, :, 16 * half:16 * half + 16],
                                        v[r, bass.ds(b, 1), :].rearrange("p o (i s d) -> p (o i) s d", s=2, d=16)
                                        [:, :, half, :]).then_inc(picked, 1)
                    dve.tensor_copy(lw[:, :, :], logw[:, 0, bass.ds(b * NK, NK)].unsqueeze(1)
                                    .to_broadcast([P, 8, NK])).then_inc(picked, 1)
            head_columns(k, km, kb, mask8, NK)
            project(k, [Product(qT[:, c, :], [(wq[:, i, c * P:(c + 1) * P], k.xnT[:, i, :]) for i in range(KC)],
                                P, T, add=k.vec("L0_xattn_bq")[:, c:c + 1], mult=0.25) for c in range(KC)])
            items = [(t, c) for t in range(TT) for c in range(KC)]
            N = len(items)
            with signals(nc, "scored", "maxed", "below", "exped", "summed", "turned", "copied", "valued", "stored",
                         "order") as (scored, maxed, below, exped, summed, turned, copied, valued, stored,
                                      order), nc.Block() as block:
                @block.tensor
                def _(pe):
                    for i in range(N + 3):
                        if i < N:
                            t, c = items[i]
                            if i >= 3:
                                pe.wait_ge(below, i - 2)
                            pe.matmul(k.ps[:, i % 3, :], qT[:, c, t * P:(t + 1) * P],
                                      km[:, 8 * c:8 * c + 8, :].rearrange("p h n -> p (h n)"), start=True,
                                      stop=False)
                            pe.matmul(k.ps[:, i % 3, :], k.ones[0:1, :],
                                      lw[0:1, :, :].rearrange("p h n -> p (h n)"), start=False,
                                      stop=True).then_inc(scored, 1)
                        if 2 <= i < N + 2:
                            j = i - 2
                            pe.wait_ge(exped, j + 1)
                            if j >= 2:
                                pe.wait_ge(copied, j - 1)
                            for a in range(4):
                                last = pe.transpose(k.ps[:, 4 + j % 2, a * P:(a + 1) * P],
                                                    prob[:, j % 3, 2 * a:2 * a + 2, :].rearrange(
                                                        "p h n -> p (h n)"), k.ident[:, :])
                            last.then_inc(turned, 1)
                        if i >= 3:
                            j = i - 3
                            t, c = items[j]
                            pe.wait_ge(copied, j + 1)
                            if j >= 2:
                                pe.wait_ge(stored, j - 1)
                            for a in range(4):
                                last = pe.matmul(k.ps[:, 6 + j % 2, 32 * a:32 * a + 32], pT[:, j % 2, a, :],
                                                 vb[:, 4 * c + a, :], start=True, stop=True)
                            last.then_inc(valued, 1)

                @block.scalar
                def _(act):
                    for i in range(N + 2):
                        if i < N:
                            act.wait_ge(below, i + 1)
                            act.activation(prob[:, i % 3, :, :], prob[:, i % 3, :, :],
                                           ACT.Exp).then_inc(exped, 1)
                        if i >= 2:
                            j = i - 2
                            act.wait_ge(turned, j + 1)
                            if j >= 2:
                                act.wait_ge(valued, j - 1)
                            act.copy(pT[:, j % 2, :, :], k.ps[:, 4 + j % 2, :].rearrange(
                                "p (c q) -> p c q", c=4)).then_inc(copied, 1)

                @block.vector
                def _(dve):
                    ord_ = Order(dve, order)
                    for i in range(N + 3):
                        if i < N:
                            dve.wait_ge(scored, i + 1)
                            s_ps = k.ps[:, i % 3, :].rearrange("p (h n) -> p h n", h=8)
                            dve.reduce_max(mx[:, i % 4, :], s_ps, AX.X).then_inc(maxed, 1)
                            dve.wait_ge(maxed, i + 1)
                            if i >= 3:
                                dve.wait_ge(turned, i - 2)
                                dve.wait_ge(summed, i - 2)
                            dve.tensor_tensor(prob[:, i % 3, :, :], s_ps, mx[:, i % 4, :].unsqueeze(2)
                                              .to_broadcast([P, 8, NK]), ALU.subtract).then_inc(below, 1)
                        if 1 <= i < N + 1:
                            j = i - 1
                            dve.wait_ge(exped, j + 1)
                            dve.reduce_sum(tot[:, j % 4, :], prob[:, j % 3, :, :], AX.X).then_inc(summed, 1)
                            dve.wait_ge(summed, j + 1)
                            ord_.mark(dve.reciprocal(inv[:, j % 4, :], tot[:, j % 4, :]))
                        if i >= 3:
                            j = i - 3
                            t, c = items[j]
                            dve.wait_ge(valued, j + 1)
                            dve.wait_ge(order, j + 1)
                            dve.tensor_tensor(o[:, t, c * P:(c + 1) * P].rearrange("p (h d) -> p h d", h=8),
                                              k.ps[:, 6 + j % 2, 0:P].rearrange("p (h d) -> p h d", h=8),
                                              inv[:, j % 4, :].unsqueeze(2).to_broadcast([P, 8, 16]),
                                              ALU.mult).then_inc(stored, 1)
            output_projection(k, b, o, wo, D, bias_row=k.row("L0_xattn_bo"))


def l2_attn(k):
    nc = k.nc
    with ExitStack() as st:
        wq, wk, wv, wo = (k.weight("L2_attn_" + n, st) for n in ("Wq", "Wk", "Wv", "Wo"))
        mask8 = k.const("head_mask8", st)
        block_mask = k.const("block_mask", st)
        k.load(wq, wk, wv, wo, mask8, block_mask)
        qT = k.sb("queries_T", [P, KC, T], st)
        kT = k.sb("keys_T", [P, KC, T], st)
        km = k.sb("keys_by_head", [P, 16, T], st)
        v = k.sb("values", [P, TT, D], st)
        vh = k.sb("values_by_head", [P, TT, 16, P], st)
        o = k.sb("attended_T", [P, KC, T], st)
        with signals(nc, "zeroed") as (zeroed,), nc.Block() as block:
            @block.gpsimd
            def _(pool):
                pool.memset(vh[:, :, :, :], 0.0).then_inc(zeroed, 1)
        with nc.Fori(0, B) as b:
            normed_batch(k, b, twice=False)
            project(k, [Product(qT[:, c, :], [(wq[:, i, c * P:(c + 1) * P], k.xnT[:, i, :]) for i in range(KC)],
                                P, T, add=k.vec("L2_attn_bq")[:, c:c + 1], mult=k.vec("L2_scale")[:, 0:1])
                        for c in range(KC)] +
                    [Product(kT[:, c, :], [(wk[:, i, c * P:(c + 1) * P], k.xnT[:, i, :]) for i in range(KC)],
                             P, T, add=k.vec("L2_attn_bk")[:, c:c + 1]) for c in range(KC)] +
                    [Product(v[:, t, :], [(k.xnT[:, i, t * P:(t + 1) * P], wv[:, i, :]) for i in range(KC)],
                             P, D, row=k.row("L2_attn_bv")) for t in range(TT)])
            head_columns(k, km, kT, mask8, T)
            with signals(nc, "spread") as (spread,), nc.Block() as block:
                @block.vector
                def _(dve):
                    for c in range(TT):
                        for g in range(KC):
                            dve.tensor_copy(vh[:, c, 8 * g:8 * g + 8, :].rearrange(
                                "p h (a d) -> p (h a) d", d=16)[:, 0:64:9, :],
                                v[:, c, g * P:(g + 1) * P].rearrange("p (h d) -> p h d", d=16)).then_inc(spread, 1)

            def parts(h):
                return [[(c, P, vh[:, c, h, :], (c + 1) * P, h % 8 == 0 and c == TT - 1, h % 8 == 7 and c == 0)]
                        for c in reversed(range(TT))]

            attend(k, [Item([T - t * P], [(qT[:, h // 8, t * P:(t + 1) * P], km[:, h, t * P:T], 0)],
                            [(c, P) for c in range(t, TT)], mask=(0, 0, P, block_mask[:, :]))
                       for h in range(16) for t in range(TT)],
                   [Head(slice(0, P), parts(h), store=(slice(0, P), o[:, h // 8, :]) if h % 8 == 7 else None)
                    for h in range(16)])
            output_projection(k, b, None, wo, D, oT=o, bias_row=k.row("L2_attn_bo"))


def unit_heads(k, units, src, w, inv_width, floor):
    nc, N = k.nc, len(units)
    with ExitStack() as st, signals(nc, "made", "squared", "summed", "floored", "inverted", "scaled", "turned",
                                    "moved") as (made, squared, summed, floored, inverted, scaled, turned, moved):
        sq = k.sb("squares", [P, 2, 512], st)
        un = k.sb("unit_rows", [P, 2, 512], st)
        ss = k.sb("square_sum", [P, 4, 3, 8], st)
        with nc.Block() as block:
            @block.tensor
            def _(pe):
                for i in range(N + 3):
                    if i < N:
                        t0, n, c0, _, _ = units[i]
                        if i >= 4:
                            pe.wait_ge(scaled, i - 3)
                        for c in range(KC):
                            last = pe.matmul(k.ps[0:n, i % 4, :], src[:, c, t0:t0 + n], w[:, c, c0:c0 + 512],
                                             start=c == 0, stop=c == KC - 1)
                        last.then_inc(made, 1)
                    if i >= 3:
                        j = i - 3
                        n = units[j][1]
                        pe.wait_ge(scaled, j + 1)
                        if j >= 4:
                            pe.wait_ge(moved, j - 3)
                        for c in range(4):
                            last = pe.transpose(k.ps[:, 4 + j % 4, c * n:(c + 1) * n],
                                                un[0:n, j % 2, c * P:(c + 1) * P], k.ident[0:n, 0:n])
                        last.then_inc(turned, 1)

            @block.scalar
            def _(act):
                for i in range(N + 3):
                    if i < N:
                        n = units[i][1]
                        act.wait_ge(made, i + 1)
                        if i >= 2:
                            act.wait_ge(summed, i - 1)
                        act.activation(sq[0:n, i % 2, :], k.ps[0:n, i % 4, :], ACT.Square).then_inc(squared, 1)
                    if i >= 3:
                        _, n, _, dst, gain = units[i - 3]
                        act.wait_ge(turned, i - 2)
                        act.mul(dst, k.ps[:, 4 + (i - 3) % 4, 0:4 * n].rearrange("p (c n) -> p c n", c=4),
                                gain).then_inc(moved, 1)

            @block.vector
            def _(dve):
                for i in range(N + 1):
                    if i < N:
                        n = units[i][1]
                        dve.wait_ge(squared, i + 1)
                        if i >= 4:
                            dve.wait_ge(floored, i - 3)
                        dve.reduce_sum(ss[0:n, i % 4, 0, :], sq[0:n, i % 2, :].rearrange("p (h d) -> p h d", h=8),
                                       AX.X).then_inc(summed, 1)
                    if i >= 1:
                        j = i - 1
                        n = units[j][1]
                        dve.wait_ge(inverted, j + 1)
                        if j >= 2:
                            dve.wait_ge(turned, j - 1)
                        dve.tensor_tensor(un[0:n, j % 2, :].rearrange("p (h d) -> p h d", h=8),
                                          k.ps[0:n, j % 4, :].rearrange("p (h d) -> p h d", h=8),
                                          ss[0:n, j % 4, 2, :].unsqueeze(2).to_broadcast([n, 8, 64]),
                                          ALU.mult).then_inc(scaled, 1)

            @block.gpsimd
            def _(pool):
                for i in range(N):
                    n = units[i][1]
                    pool.wait_ge(summed, i + 1)
                    pool.tensor_scalar(ss[0:n, i % 4, 1, :], ss[0:n, i % 4, 0, :], inv_width, floor, ALU.mult,
                                       ALU.max).then_inc(floored, 1)
                    pool.wait_ge(floored, i + 1)
                    if i >= 4:
                        pool.wait_ge(scaled, i - 3)
                    pool.tensor_tensor(ss[0:n, i % 4, 2, :], ss[0:n, i % 4, 1, :], k.half[0:n, 0:8],
                                       ALU.pow).then_inc(inverted, 1)


def latent_attention(k, pre, H, names, unit=None, mask=None, **out_rows):
    nc = k.nc
    NC = 64
    W = H * 64
    NK = T + NC
    PAIRS = W // P
    lg, lb, cg, cb, w_out = names
    with ExitStack() as st:
        wq, wkv, wo = (k.weight(pre + n, st) for n in ("Wq", "Wkv", w_out))
        ctx = k.const("ctx_rows", st)
        kmask = k.weight(mask, st) if mask else None
        k.load(wq, wkv, wo, ctx, *([kmask] if mask else []))
        ctxT = k.sb("context_T", [P, KC, B * NC], st)
        cn = k.sb("context_normed", [P, B, D], st)
        with signals(nc, *norm_names("c_")) as sems, ExitStack() as cs:
            n = Norm(k, cs, sems, "c", twice=False, gain=k.vec(pre + cg), offset=k.vec(pre + cb), tiles=B, rows=NC)
            with nc.Block() as block:
                @block.vector
                def _(dve):
                    n.dve(dve, lambda t: ctx[:, t, :], cn)

                @block.gpsimd
                def _(pool):
                    n.pool(pool)

                @block.tensor
                def _(pe):
                    n.pe(pe, cn, (6, 7))

                @block.scalar
                def _(act):
                    n.act(act, ctxT, (6, 7))
        kvT = k.sb("kv_input_T", [P, KC, NK], st)
        qT = k.sb("queries_T", [P, PAIRS, T], st)
        kT = k.sb("keys_T", [P, PAIRS, NK], st)
        v = k.sb("values", [P, TT + 1, W], st)
        km = k.sb("key_mask", [P, NC], st) if mask else None
        o = k.sb("attended_T", [P, PAIRS, T], st)
        with nc.Fori(0, B) as b:
            normed_batch(k, b, gain=k.vec(pre + lg), offset=k.vec(pre + lb), dst=kvT)
            with signals(nc, "picked") as (picked,), nc.Block() as block:
                @block.vector
                def _(dve):
                    dve.tensor_copy(kvT[:, :, T:NK], ctxT[:, :, bass.ds(b * NC, NC)]).then_inc(picked, 1)
                    if mask:
                        dve.tensor_scalar(km[:, :], kmask[:, 0, bass.ds(b * NC, NC)], 1.0, -1.0, ALU.min,
                                          ALU.add).then_inc(picked, 1)
                        dve.wait_ge(picked, 2)
                        dve.tensor_scalar(km[:, :], km[:, :], 1e30, None, ALU.mult).then_inc(picked, 1)
            values = [Product(v[0:n, t, a * 512:(a + 1) * 512],
                              [(kvT[:, i, t * P:t * P + n], wkv[:, i, W + a * 512:W + (a + 1) * 512])
                               for i in range(KC)], n, 512)
                      for t, n in enumerate([P] * TT + [NC]) for a in range(W // 512)]
            if unit is None:
                project(k, [Product(qT[:, j, :], [(wq[:, i, j * P:(j + 1) * P], kvT[:, i, 0:T])
                                                  for i in range(KC)], P, T, mult=0.125) for j in range(PAIRS)] +
                        [Product(kT[:, j, c0:c1], [(wkv[:, i, j * P:(j + 1) * P], kvT[:, i, c0:c1])
                                                   for i in range(KC)], P, c1 - c0)
                         for j in range(PAIRS) for c0, c1 in ((0, T), (T, NK))] + values)
            else:
                inv_width, floor, qg, kg = unit
                for w, dst, gain, last in ((wq, qT, qg, TT), (wkv, kT, kg, TT + 1)):
                    unit_heads(k, [(t * P, P if t < TT else NC, a * 512,
                                    dst[:, 4 * a:4 * a + 4, t * P:t * P + (P if t < TT else NC)], gain)
                                   for t in range(last) for a in range(W // 512)], kvT, w, inv_width, floor)
                project(k, values)
            items, heads = [], []
            half = NK // 2
            for h in range(H):
                r = slice(64 * (h % 2), 64 * (h % 2) + 64)
                for t in range(TT):
                    q = qT[r, h // 2, t * P:(t + 1) * P]
                    items.append(Item([half, half], [(q, kT[r, h // 2, a * half:(a + 1) * half], a)
                                                     for a in range(2)],
                                      list(enumerate([P] * TT + [NC])),
                                      mask=(1, half - NC, NC, km[:, :]) if mask else None))
                pieces = [(c, n, v[0:n, c, h * 64:(h + 1) * 64], T, c == 0, c == TT)
                          for c, n in enumerate([P] * TT + [NC])]
                heads.append(Head(r, [pieces[0:2], pieces[2:3], pieces[3:4], pieces[4:5]],
                                  store=(r, o[r, h // 2, :])))
            attend(k, items, heads)
            output_projection(k, b, None, wo, W, oT=o, **out_rows)


def l1_xattn(k):
    latent_attention(k, "L1_xattn_", 16, ("ln_l_g", "ln_l_b", "ln_m_g", "ln_m_b", "Wout"))


def l2_xattn(k):
    latent_attention(k, "L2_xattn_", 16, ("ln_l_g", "ln_l_b", "ln_x_g", "ln_x_b", "Wout"),
                     unit=(1.0 / 64, 1e-16, k.vec("L2_query_gain")[:, 0:1], k.vec("L2_xattn_kn_g2")[:, 0:1]),
                     mask="mask_bf1", bias_row=k.row("L2_xattn_bout"))


def l3_xattn(k):
    latent_attention(k, "L3_xattn_", 8, ("ln_l_w", "ln_l_b", "ln_x_w", "ln_x_b", "Wo"),
                     unit=(1.0, 1e-24, k.vec("L3_query_gain")[:, 0:1], k.vec("L3_xattn_k_scale2")[:, 0:1]),
                     mask="mask_bk0", gain_row=k.row("L3_xattn_ln_o_w"), offset_row=k.row("L3_xattn_ln_o_b"))



def l1_attn(k):
    nc = k.nc
    C = 16
    NCH = T // C
    PER = P // C
    with ExitStack() as st:
        ws = {n: k.weight("L1_attn_" + n, st) for n in ("Wq", "Wk", "Wv", "Wg", "Wo")}
        mask8 = k.const("head_mask8", st)
        diag = k.const("chunk_diagonal", st)
        k.load(*ws.values(), mask8, diag)
        q = k.sb("queries_decayed", [P, 2, NCH, C], st)
        kT = k.sb("keys_T", [P, NCH, C], st)
        g = k.sb("gates_T", [P, NCH, C], st)
        v = k.sb("values", [P, TT, P], st)
        vj = k.sb("values_by_position", [NCH, C, P], st)
        kd = k.sb("keys_decayed", [P, NCH, C], st)
        kdt = k.sb("keys_decayed_rows", [P, TT, P], st)
        r = k.sb("suffix_gates", [P, NCH], st)
        a = k.sb("scores_diagonal", [NCH, 2, NCH * C], st)
        vm = k.sb("values_by_chunk", [P, TT, PER, P], st)
        state = k.sb("states", [P, NCH + 1, P], st)
        zero = k.sb("zeros", [P, T], st)
        oT = k.sb("attended_T", [P, 1, T], st)
        with signals(nc, "zeroed") as (zeroed,), nc.Block() as block:
            @block.gpsimd
            def _(pool):
                pool.memset(zero[:, :], 0.0).then_inc(zeroed, 1)
                pool.memset(state[:, 0, :], 0.0).then_inc(zeroed, 1)
        with nc.Fori(0, B) as b:
            normed_batch(k, b, twice=False)
            flat = lambda w: w.rearrange("p c j -> p (c j)")
            positions = k.xnT[:, :, :].rearrange("p i (c j) -> p i c j", j=C)
            project(k, [Product(flat(dst), [(ws[n][:, i, :], k.xnT[:, i, :]) for i in range(KC)], P, T,
                                add=k.vec("L1_attn_b" + n[1])[:, 0:1])
                        for n, dst in (("Wg", g[:, :, :]), ("Wq", q[:, 0, :, :]), ("Wq", q[:, 1, :, :]),
                                       ("Wk", kT[:, :, :]))] +
                    [Product(v[:, t, :], [(k.xnT[:, i, t * P:(t + 1) * P], ws["Wv"][:, i, :]) for i in range(KC)],
                             P, P, row=k.row("L1_attn_bv")) for t in range(TT)] +
                    [Product(vj[:, j, :], [(positions[:, i, :, j], ws["Wv"][:, i, :]) for i in range(KC)],
                             NCH, P, row=k.row("L1_attn_bv")[0:NCH, :]) for j in range(C)])
            with signals(nc, "gated", "scored", "scored_diag", "decayed", "order", "within", "spread", "turned",
                         "moved", "kv_made", "carried", "outed") as (
                    gated, scored, scored_diag, decayed, order, within, spread, turned, moved, kv_made, carried,
                    outed), nc.Block() as block:
                @block.scalar
                def _(act):
                    act.activation(g[:, :, :], g[:, :, :], ACT.Sigmoid).then_inc(gated, 1)
                    act.wait_ge(turned, 1)
                    act.copy(kdt[:, :, :], k.ps[:, 3, :].rearrange("p (t s) -> p t s", t=TT)).then_inc(moved, 1)
                    act.wait_ge(outed, 1)
                    act.copy(oT[:, 0, :], k.ps[:, 2, :]).then_inc(moved, 1)

                @block.gpsimd
                def _(pool):
                    for t in range(TT):
                        pool.tensor_tensor(vm[:, t, :, :], v[:, t, :].unsqueeze(1).to_broadcast([P, PER, P]),
                                           mask8[:, :].unsqueeze(2).to_broadcast([P, PER, P]),
                                           ALU.mult).then_inc(spread, 1)

                @block.vector
                def _(dve):
                    o = Order(dve, order)
                    o.mark(dve.memset(r[:, :], 1.0))
                    dve.wait_ge(gated, 1)
                    for n in range(C):
                        j = C - 1 - n
                        w = C - j
                        src, dst = q[:, n % 2, :, j:C], q[:, (n + 1) % 2, :, j:C]
                        o.wait()
                        o.mark(dve.tensor_tensor(kd[:, :, j], kT[:, :, j], r[:, :], ALU.mult))
                        if n >= 1:
                            dve.wait_ge(scored, n)
                            dve.wait_ge(decayed, n)
                        dve.tensor_tensor(dst, src, g[:, :, j:j + 1].to_broadcast([P, NCH, w]),
                                          ALU.mult).then_inc(decayed, 1)
                        o.wait()
                        o.mark(dve.tensor_tensor(r[:, :], r[:, :], g[:, :, j], ALU.mult))
                        dve.wait_ge(scored, n + 1)
                        if n >= 2:
                            dve.wait_ge(within, n - 1)
                        dve.tensor_tensor(a[:, n % 2, 0:NCH * w].rearrange("p (c i) -> p c i", i=w),
                                          k.ps[0:NCH, n % 2, 0:NCH * w].rearrange("p (c i) -> p c i", i=w),
                                          diag[:, :].unsqueeze(2).to_broadcast([NCH, NCH, w]),
                                          ALU.mult).then_inc(scored_diag, 1)
                    o.wait()
                    for c in range(NCH):
                        dve.wait_ge(kv_made, c // 4 + 1)
                        if c:
                            dve.wait_ge(carried, c)
                        dve.scalar_tensor_tensor(out=state[:, c + 1, :], in0=state[:, c, :], scalar=r[:, c:c + 1],
                                                 in1=k.ps[:, 4 + (c // 4) % 4, (c % 4) * P:(c % 4 + 1) * P],
                                                 op0=ALU.mult, op1=ALU.add).then_inc(carried, 1)

                @block.tensor
                def _(pe):
                    pe.matmul(k.ps[:, 2, :], zero[0:1, 0:P], zero[0:1, :], start=True, stop=False,
                              skip_group_check=True)
                    out = k.ps[:, 2, :].rearrange("p (c i) -> p c i", i=C)

                    def add_within(n):
                        j = C - 1 - n
                        w = C - j
                        pe.wait_ge(scored_diag, n + 1)
                        pe.matmul(out[:, :, j:C], vj[:, j, :],
                                  a[:, n % 2, 0:NCH * w].rearrange("p (c i) -> p c i", i=w), start=False,
                                  stop=False, skip_group_check=True).then_inc(within, 1)

                    for n in range(C):
                        j = C - 1 - n
                        w = C - j
                        if n >= 1:
                            pe.wait_ge(decayed, n)
                        if n >= 2:
                            pe.wait_ge(scored_diag, n - 1)
                        pe.matmul(k.ps[0:NCH, n % 2, 0:NCH * w].rearrange("p (c i) -> p c i", i=w), kT[:, :, j],
                                  q[:, n % 2, :, j:C], start=True, stop=True).then_inc(scored, 1)
                        if n >= 1:
                            add_within(n - 1)
                    add_within(C - 1)
                    pe.wait_ge(order, 2 * C)
                    flat_kd = flat(kd[:, :, :])
                    for t in range(TT):
                        last = pe.transpose(k.ps[:, 3, t * P:(t + 1) * P], flat_kd[:, t * P:(t + 1) * P],
                                            k.ident[:, :])
                    last.then_inc(turned, 1)
                    pe.wait_ge(moved, 1)
                    pe.wait_ge(spread, TT)
                    for u in range(2 * TT):
                        if u >= 4:
                            pe.wait_ge(carried, 4 * (u - 3))
                        pe.matmul(k.ps[:, 4 + u % 4, :], kdt[:, u // 2, :],
                                  vm[:, u // 2, 4 * (u % 2):4 * (u % 2) + 4, :].rearrange("p c v -> p (c v)"),
                                  start=True, stop=True).then_inc(kv_made, 1)
                    pe.wait_ge(decayed, C)
                    for c in range(NCH):
                        if c:
                            pe.wait_ge(carried, c)
                        last = pe.matmul(out[:, c, :], state[:, c, :], q[:, C % 2, c, :], start=False,
                                         stop=c == NCH - 1, skip_group_check=True)
                    last.then_inc(outed, 1)
            output_projection(k, b, None, ws["Wo"], P, oT=oT, gain_row=k.row("L1_attn_gamma"),
                              offset_row=k.row("L1_attn_beta"),
                              before=(k.row("L1_attn_bo"), lambda t: k.xn[:, t, :]))



def l1_ffn(k):
    nc = k.nc
    NG = 16
    KEYS = 32
    QC = 4
    with ExitStack() as st:
        wq, down, up = (k.weight(n, st) for n in ("L1_ffn_Wq", "L1_ffn_expert_down", "L1_ffn_expert_up"))
        keys = k.weight("L1_sub_keys", st)
        pair_mean = k.const("pair_mean", st)
        group4 = k.const("group_of_32", st)
        k.load(wq, down, up, keys, pair_mean, group4)
        q = k.sb("queries_T", [P, QC, B * T], st)
        stat = k.sb("query_stat", [P, B * QC, 6], st)
        mv = k.sb("query_mv", [P, 2], st)
        col = k.sb("query_columns", [P, 8], st)
        with signals(nc, "squared", "summed", "floored", "inverted", "unit") as (
                squared, summed, floored, inverted, unit), ExitStack() as ks, nc.Block() as block:
            k2 = k.sb("keys_squared", [P, 3, P], ks)

            @block.vector
            def _(dve):
                dve.tensor_tensor(k2[:, 0, :], keys[:, 0, :], keys[:, 0, :], ALU.mult).then_inc(squared, 1)
                dve.wait_ge(summed, 1)
                dve.tensor_scalar(k2[:, 1, :], k.ps[:, 0, 0:P], 1e-24, None, ALU.max).then_inc(floored, 1)
                dve.wait_ge(inverted, 1)
                dve.tensor_tensor(keys[:, 0, :], keys[:, 0, :], k2[:, 2, :], ALU.mult).then_inc(unit, 1)

            @block.tensor
            def _(pe):
                pe.wait_ge(squared, 1)
                pe.matmul(k.ps[:, 0, 0:P], k.ones[:, :], k2[:, 0, :], start=True, stop=True).then_inc(summed, 1)

            @block.gpsimd
            def _(pool):
                pool.wait_ge(floored, 1)
                pool.tensor_tensor(k2[:, 2, :], k2[:, 1, :], k.half[:, 0:1].to_broadcast([P, P]),
                                   ALU.pow).then_inc(inverted, 1)

        with nc.Fori(0, B) as b:
            normed_batch(k, b, twice=False)
            project(k, [Product(q[:, c, bass.ds(b * T, T)], [(wq[:, i, c * P:(c + 1) * P], k.xnT[:, i, :])
                                                             for i in range(KC)], P, T,
                                add=k.vec("L1_ffn_bq")[:, c:c + 1]) for c in range(QC)])
            with signals(nc, "stats") as (stats,), nc.Block() as block:
                @block.vector
                def _(dve):
                    for c in range(QC):
                        dve.bn_stats(stat[:, bass.ds(b * QC + c, 1), :].rearrange("p o s -> p (o s)"),
                                     q[:, c, bass.ds(b * T, T)]).then_inc(stats, 1)

        with signals(nc, "order", "aggregated", "averaged", "deviated", "spread", "shifted", "inverted") as (
                order, aggregated, averaged, deviated, spread, shifted, inverted), nc.Block() as block:
            @block.vector
            def _(dve):
                o = Order(dve, order)
                dve.bn_aggr(mv[:, :], stat[:, :, :].rearrange("p a s -> p (a s)")).then_inc(aggregated, 1)
                dve.wait_ge(averaged, 1)
                o.do(dve.tensor_copy(col[:, 0:2], k.ps[:, 0, 0:2]))
                dve.wait_ge(aggregated, 1)
                o.do(dve.tensor_tensor(col[:, 2:3], mv[:, 0:1], col[:, 0:1], ALU.subtract))
                o.do(dve.tensor_tensor(col[:, 3:4], col[:, 2:3], col[:, 2:3], ALU.mult))
                dve.tensor_copy(col[:, 2:3], col[:, 3:4]).then_inc(deviated, 1)
                dve.wait_ge(spread, 1)
                dve.tensor_tensor(col[:, 4:5], k.ps[:, 1, 0:1], col[:, 1:2], ALU.add).then_inc(deviated, 1)
                dve.wait_ge(inverted, 1)
                o.do(dve.tensor_tensor(col[:, 6:7], col[:, 5:6], k.vec("L1_bn_gamma2"), ALU.mult))
                o.do(dve.tensor_tensor(col[:, 7:8], col[:, 0:1], col[:, 6:7], ALU.mult))
                o.do(dve.tensor_tensor(col[:, 7:8], k.vec("L1_bn_beta2"), col[:, 7:8], ALU.subtract))

            @block.tensor
            def _(pe):
                pe.wait_ge(aggregated, 1)
                pe.matmul(k.ps[:, 0, 0:2], pair_mean[:, :], mv[:, :], start=True, stop=True).then_inc(averaged, 1)
                pe.wait_ge(deviated, 1)
                pe.matmul(k.ps[:, 1, 0:2], pair_mean[:, :], col[:, 2:4], start=True, stop=True).then_inc(spread, 1)

            @block.gpsimd
            def _(pool):
                pool.wait_ge(deviated, 2)
                pool.tensor_scalar(col[:, 5:6], col[:, 4:5], EPS, 1.0, ALU.add, ALU.mult).then_inc(shifted, 1)
                pool.wait_ge(shifted, 1)
                pool.tensor_tensor(col[:, 5:6], col[:, 5:6], k.half[:, 0:1], ALU.pow).then_inc(inverted, 1)

        qn = k.sb("queries_normed", [P, QC, T], st)
        sq = k.sb("queries_squared", [P, QC, T], st)
        gel = k.sb("expert_hidden", [P, TT, D], st)
        s = k.sb("key_scores", [P, TT, NG, KEYS + 4], st)
        marked = k.sb("key_marked", [P, 2, NG, KEYS + 4], st)
        top = k.sb("key_top", [P, TT, NG, 8], st)
        e = k.sb("key_exp", [P, TT, NG, KEYS], st)
        m = k.sb("key_mask", [P, TT, NG, KEYS], st)
        nrm = k.sb("query_norms", [P, TT, 2, NG], st)
        tot = k.sb("key_sums", [P, TT, 2, NG], st)
        pairs = k.sb("pair_weights", [P, 2, 8, D], st)
        w = k.sb("expert_weights", [P, TT, D], st)
        wt = k.sb("expert_weights_T", [P, KC, T], st)
        far = k.sb("far_weight", [P, TT], st)
        x_ = None
        with signals(nc, "sentinels") as (sentinels,), nc.Block() as block:
            @block.vector
            def _(dve):
                dve.memset(s[:, :, :, KEYS:KEYS + 4], BIG).then_inc(sentinels, 1)
        with nc.Fori(0, B) as b:
            normed_batch(k, b, twice=False)
            x_ = batch_tiles(k, b)
            with signals(nc, "q_normed", "q_squared", "hid_made", "gelued", "scored", "floored", "inverted",
                         "scaled", "topped", "marked", "masked", "below", "exped", "order", "shared", "paired",
                         "summed", "weighted", "turned", "moved", "made", "added") as (
                    q_normed, q_squared, hid_made, gelued, scored, floored, inverted, scaled, topped, marked_s,
                    masked, below, exped, order, shared, paired, summed, weighted, turned, moved, made,
                    added), nc.Block() as block:
                @block.scalar
                def _(act):
                    for c in range(QC):
                        act.activation(qn[:, c, :], q[:, c, bass.ds(b * T, T)], ACT.Identity, bias=col[:, 7:8],
                                       scale=col[:, 6:7]).then_inc(q_normed, 1)
                    act.wait_ge(q_normed, QC)
                    for c in range(QC):
                        act.activation(sq[:, c, :], qn[:, c, :], ACT.Square).then_inc(q_squared, 1)
                    for t in range(TT):
                        act.wait_ge(hid_made, t + 1)
                        act.activation(gel[:, t, :], k.ps[:, 4 + t, 0:D], ACT.Gelu).then_inc(gelued, 1)
                    for t in range(TT):
                        act.wait_ge(below, t + 1)
                        act.activation(e[:, t, :, :], e[:, t, :, :], ACT.Exp).then_inc(exped, 1)
                    for c in range(KC):
                        act.wait_ge(turned, c + 1)
                        act.copy(wt[:, c, :], k.ps[:, c, :]).then_inc(moved, 1)

                @block.tensor
                def _(pe):
                    for t in range(TT):
                        for c in range(KC):
                            last = pe.matmul(k.ps[:, 4 + t, 0:D], k.xnT[:, c, t * P:(t + 1) * P], down[:, c, :],
                                             start=c == 0, stop=c == KC - 1)
                        last.then_inc(hid_made, 1)
                    pe.wait_ge(q_squared, QC)
                    for t in range(TT):
                        if t >= 2:
                            pe.wait_ge(scaled, t - 1)
                        for c in range(QC):
                            pe.matmul(k.ps[:, t % 2, c * P:(c + 1) * P], qn[:, c, t * P:(t + 1) * P],
                                      keys[:, 0, :], start=True, stop=True)
                        for c in range(QC):
                            last = pe.matmul(k.ps[:, 2 + t % 2, 4 * c:4 * c + 4], sq[:, c, t * P:(t + 1) * P],
                                             group4[:, :], start=True, stop=True)
                        last.then_inc(scored, 1)
                    pe.wait_ge(weighted, TT)
                    for c in range(KC):
                        for t in range(TT):
                            last = pe.transpose(k.ps[:, c, t * P:(t + 1) * P], w[:, t, c * P:(c + 1) * P],
                                                k.ident[:, :])
                        last.then_inc(turned, 1)
                    pe.wait_ge(moved, KC)
                    for t in range(TT):
                        for c in range(KC):
                            last = pe.matmul(k.ps[:, 4 + t, 0:D], wt[:, c, t * P:(t + 1) * P], up[:, c, :],
                                             start=c == 0, stop=c == KC - 1)
                        last.then_inc(made, 1)

                @block.gpsimd
                def _(pool):
                    for t in range(TT):
                        pool.wait_ge(floored, t + 1)
                        pool.tensor_tensor(nrm[:, t, 1, :], nrm[:, t, 0, :], k.half[:, 0:NG],
                                           ALU.pow).then_inc(inverted, 1)
                    for t in range(TT):
                        pool.wait_ge(shared, t + 1)
                        if t >= 2:
                            pool.wait_ge(summed, t - 1)
                        halves = e[:, t, :, :].rearrange("p (h s) n -> p h s n", s=2)
                        for h in range(8):
                            last = pool.tensor_tensor(
                                pairs[:, t % 2, h, :].rearrange("p (a c) -> p a c", a=8),
                                halves[:, h, 0, 0:8].unsqueeze(2).to_broadcast([P, 8, KEYS]),
                                halves[:, h, 1, :].unsqueeze(1).to_broadcast([P, 8, KEYS]), ALU.mult)
                            last.then_inc(paired, 1)

                @block.vector
                def _(dve):
                    o = Order(dve, order)
                    for t in range(TT):
                        dve.wait_ge(scored, t + 1)
                        dve.tensor_scalar(nrm[:, t, 0, :], k.ps[:, 2 + t % 2, 0:NG], 1e-24, None,
                                          ALU.max).then_inc(floored, 1)
                        dve.wait_ge(inverted, t + 1)
                        dve.tensor_tensor(s[:, t, :, 0:KEYS],
                                          k.ps[:, t % 2, :].rearrange("p (g n) -> p g n", g=NG),
                                          nrm[:, t, 1, :].unsqueeze(2).to_broadcast([P, NG, KEYS]),
                                          ALU.mult).then_inc(scaled, 1)
                    def best_four(t):
                        dve.wait_ge(scaled, t + 1)
                        for g in range(NG):
                            dve.max(top[:, t, g, :], s[:, t, g, :]).then_inc(topped, 1)
                        dve.wait_ge(topped, NG * (t + 1))
                        o.do(dve.tensor_tensor(e[:, t, :, :], s[:, t, :, 0:KEYS],
                                               top[:, t, :, 4:5].to_broadcast([P, NG, KEYS]), ALU.subtract))
                        dve.tensor_scalar(e[:, t, :, :], e[:, t, :, :], 0.0, None, ALU.min).then_inc(below, 1)
                        if t >= 2:
                            dve.wait_ge(masked, t - 1)
                        for g in range(NG):
                            dve.match_replace(marked[:, t % 2, g, :], top[:, t, g, :], s[:, t, g, :],
                                              -BIG).then_inc(marked_s, 1)
                        dve.wait_ge(marked_s, NG * (t + 1))
                        dve.tensor_scalar(m[:, t, :, :], marked[:, t % 2, :, 0:KEYS], -BIG, None,
                                          ALU.is_equal).then_inc(masked, 1)

                    def share(t):
                        dve.wait_ge(exped, t + 1)
                        dve.wait_ge(masked, t + 1)
                        o.do(dve.tensor_tensor(e[:, t, :, :], e[:, t, :, :], m[:, t, :, :], ALU.mult))
                        o.do(dve.reduce_sum(tot[:, t, 0, :], e[:, t, :, :], AX.X))
                        o.do(dve.reciprocal(tot[:, t, 1, :], tot[:, t, 0, :]))
                        dve.tensor_tensor(e[:, t, :, :], e[:, t, :, :],
                                          tot[:, t, 1, :].unsqueeze(2).to_broadcast([P, NG, KEYS]),
                                          ALU.mult).then_inc(shared, 1)
                        dve.wait_ge(shared, t + 1)
                        o.mark(dve.tensor_reduce(far[:, t:t + 1], e[:, t, :, :].rearrange(
                            "p (h s) n -> p h s n", s=2)[:, :, 0, 8:KEYS], AX.XY, ALU.add))

                    def weigh(t):
                        dve.wait_ge(paired, 8 * (t + 1))
                        dve.tensor_reduce(w[:, t, :], pairs[:, t % 2, :, :].rearrange("p h n -> p n h"), AX.X,
                                          ALU.add).then_inc(summed, 1)
                        dve.wait_ge(summed, t + 1)
                        o.wait()
                        o.do(dve.tensor_tensor(w[:, t, D - 1:D], w[:, t, D - 1:D], far[:, t:t + 1], ALU.add))
                        dve.wait_ge(gelued, t + 1)
                        dve.tensor_tensor(w[:, t, :], w[:, t, :], gel[:, t, :], ALU.mult).then_inc(weighted, 1)

                    best_four(0)
                    for t in range(TT):
                        share(t)
                        if t + 1 < TT:
                            best_four(t + 1)
                        if t >= 1:
                            weigh(t - 1)
                    weigh(TT - 1)
                    for t in range(TT):
                        dve.wait_ge(made, t + 1)
                        dve.tensor_tensor(x_(t), x_(t), k.ps[:, 4 + t, 0:D], ALU.add).then_inc(added, 1)



def l3_attn(k):
    nc = k.nc
    S = B
    with ExitStack() as st:
        ws = {n: k.weight("L3_attn_" + n, st) for n in ("w_q", "w_k", "w_v", "w_o")}
        rk, rv = k.const("rel_k_rows", st), k.const("rel_v_rows", st)
        k.load(*ws.values(), rk, rv)
        qkv = [k.sb(n, [P, S, TT, D], st) for n in ("queries", "keys", "values")]
        out = k.sb("attended", [P, S, TT, D], st)
        with nc.Fori(0, B) as b:
            normed_batch(k, b, twice=False)
            project(k, [Product(dst[:, bass.ds(b, 1), t, :].rearrange("p o d -> p (o d)"),
                                [(k.xnT[:, i, t * P:(t + 1) * P], ws[n][:, i, :]) for i in range(KC)], P, D)
                        for n, dst in zip(("w_q", "w_k", "w_v"), qkv) for t in range(TT)])
        qq = k.sb("queries_tile", [P, S, D], st)
        kk = k.sb("keys_relative", [P, 2, S, D], st)
        vv = k.sb("values_relative", [P, 2, S, D], st)
        prod = k.sb("products", [P, 2, S, D], st)
        sc = k.sb("scores", [P, S * S, 16], st)
        red = k.sb("reduced", [P, 3, S * S], st)
        with nc.Fori(0, TT) as j, signals(nc, "keyed", "valued", "multiplied", "weighted", "order", "exped",
                                          "below", "stored") as (
                keyed, valued, multiplied, weighted, order, exped, below, stored), nc.Block() as block:
            q, kt, v = (w[:, :, bass.ds(j, 1), :].rearrange("p s o d -> p s (o d)") for w in qkv)

            @block.gpsimd
            def _(pool):
                for s in range(S):
                    if s >= 2:
                        pool.wait_ge(multiplied, s - 1)
                    pool.tensor_tensor(kk[:, s % 2, :, :], kt, rk[:, S - 1 - s:2 * S - 1 - s, :],
                                       ALU.add).then_inc(keyed, 1)
                for s in range(S):
                    if s >= 2:
                        pool.wait_ge(weighted, s - 1)
                    pool.tensor_tensor(vv[:, s % 2, :, :], v, rv[:, S - 1 - s:2 * S - 1 - s, :],
                                       ALU.add).then_inc(valued, 1)

            @block.scalar
            def _(act):
                act.wait_ge(below, 1)
                act.activation(sc[:, :, :], sc[:, :, :], ACT.Exp, scale=0.25).then_inc(exped, 1)

            @block.vector
            def _(dve):
                o = Order(dve, order)
                o.do(dve.tensor_copy(qq[:, :, :], q))
                for s in range(S):
                    dve.wait_ge(keyed, s + 1)
                    dve.tensor_tensor(prod[:, s % 2, :, :], kk[:, s % 2, :, :],
                                      qq[:, s, :].unsqueeze(1).to_broadcast([P, S, D]),
                                      ALU.mult).then_inc(multiplied, 1)
                    dve.wait_ge(multiplied, s + 1)
                    o.do(dve.reduce_sum(sc[:, S * s:S * s + S, :], prod[:, s % 2, :, :].rearrange(
                        "p t (h d) -> p t h d", d=16), AX.X))
                o.do(dve.tensor_reduce(red[:, 0, :], sc[:, :, :], AX.X, ALU.max))
                dve.tensor_tensor(sc[:, :, :], sc[:, :, :],
                                  red[:, 0, :].unsqueeze(2).to_broadcast([P, S * S, 16]),
                                  ALU.subtract).then_inc(below, 1)
                dve.wait_ge(exped, 1)
                o.do(dve.reduce_sum(red[:, 1, :], sc[:, :, :], AX.X))
                o.do(dve.reciprocal(red[:, 2, :], red[:, 1, :]))
                o.do(dve.tensor_tensor(sc[:, :, :], sc[:, :, :],
                                       red[:, 2, :].unsqueeze(2).to_broadcast([P, S * S, 16]), ALU.mult))
                for s in range(S):
                    dve.wait_ge(valued, s + 1)
                    dve.tensor_tensor(prod[:, s % 2, :, :].rearrange("p t (h d) -> p (t h) d", d=16),
                                      vv[:, s % 2, :, :].rearrange("p t (h d) -> p (t h) d", d=16),
                                      sc[:, S * s:S * s + S, :].rearrange("p t h -> p (t h)").unsqueeze(2)
                                      .to_broadcast([P, S * 16, 16]), ALU.mult).then_inc(weighted, 1)
                    dve.wait_ge(weighted, s + 1)
                    dve.reduce_sum(out[:, s, bass.ds(j, 1), :].rearrange("p o d -> p (o d)"),
                                   prod[:, s % 2, :, :].rearrange("p t d -> p d t"), AX.X).then_inc(stored, 1)
        with nc.Fori(0, B) as b:
            with signals(nc, "picked") as (picked,), nc.Block() as block:
                @block.vector
                def _(dve):
                    dve.tensor_copy(k.xn[:, :, :], out[:, bass.ds(b, 1), :, :].rearrange("p o t d -> p (o t) d"))\
                        .then_inc(picked, 1)
            output_projection(k, b, k.xn, ws["w_o"], D, bias_row=k.row("L3_attn_b_o"))



E = 8


def top_two_gate(k, st, sems, from_sigmoid):
    scored, rowed, picked, exped, combined, turned, ready, order = sems
    row = k.sb("gate_row", [P, TT, 14], st)
    marked = k.sb("gate_marked", [P, TT, 14], st)
    top = k.sb("gate_top", [P, TT, 8], st)
    mask = k.sb("gate_mask", [P, TT, E], st)
    e = k.sb("gate_exp", [P, TT, E], st)
    tot = k.sb("gate_total", [P, TT, 2], st)
    comb = k.sb("gate_combine", [P, TT, E], st)
    combT = k.sb("combine_T", [E, T], st)
    bank = k.ps[:, 7, :]

    def dve_part(dve):
        o = Order(dve, order)
        o.do(dve.memset(row[:, :, E:14], BIG))
        dve.wait_ge(scored, 1)
        if from_sigmoid:
            dve.wait_ge(rowed, 1)
        else:
            dve.tensor_copy(row[:, :, 0:E], bank[:, 0:TT * E].rearrange("p (t e) -> p t e", t=TT)).then_inc(rowed, 1)
            dve.wait_ge(rowed, 1)
        for t in range(TT):
            o.mark(dve.max(top[:, t, :], row[:, t, :]))
        o.wait()
        for t in range(TT):
            o.mark(dve.match_replace(marked[:, t, :], top[:, t, :], row[:, t, :], -BIG))
        o.wait()
        o.do(dve.tensor_scalar(mask[:, :, :], marked[:, :, 0:E], -BIG, None, ALU.is_equal))
        if from_sigmoid:
            o.do(dve.tensor_tensor(e[:, :, :], row[:, :, 0:E], mask[:, :, :], ALU.mult))
        else:
            o.do(dve.tensor_tensor(e[:, :, :], row[:, :, 0:E], top[:, :, 6:7].to_broadcast([P, TT, E]),
                                   ALU.subtract))
            dve.tensor_scalar(e[:, :, :], e[:, :, :], 0.0, None, ALU.min).then_inc(picked, 1)
            dve.wait_ge(exped, 1)
            o.do(dve.tensor_tensor(e[:, :, :], e[:, :, :], mask[:, :, :], ALU.mult))
        o.do(dve.reduce_sum(tot[:, :, 0], e[:, :, :], AX.X))
        if from_sigmoid:
            o.do(dve.tensor_scalar(tot[:, :, 0], tot[:, :, 0], 1e-20, None, ALU.add))
        o.do(dve.reciprocal(tot[:, :, 1], tot[:, :, 0]))
        dve.tensor_tensor(comb[:, :, :], e[:, :, :], tot[:, :, 1:2].to_broadcast([P, TT, E]),
                          ALU.mult).then_inc(combined, 1)

    def act_part(act):
        act.wait_ge(scored, 1)
        if from_sigmoid:
            act.activation(row[:, :, 0:E], bank[:, 0:TT * E].rearrange("p (t e) -> p t e", t=TT),
                           ACT.Sigmoid).then_inc(rowed, 1)
        else:
            act.wait_ge(picked, 1)
            act.activation(e[:, :, :], e[:, :, :], ACT.Exp).then_inc(exped, 1)
        act.wait_ge(turned, 1)
        act.copy(combT[:, :], bank[0:E, :]).then_inc(ready, 1)

    def pe_part(pe, router):
        for t in range(TT):
            for c in range(KC):
                last = pe.matmul(bank[:, t * E:(t + 1) * E], k.xnT[:, c, t * P:(t + 1) * P], router[:, c, :],
                                 start=c == 0, stop=c == KC - 1)
        last.then_inc(scored, 1)
        pe.wait_ge(combined, 1)
        for t in range(TT):
            last = pe.transpose(bank[0:E, t * P:(t + 1) * P], comb[:, t, :], k.ident[:, :])
        last.then_inc(turned, 1)

    return dve_part, act_part, pe_part, combT, comb


GATE = ["g_scored", "g_rowed", "g_picked", "g_exped", "g_combined", "g_turned", "g_ready", "g_order"]


def l2_ffn(k):
    nc = k.nc
    HC = 3072 // P
    expert_of = [n // 2 if n < 8 else 4 + (n - 8) // 4 for n in range(HC)]
    R = 4
    with ExitStack() as st:
        router = k.weight("L2_ffn_router_w", st)
        w1 = k.weight("L2_ffn_w1", st)
        w2 = k.weight("L2_ffn_w2", st)
        sel = k.const("select8", st)
        k.load(router, w1, w2, sel)
        relu = k.sb("relu", [P, R, T], st)
        rw = k.sb("relu_weighted", [P, R, T], st)
        hT = k.sb("hidden_T", [P, R, T], st)
        wb = k.sb("expert_weight", [P, E, T], st)
        with nc.Fori(0, B) as b, signals(
                nc, *norm_names("n_"), *GATE, "spread", "spread_copied", "up", "relued", "weighted", "squared",
                "consumed", "added") as (*sems, spread, spread_copied, up, relued, weighted, squared,
                                                  consumed, added), ExitStack() as bs:
            n1 = Norm(k, bs, sems[:7], "n", twice=False)
            g_dve, g_act, g_pe, combT, _ = top_two_gate(k, bs, sems[7:], True)
            x = batch_tiles(k, b)
            with nc.Block() as block:
                @block.vector
                def _(dve):
                    n1.dve(dve, x, k.xn)
                    g_dve(dve)
                    for n in range(HC):
                        dve.wait_ge(weighted, n + 1)
                        if n >= R:
                            dve.wait_ge(consumed, n - R + 1)
                        dve.tensor_tensor(hT[:, n % R, :], relu[:, n % R, :], rw[:, n % R, :],
                                          ALU.mult).then_inc(squared, 1)
                    dve.wait_ge(consumed, HC)
                    for t in range(TT):
                        dve.tensor_tensor(x(t), x(t), k.ps[:, t, 0:D], ALU.add).then_inc(added, 1)

                @block.gpsimd
                def _(pool):
                    n1.pool(pool)
                    for n in range(HC):
                        pool.wait_ge(relued, n + 1)
                        pool.wait_ge(spread_copied, expert_of[n] + 1)
                        if n >= R:
                            pool.wait_ge(squared, n - R + 1)
                        pool.tensor_tensor(rw[:, n % R, :], relu[:, n % R, :], wb[:, expert_of[n], :],
                                           ALU.mult).then_inc(weighted, 1)

                @block.scalar
                def _(act):
                    n1.act(act, k.xnT, (4, 5))
                    g_act(act)
                    for e in range(E):
                        act.wait_ge(spread, e + 1)
                        act.copy(wb[:, e, :], k.ps[:, 4 + e % 2, :]).then_inc(spread_copied, 1)
                    for n in range(HC):
                        act.wait_ge(up, n + 1)
                        if n >= R:
                            act.wait_ge(squared, n - R + 1)
                        act.activation(relu[:, n % R, :], k.ps[:, 4 + n % 4, :], ACT.Relu).then_inc(relued, 1)

                @block.tensor
                def _(pe):
                    n1.pe(pe, k.xn, (4, 5))
                    pe.wait_ge(n1.s_ready, KC)
                    g_pe(pe, router)
                    pe.wait_ge(sems[7 + 6], 1)
                    for e in range(E):
                        if e >= 2:
                            pe.wait_ge(spread_copied, e - 1)
                        pe.matmul(k.ps[:, 4 + e % 2, :], sel[:, e, :], combT[:, :], start=True,
                                  stop=True).then_inc(spread, 1)
                    pe.wait_ge(spread_copied, E)

                    def product_down(n):
                        pe.wait_ge(squared, n + 1)
                        for t in range(TT):
                            last = pe.matmul(k.ps[:, t, 0:D], hT[:, n % R, t * P:(t + 1) * P], w2[:, n, :],
                                             start=n == 0, stop=n == HC - 1)
                        last.then_inc(consumed, 1)
                        return last

                    for n in range(HC):
                        if n >= 4:
                            pe.wait_ge(relued, n - 3)
                        for c in range(KC):
                            last = pe.matmul(k.ps[:, 4 + n % 4, :], w1[:, c, n * P:(n + 1) * P], k.xnT[:, c, :],
                                             start=c == 0, stop=c == KC - 1)
                        last.then_inc(up, 1)
                        if n >= 2:
                            product_down(n - 2)
                    product_down(HC - 2)
                    product_down(HC - 1)
                    

def l3_ffn(k):
    nc = k.nc
    HC = E * 512 // P
    R = 4
    with ExitStack() as st:
        router = k.weight("L3_ffn_Wg", st)
        w1 = k.weight("L3_ffn_W1", st)
        w2 = k.weight("L3_ffn_W2", st)
        w3 = k.weight("L3_ffn_W3", st)
        b3 = k.const("L3_ffn_b3", st)
        sel = k.const("select8", st)
        k.load(router, w1, w2, w3, b3, sel)
        b1, b2 = k.vec("L3_ffn_b1"), k.vec("L3_ffn_b2")
        silu = k.sb("silu", [P, R, T], st)
        gv = k.sb("gated", [P, R, T], st)
        hT = k.sb("hidden_T", [P, R, T], st)
        wb = k.sb("expert_weight", [P, 2, T], st)
        with nc.Fori(0, B) as b, signals(
                nc, *norm_names("n_"), *GATE, "spread", "spread_copied", "up_g", "up_v", "silued", "gated",
                "weighted", "consumed", "added") as (*sems, spread, spread_copied, up_g, up_v, silued, gated,
                                                      weighted, consumed, added), ExitStack() as bs:
            n1 = Norm(k, bs, sems[:7], "n", twice=False)
            g_dve, g_act, g_pe, combT, _ = top_two_gate(k, bs, sems[7:], False)
            g_ready = sems[7 + 6]
            x = batch_tiles(k, b)
            with nc.Block() as block:
                @block.vector
                def _(dve):
                    n1.dve(dve, x, k.xn)
                    g_dve(dve)
                    for n in range(HC):
                        dve.wait_ge(up_v, n + 1)
                        dve.wait_ge(silued, n + 1)
                        if n >= R:
                            dve.wait_ge(weighted, n - R + 1)
                        dve.scalar_tensor_tensor(out=gv[:, n % R, :], in0=k.ps[:, 5 + 2 * (n % 2), :],
                                                 scalar=b2[:, n:n + 1], in1=silu[:, n % R, :], op0=ALU.add,
                                                 op1=ALU.mult).then_inc(gated, 1)
                    dve.wait_ge(consumed, HC)
                    for t in range(TT):
                        dve.tensor_tensor(x(t), x(t), k.ps[:, t, 0:D], ALU.add).then_inc(added, 1)

                @block.gpsimd
                def _(pool):
                    n1.pool(pool)
                    for n in range(HC):
                        pool.wait_ge(gated, n + 1)
                        pool.wait_ge(spread_copied, n // 4 + 1)
                        if n >= R:
                            pool.wait_ge(consumed, n - R + 1)
                        pool.tensor_tensor(hT[:, n % R, :], gv[:, n % R, :], wb[:, (n // 4) % 2, :],
                                           ALU.mult).then_inc(weighted, 1)

                @block.scalar
                def _(act):
                    n1.act(act, k.xnT, (4, 5))
                    g_act(act)
                    for n in range(HC):
                        if n % 4 == 0:
                            e = n // 4
                            act.wait_ge(spread, e + 1)
                            if e >= 2:
                                act.wait_ge(weighted, 4 * (e - 1))
                            act.copy(wb[:, e % 2, :], k.ps[:, 7, :]).then_inc(spread_copied, 1)
                        act.wait_ge(up_g, n + 1)
                        if n >= R:
                            act.wait_ge(gated, n - R + 1)
                        act.activation(silu[:, n % R, :], k.ps[:, 4 + 2 * (n % 2), :], ACT.Silu,
                                       bias=b1[:, n:n + 1]).then_inc(silued, 1)

                @block.tensor
                def _(pe):
                    n1.pe(pe, k.xn, (4, 5))
                    pe.wait_ge(n1.s_ready, KC)
                    g_pe(pe, router)
                    pe.wait_ge(g_ready, 1)
                    for t in range(TT):
                        pe.matmul(k.ps[:, t, 0:D], combT[:, t * P:(t + 1) * P], b3[:, :], start=True, stop=False)

                    def product_down(n):
                        pe.wait_ge(weighted, n + 1)
                        for t in range(TT):
                            last = pe.matmul(k.ps[:, t, 0:D], hT[:, n % R, t * P:(t + 1) * P], w3[:, n, :],
                                             start=False, stop=n == HC - 1)
                        last.then_inc(consumed, 1)

                    for n in range(HC):
                        if n >= 2:
                            pe.wait_ge(silued, n - 1)
                            pe.wait_ge(gated, n - 1)
                        if n % 4 == 0:
                            if n:
                                pe.wait_ge(gated, n)
                            pe.matmul(k.ps[:, 7, :], sel[:, n // 4, :], combT[:, :], start=True,
                                      stop=True).then_inc(spread, 1)
                        for bank, w, sem in ((4, w1, up_g), (5, w2, up_v)):
                            bank += 2 * (n % 2)
                            if bank == 7:
                                pe.wait_ge(spread_copied, n // 4 + 1)
                            for c in range(KC):
                                last = pe.matmul(k.ps[:, bank, :], w[:, c, n * P:(n + 1) * P], k.xnT[:, c, :],
                                                 start=c == 0, stop=c == KC - 1)
                            last.then_inc(sem, 1)
                        if n >= 2:
                            product_down(n - 2)
                    product_down(HC - 2)
                    product_down(HC - 1)



STAGES = [None] * 12
STAGES[0] = l0_attn
STAGES[1] = l0_xattn
STAGES[2] = l0_ffn
STAGES[3] = l1_attn
STAGES[5] = l1_ffn
STAGES[9] = l3_attn
STAGES[4] = l1_xattn
STAGES[6] = l2_attn
STAGES[7] = l2_xattn
STAGES[10] = l3_xattn
STAGES[8] = l2_ffn
STAGES[11] = l3_ffn

VECS = ["L1_attn_bq", "L1_attn_bk", "L1_attn_bg", "L1_ffn_bq", "L1_bn_gamma2", "L1_bn_beta2", "L0_xattn_bq", "L0_xattn_bk", "L2_attn_bq", "L2_attn_bk", "L2_scale", "L2_query_gain", "L2_xattn_kn_g2",
        "L3_query_gain", "L3_xattn_k_scale2"] + [
    p + n for p, ns in (("L1_xattn_", ("ln_l_g", "ln_l_b", "ln_m_g", "ln_m_b")),
                        ("L2_xattn_", ("ln_l_g", "ln_l_b", "ln_x_g", "ln_x_b")),
                        ("L3_xattn_", ("ln_l_w", "ln_l_b", "ln_x_w", "ln_x_b"))) for n in ns] + [
        "L0_freq", "L0_decay", "re_im_sign", "half_pi", "L0_attn_n1_g", "L0_attn_n1_b", "L0_attn_n2_g",
        "L0_attn_n2_b", "L0_attn_mlp_b1", "L3_ffn_b1", "L3_ffn_b2",
        "L0_ffn_ln1_g", "L0_ffn_ln1_b", "L0_ffn_ln2_g", "L0_ffn_ln2_b"]
ROWS = ["L1_attn_bv", "L1_attn_bo", "L1_attn_gamma", "L1_attn_beta", "L3_attn_b_o", "L0_xattn_bv", "L0_xattn_bo", "L2_attn_bv", "L2_attn_bo", "L2_xattn_bout", "L3_xattn_ln_o_w",
        "L3_xattn_ln_o_b", "L0_attn_gate_b", "L0_attn_mlp_b2", "L0_ffn_b1", "L0_ffn_b2"]
WEIGHTS = {"L0_ffn_w1": "T", "L0_ffn_w2": "T", "L2_ffn_router_w": "T", "L2_ffn_w1": "", "L2_ffn_w2": "",
           "L0_in": "", "L0_attn_out_proj_w": "T", "L0_coupling": "", "L0_attn_gate_w": "T",
           "L0_attn_mlp_w1": "T", "L0_attn_mlp_w2": "T", "L3_ffn_Wg": "T", "L3_ffn_W1": "T", "L3_ffn_W2": "T",
           "L3_ffn_W3": "", "L1_ffn_Wq": "", "L1_ffn_expert_down": "T", "L1_ffn_expert_up": "", "L1_sub_keys": "",
           **{"L1_attn_" + n: "" for n in ("Wq", "Wk", "Wv", "Wg", "Wo")},
           **{"L3_attn_" + n: "T" for n in ("w_q", "w_k", "w_v", "w_o")},
           "ctx_T": "", "L0_side": "", "mask_bf1": "", "mask_bk0": "",
           **{"L0_xattn_" + n: "" for n in ("wq", "wk", "wv", "wo")},
           **{"L2_attn_" + n: "T" for n in ("Wq", "Wk", "Wv", "Wo")},
           **{p + n: "" for p, o in (("L1_xattn_", "Wout"), ("L2_xattn_", "Wout"), ("L3_xattn_", "Wo"))
              for n in ("Wq", "Wkv", o)}}


def program(nc, dram, slots_v, slots_r):
    with ExitStack() as ctx:
        k = Core(nc, ctx, dram)
        k.slots_v, k.slots_r = slots_v, slots_r
        with signals(nc, "in_loaded", "consts_set") as (loaded, consts), nc.Block() as block:
            @block.sync
            def _(sp):
                sp.dma_start(k.x[:, :, :], dram["x"]).then_inc(loaded, 16)
                sp.dma_start(k.vecs[:, :], dram["vecs"]).then_inc(loaded, 16)
                sp.dma_start(k.rows[:, :], dram["rows"]).then_inc(loaded, 16)
                sp.dma_start(k.ident[:, :], dram["ident"]).then_inc(loaded, 16)
                sp.wait_ge(loaded, 64)

            @block.gpsimd
            def _(pool):
                pool.memset(k.ones[:, :], 1.0).then_inc(consts, 1)
                pool.memset(k.half[:, :], -0.5).then_inc(consts, 1)
                pool.wait_ge(consts, 2)

        with signals(nc, "folded") as (folded,), nc.Block() as block:
            @block.vector
            def _(dve):
                for name, c in (("L2_query_gain", 64 ** -0.5), ("L3_query_gain", 8.0)):
                    dve.tensor_scalar(k.vec(name), k.vec(name), c, None, ALU.mult).then_inc(folded, 1)

        for stage in STAGES[FIRST:LAST]:
            stage(k)

        with signals(nc, "out_stored") as (stored,), nc.Block() as block:
            @block.sync
            def _(sp):
                sp.dma_start(dram["out"], k.x[:, :, :]).then_inc(stored, 16)
                sp.wait_ge(stored, 16)


def words_of_bools(m):
    return np.broadcast_to(np.repeat(m.view(np.uint8).reshape(1, -1), 4, axis=1).view(np.int32), (P, m.size))


def lay_out(a, arrays):
    f = np.float32
    w = a["L0_attn_in_proj_w"].T
    a["L0_in"] = np.concatenate([w, w[:, 64:], w[:, :64]], axis=1)
    a["L0_freq"] = np.concatenate([a["L0_attn_frequency"]] * 2)
    a["L0_decay"] = np.concatenate([a["L0_attn_log_decay"]] * 2)
    a["re_im_sign"] = np.repeat(np.array([1, -1], f), 64)
    a["half_pi"] = np.full((P,), np.pi / 2, f)
    cp = np.zeros((P, 2 * P), f)
    for ri in range(2):
        for h in range(4):
            i = 64 * ri + 16 * h
            cp[i:i + 16, i:i + 16] = a["L0_attn_coupling"][h]
            j = P + 64 * (1 - ri) + 16 * h
            cp[i:i + 16, j:j + 16] = a["L0_attn_coupling"][h]
    a["L0_coupling"] = cp
    ctx = a["ctx_1024"]
    a["ctx_T"] = ctx.reshape(-1, D).T
    arrays["ctx_rows"] = np.ascontiguousarray(ctx.transpose(1, 0, 2))
    a["L0_side"] = np.broadcast_to(a["fside_BxS2_0"].reshape(1, -1), (P, B * 64))
    a["mask_bf1"] = words_of_bools(a["mask_BxS2_bf1"])
    a["mask_bk0"] = words_of_bools(a["mask_BxS2_bk0"])
    arrays["head_mask8"] = np.repeat(np.eye(8, dtype=f), 16, axis=0)
    q, c = np.arange(P)[:, None], np.arange(P)[None, :]
    hidden = (q // 64 > c // 64) | ((q // 64 == c // 64) & (c > q))
    arrays["block_mask"] = np.where(hidden, f(-1e30), f(0))
    a["L2_scale"] = np.broadcast_to(a["L2_attn_attn_scale"], (P,))
    a["L2_query_gain"] = np.tile(a["L2_xattn_qn_g"], 2)
    a["L2_xattn_kn_g2"] = np.tile(a["L2_xattn_kn_g"], 2)
    a["L3_query_gain"] = np.tile(a["L3_xattn_q_scale"], 2)
    a["L3_xattn_k_scale2"] = np.tile(a["L3_xattn_k_scale"], 2)
    arrays["chunk_diagonal"] = np.eye(T // 16, dtype=f)
    arrays["pair_mean"] = np.tile(np.eye(64, dtype=f) * f(0.5), (2, 2))
    arrays["group_of_32"] = np.repeat(np.eye(4, dtype=f), 32, axis=0)
    sk = np.zeros((P, P), f)
    for i in range(4):
        sk[32 * i:32 * i + 32, 32 * i:32 * i + 32] = a["L1_ffn_sub_key%d" % (i % 2)].T
    a["L1_sub_keys"] = sk
    a["L1_bn_gamma2"] = np.tile(a["L1_ffn_bn_gamma"], 2)
    a["L1_bn_beta2"] = np.tile(a["L1_ffn_bn_beta"], 2)
    for n in ("rel_k", "rel_v"):
        rel = np.tile(a["L3_attn_" + n][128 - 3:128 + 4][::-1], (1, 16))
        arrays[n + "_rows"] = np.ascontiguousarray(np.broadcast_to(rel[None], (P, 7, D)))
    arrays["counting"] = np.ascontiguousarray(np.broadcast_to(np.arange(T, dtype=f)[None], (P, T)))
    arrays["select8"] = np.ascontiguousarray(np.repeat(np.eye(E, dtype=f)[:, :, None], P, axis=2))
    for n in ("L3_ffn_W1", "L3_ffn_W2"):
        a[n] = a[n].reshape(-1, D)
    a["L3_ffn_W3"] = a["L3_ffn_W3"].transpose(0, 2, 1).reshape(-1, D)
    arrays["L3_ffn_b3"] = a["L3_ffn_b3"]


def kernel(**inputs):
    import concourse.bacc as _bacc
    from concourse.bass_utils import run_bass_kernel_spmd as _run

    nc = _bacc.Bacc("TRN2", target_bir_lowering=False, num_devices=1)
    a = {n: np.asarray(v) for n, v in inputs.items()}
    arrays = {"x": np.ascontiguousarray(a["x"].reshape(NT, P, D).transpose(1, 0, 2))}
    lay_out(a, arrays)
    slots_v, slots_r, at = {}, {}, 0
    for n in VECS:
        slots_v[n] = (at, at + a[n].size // P)
        at += a[n].size // P
    arrays["vecs"] = np.ascontiguousarray(np.concatenate([a[n].reshape(-1, P).T for n in VECS], axis=1))
    at = 0
    for n in ROWS:
        slots_r[n] = (at, at + a[n].size)
        at += a[n].size
    arrays["rows"] = np.ascontiguousarray(
        np.broadcast_to(np.concatenate([a[n].reshape(-1) for n in ROWS])[None, :], (P, at)))
    arrays["ident"] = np.eye(P, dtype=np.float32)
    for n, how in WEIGHTS.items():
        w = a[n].T if how == "T" else a[n]
        arrays[n] = np.ascontiguousarray(w.reshape(w.shape[0] // P, P, w.shape[1]).transpose(1, 0, 2))
    dram = {n: nc.dram_tensor("in_" + n, v.shape, mybir.dt.from_np(v.dtype), kind="ExternalInput").ap()
            for n, v in arrays.items()}
    dram["out"] = nc.dram_tensor("out_x", (P, NT, D), F32, kind="ExternalOutput").ap()
    program(nc, dram, slots_v, slots_r)
    r = _run(nc, [{"in_" + n: v for n, v in arrays.items()}], core_ids=[0])
    out = np.asarray(r.results[0]["out_x"])
    return out.transpose(1, 0, 2).reshape(B, T, D)
```

```python
from contextlib import ExitStack, contextmanager

import numpy as np

import concourse.bass as bass
from concourse import mybir

F32 = mybir.dt.float32
ALU = mybir.AluOpType
ACT = mybir.ActivationFunctionType
AX = mybir.AxisListType

P = 128
D = 256
KC = D // P
B = 4
T = 512
TT = T // P
NT = B * TT
EPS = 1e-5
FIRST, LAST = 0, 12


@contextmanager
def signals(nc, *names):
    with ExitStack() as st:
        sems = [st.enter_context(nc.semaphore(n)) for n in names]
        yield sems
        for s in sems:
            nc.gpsimd.sem_clear(s)
        nc.all_engine_barrier()


class Order:

    def __init__(self, eng, sem):
        self.eng, self.sem, self.n = eng, sem, 0

    def mark(self, ins):
        self.n += 1
        ins.then_inc(self.sem, 1)
        return self.n

    def wait(self):
        if self.n:
            self.eng.wait_ge(self.sem, self.n)

    def do(self, ins):
        self.mark(ins)
        self.wait()


class Core:

    def __init__(self, nc, ctx, dram):
        self.nc, self.ctx, self.dram = nc, ctx, dram
        self.used = {}
        self.weights_loaded = [ctx.enter_context(nc.semaphore(n)) for n in ("weights_loaded", "late_weights_loaded")]
        self.loads = [0, 0]
        sb = self.sb
        self.x = sb("x_res", [P, NT, D])
        self.ident = sb("ident", [P, P])
        self.ones = sb("ones", [P, P])
        self.half = sb("neg_half", [P, 64])
        self.xn = sb("x_normed", [P, TT, D])
        self.xnT = sb("x_normed_T", [P, KC, T])
        self.vecs = sb("feature_vectors", [P, dram["vecs"].shape[1]])
        self.rows = sb("row_vectors", [P, dram["rows"].shape[1]])
        self.ps = ctx.enter_context(nc.psum_tensor("psum_banks", [P, 8, 512], F32))

    def vec(self, n):
        return self.vecs[:, self.slots_v[n][0]:self.slots_v[n][1]]

    def row(self, n):
        return self.rows[:, self.slots_r[n][0]:self.slots_r[n][1]]

    def weight(self, name, ctx):
        src = self.dram[name]
        return Loaded(self.sb("w_" + name, list(src.shape), ctx, src.dtype), src)

    const = weight

    def load(self, sp, what, late=False):
        for w in what:
            whole = tuple(slice(None) for _ in w.src.shape)
            sp.dma_start(w.dst[whole], w.src[whole]).then_inc(self.weights_loaded[late], 16)
            self.loads[late] += 1

    def wait_weights(self, sp, late=False):
        sp.wait_ge(self.weights_loaded[late], 16 * self.loads[late])

    def sb(self, name, shape, ctx=None, dtype=F32):
        self.used[name] = n = self.used.get(name, 0) + 1
        name = name if n == 1 else f"{name}_{n}"
        return (ctx or self.ctx).enter_context(self.nc.sbuf_tensor(name, shape, dtype))


class Loaded:

    def __init__(self, dst, src):
        self.dst, self.src = dst, src

    def __getitem__(self, i):
        return self.dst[i]


class Norm:

    NAMES = ("stats", "aggr", "rstd", "normed", "turned", "ready", "pool_order")

    def __init__(self, k, ctx, sems, name, twice=True, gain=None, offset=None, tiles=TT, rows=P, eps=EPS, eps2=EPS):
        (self.s_stats, self.s_aggr, self.s_rstd, self.s_normed, self.s_turned, self.s_ready, self.s_pool) = sems
        self.k, self.twice, self.gain, self.offset, self.tiles, self.rows = k, twice, gain, offset, tiles, rows
        self.eps, self.eps2 = eps, eps2
        self.stat = k.sb(name + "_stat", [P, tiles, 6], ctx)
        self.mv = k.sb(name + "_mv", [P, tiles, 2], ctx)
        self.rs = k.sb(name + "_rstd", [P, 4, tiles], ctx)

    def dve(self, dve, src, dst):
        r = self.rows
        for t in range(self.tiles):
            dve.bn_stats(self.stat[0:r, t, :], src(t)).then_inc(self.s_stats, 1)
        dve.wait_ge(self.s_stats, self.tiles)
        for t in range(self.tiles):
            dve.bn_aggr(self.mv[0:r, t, :], self.stat[0:r, t, :]).then_inc(self.s_aggr, 1)
        dve.wait_ge(self.s_aggr, self.tiles)
        dve.wait_ge(self.s_rstd, 1)
        for t in range(self.tiles):
            dve.tensor_scalar(dst[0:r, t, :], src(t), self.mv[0:r, t, 0:1], self.rs[0:r, 3, t:t + 1],
                              ALU.subtract, ALU.mult).then_inc(self.s_normed, 1)

    def pool(self, pool):
        k, r, n = self.k, self.rows, self.tiles
        rs, var = self.rs, self.mv[0:r, :, 1]
        o = Order(pool, self.s_pool)
        pool.wait_ge(self.s_aggr, n)
        o.do(pool.tensor_scalar(rs[0:r, 0, :], var, self.eps, 1.0, ALU.add, ALU.mult))
        if not self.twice:
            pool.tensor_tensor(rs[0:r, 3, :], rs[0:r, 0, :], k.half[0:r, 0:n], ALU.pow).then_inc(self.s_rstd, 1)
            return
        o.do(pool.tensor_tensor(rs[0:r, 1, :], rs[0:r, 0, :], k.half[0:r, 0:n], ALU.pow))
        o.do(pool.tensor_tensor(rs[0:r, 2, :], rs[0:r, 1, :], rs[0:r, 1, :], ALU.mult))
        o.do(pool.tensor_tensor(rs[0:r, 2, :], rs[0:r, 2, :], var, ALU.mult))
        o.do(pool.tensor_scalar(rs[0:r, 2, :], rs[0:r, 2, :], self.eps2, 1.0, ALU.add, ALU.mult))
        o.do(pool.tensor_tensor(rs[0:r, 2, :], rs[0:r, 2, :], k.half[0:r, 0:n], ALU.pow))
        pool.tensor_tensor(rs[0:r, 3, :], rs[0:r, 2, :], rs[0:r, 1, :], ALU.mult).then_inc(self.s_rstd, 1)

    def pe(self, pe, src, banks, chunks=KC):
        k, r = self.k, self.rows
        pe.wait_ge(self.s_normed, self.tiles)
        for c in range(chunks):
            for t in range(self.tiles):
                last = pe.transpose(k.ps[:, banks[c], t * r:(t + 1) * r], src[0:r, t, c * P:(c + 1) * P],
                                    k.ident[0:r, 0:r])
            last.then_inc(self.s_turned, 1)

    def act(self, act, dst, banks, chunks=KC):
        k, n = self.k, self.rows * self.tiles
        for c in range(chunks):
            act.wait_ge(self.s_turned, c + 1)
            if self.gain is None:
                act.copy(dst[:, c, 0:n], k.ps[:, banks[c], 0:n]).then_inc(self.s_ready, 1)
            else:
                act.activation(dst[:, c, 0:n], k.ps[:, banks[c], 0:n], ACT.Identity,
                               bias=self.offset[:, c:c + 1], scale=self.gain[:, c:c + 1]).then_inc(self.s_ready, 1)


def norm_names(p):
    return [p + n for n in Norm.NAMES]


def batch_tiles(k, b, of=None):
    v = (k.x if of is None else of)[:, :, :].rearrange("p (b t) d -> p b t d", b=B)
    return lambda t: v[:, bass.ds(b, 1), t, :].rearrange("p o d -> p (o d)")


def norm_all(k, st, twice=True, gain=None, offset=None, rows=None, once=None, load=(), later=()):
    nc = k.nc
    xT = k.sb("batches_normed_T", [P, KC, B * T], st)
    with ExitStack() as ts, signals(nc, "stats", "aggregated", "pool_order", "rstd", "normed", "turned",
                                    "ready", "once_made") as (
            stats, aggregated, pool_order, rstd, normed, turned, ready, once_made):
        rows = k.sb("batches_normed", [P, NT, D], ts) if rows is None else rows
        stat = k.sb("norm_stat", [P, NT, 6], ts)
        mv = k.sb("norm_mv", [P, NT, 2], ts)
        rs = k.sb("norm_rstd", [P, 4, NT], ts)
        with nc.Block() as block:
            @block.sync
            def _(sp):
                k.load(sp, load)
                k.load(sp, later, late=True)
                k.wait_weights(sp)

            @block.vector
            def _(dve):
                for g in range(B + 1):
                    if g < B:
                        for t in range(TT * g, TT * g + TT):
                            dve.bn_stats(stat[:, t, :], k.x[:, t, :]).then_inc(stats, 1)
                        dve.wait_ge(stats, TT * (g + 1))
                        for t in range(TT * g, TT * g + TT):
                            dve.bn_aggr(mv[:, t, :], stat[:, t, :]).then_inc(aggregated, 1)
                    if g >= 1:
                        dve.wait_ge(aggregated, TT * g)
                        dve.wait_ge(rstd, g)
                        for t in range(TT * g - TT, TT * g):
                            dve.tensor_scalar(rows[:, t, :], k.x[:, t, :], mv[:, t, 0:1], rs[:, 2, t:t + 1],
                                              ALU.subtract, ALU.mult).then_inc(normed, 1)
                if once is not None:
                    for t in range(NT):
                        if t % TT == 0:
                            dve.wait_ge(rstd, B + t // TT + 1)
                        dve.tensor_scalar(once[:, t, :], k.x[:, t, :], mv[:, t, 0:1], rs[:, 1, t:t + 1],
                                          ALU.subtract, ALU.mult).then_inc(once_made, 1)

            @block.gpsimd
            def _(pool):
                o = Order(pool, pool_order)
                for g in range(B):
                    n = slice(TT * g, TT * g + TT)
                    half = k.half[:, 0:TT]
                    pool.wait_ge(aggregated, TT * (g + 1))
                    if twice:
                        o.do(pool.tensor_scalar(rs[:, 0, n], mv[:, n, 1], 1.0 + EPS, EPS * EPS, ALU.mult, ALU.add))
                    else:
                        o.do(pool.tensor_scalar(rs[:, 0, n], mv[:, n, 1], EPS, 1.0, ALU.add, ALU.mult))
                    pool.tensor_tensor(rs[:, 2, n], rs[:, 0, n], half, ALU.pow).then_inc(rstd, 1)
                if once is not None:
                    for g in range(B):
                        n = slice(TT * g, TT * g + TT)
                        o.do(pool.tensor_scalar(rs[:, 3, n], mv[:, n, 1], EPS, 1.0, ALU.add, ALU.mult))
                        pool.tensor_tensor(rs[:, 1, n], rs[:, 3, n], half, ALU.pow).then_inc(rstd, 1)

            @block.tensor
            def _(pe):
                for g in range(B):
                    pe.wait_ge(normed, TT * (g + 1))
                    for c in range(KC):
                        for t in range(TT):
                            last = pe.transpose(k.ps[:, KC * g + c, t * P:(t + 1) * P],
                                                rows[:, TT * g + t, c * P:(c + 1) * P], k.ident[:, :])
                        last.then_inc(turned, 1)

            @block.scalar
            def _(act):
                for g in range(B):
                    for c in range(KC):
                        act.wait_ge(turned, KC * g + c + 1)
                        dst, src = xT[:, c, g * T:(g + 1) * T], k.ps[:, KC * g + c, :]
                        if gain is None:
                            act.copy(dst, src).then_inc(ready, 1)
                        else:
                            act.activation(dst, src, ACT.Identity, bias=offset[:, c:c + 1],
                                           scale=gain[:, c:c + 1]).then_inc(ready, 1)
                act.wait_ge(ready, B * KC)
    return xT


def pick_batch(dve, xT, b, dst, sem):
    for c in range(KC):
        dve.tensor_copy(dst[:, c, 0:T], xT[:, c, bass.ds(b * T, T)]).then_inc(sem, 1)



def l0_ffn(k):
    nc = k.nc
    HID = 1024
    HC = HID // P
    with ExitStack() as st:
        w1, w2 = k.weight("L0_ffn_w1", st), k.weight("L0_ffn_w2", st)
        xT = norm_all(k, st, gain=k.vec("L0_ffn_ln1_g"), offset=k.vec("L0_ffn_ln1_b"), load=(w1, w2))
        h = k.sb("hidden", [P, TT, HID], st)
        hT = k.sb("hidden_T", [P, HC, T], st)
        asum = k.sb("abs_sum", [P, 2], st)
        scal = k.sb("quant_scale", [P, 2, 2], st)
        sems = norm_names("ffn2_")
        with signals(nc, "abs_summed", "summed", "scaled", "quantised") as \
                (abs_summed, summed, scaled, quantised), nc.Block() as block:
            @block.vector
            def _(dve):
                o = Order(dve, quantised)
                for i, w in enumerate((w1, w2)):
                    dve.tensor_reduce(asum[:, i:i + 1], w[:, :, :], AX.XY, ALU.add,
                                      apply_absolute_value=True).then_inc(abs_summed, 1)
                dve.wait_ge(summed, 1)
                o.do(dve.tensor_scalar(scal[:, :, 1], k.ps[:, 0, 0:2], 1.0 / (HID * D), 1e-5, ALU.mult, ALU.max))
                o.do(dve.reciprocal(scal[:, :, 0], scal[:, :, 1]))
                for i, w in enumerate((w1, w2)):
                    o.do(dve.tensor_scalar(w[:, :, :], w[:, :, :], scal[:, i, 0:1], 1.0, ALU.mult, ALU.min))
                    o.do(dve.tensor_scalar(w[:, :, :], w[:, :, :], -1.0, 12582912.0, ALU.max, ALU.add))
                    o.do(dve.tensor_scalar(w[:, :, :], w[:, :, :], -12582912.0, scal[:, i, 1:2], ALU.add, ALU.mult))

            @block.tensor
            def _(pe):
                pe.wait_ge(abs_summed, 2)
                pe.matmul(k.ps[:, 0, 0:2], k.ones[:, :], asum[:, :], start=True, stop=True).then_inc(summed, 1)

        with nc.Fori(0, B) as b, signals(nc, *sems, "dve_ready", "batch_picked", "up", "biased", "gelued", "down", "added",
                                         "freed") as \
                (s_stats, s_aggr, s_rstd, s_normed, s_turned, s_ready, s_pool, dve_ready, batch_picked, up, biased, gelued,
                 down, added, freed), ExitStack() as bs:
            stat = k.sb("hid_stat", [P, TT, 2, 6], bs)
            mv = k.sb("hid_mv", [P, TT, 2], bs)
            rs = k.sb("hid_rstd", [P, 2, TT], bs)
            x = batch_tiles(k, b)
            g2, b2 = k.vec("L0_ffn_ln2_g"), k.vec("L0_ffn_ln2_b")
            b1r, b2r = k.row("L0_ffn_b1"), k.row("L0_ffn_b2")
            with nc.Block() as block:
                @block.vector
                def _(dve):
                    pick_batch(dve, xT, b, k.xnT, batch_picked)
                    for i in range(TT + 2):
                        if i < TT:
                            dve.wait_ge(up, i + 1)
                            s0 = 2 * (i % 2)
                            dve.tensor_tensor(h[:, i, :].rearrange("p (a n) -> p a n", a=2), k.ps[:, s0:s0 + 2, :],
                                              b1r.rearrange("p (a n) -> p a n", a=2), ALU.add).then_inc(biased, 1)
                        if 1 <= i < TT + 1:
                            t = i - 1
                            dve.wait_ge(gelued, t + 1)
                            for a in range(2):
                                dve.bn_stats(stat[:, t, a, :], h[:, t, a * 512:(a + 1) * 512]).then_inc(s_stats, 1)
                            dve.wait_ge(s_stats, 2 * (t + 1))
                            dve.bn_aggr(mv[:, t, :], stat[:, t, :, :].rearrange("p a s -> p (a s)"))\
                                .then_inc(s_aggr, 1)
                        if i >= 2:
                            t = i - 2
                            dve.wait_ge(s_rstd, t + 1)
                            dve.tensor_scalar(h[:, t, :], h[:, t, :], mv[:, t, 0:1], rs[:, 1, t:t + 1],
                                              ALU.subtract, ALU.mult).then_inc(s_normed, 1)
                    for c in range(1, HC, 2):
                        dve.wait_ge(s_turned, c + 1)
                        dve.tensor_scalar(hT[:, c, :], k.ps[:, c % 4, :], g2[:, c:c + 1], b2[:, c:c + 1],
                                          ALU.mult, ALU.add).then_inc(dve_ready, 1)
                    o = Order(dve, freed)
                    for t in range(TT):
                        dve.wait_ge(down, t + 1)
                        o.do(dve.tensor_tensor(k.xn[:, t, :], k.ps[:, 4 + t % 2, 0:D], b2r, ALU.add))
                        dve.tensor_tensor(x(t), x(t), k.xn[:, t, :], ALU.add).then_inc(added, 1)

                @block.gpsimd
                def _(pool):
                    o = Order(pool, s_pool)
                    for t in range(TT):
                        pool.wait_ge(s_aggr, t + 1)
                        o.do(pool.tensor_scalar(rs[:, 0, t:t + 1], mv[:, t, 1:2], EPS, 1.0, ALU.add, ALU.mult))
                        pool.tensor_tensor(rs[:, 1, t:t + 1], rs[:, 0, t:t + 1], k.half[:, 0:1],
                                           ALU.pow).then_inc(s_rstd, 1)

                @block.scalar
                def _(act):
                    for t in range(TT):
                        act.wait_ge(biased, t + 1)
                        act.activation(h[:, t, :], h[:, t, :], ACT.Gelu).then_inc(gelued, 1)
                    for c in range(0, HC, 2):
                        act.wait_ge(s_turned, c + 1)
                        act.activation(hT[:, c, :], k.ps[:, c % 4, :], ACT.Identity, bias=b2[:, c:c + 1],
                                       scale=g2[:, c:c + 1]).then_inc(s_ready, 1)

                @block.tensor
                def _(pe):
                    pe.wait_ge(batch_picked, KC)
                    for t in range(TT):
                        if t >= 2:
                            pe.wait_ge(biased, t - 1)
                        for a in range(2):
                            for c in range(KC):
                                last = pe.matmul(k.ps[:, 2 * (t % 2) + a, :], k.xnT[:, c, t * P:(t + 1) * P],
                                                 w1[:, c, a * 512:(a + 1) * 512], start=c == 0, stop=c == KC - 1)
                        last.then_inc(up, 1)
                    pe.wait_ge(s_normed, TT)
                    for c in range(HC):
                        if c >= 4:
                            pe.wait_ge(dve_ready if c % 2 else s_ready, (c - 4) // 2 + 1)
                        for t in range(TT):
                            last = pe.transpose(k.ps[:, c % 4, t * P:(t + 1) * P], h[:, t, c * P:(c + 1) * P],
                                                k.ident[:, :])
                        last.then_inc(s_turned, 1)
                    pe.wait_ge(s_ready, HC // 2)
                    pe.wait_ge(dve_ready, HC // 2)
                    for t in range(TT):
                        if t >= 2:
                            pe.wait_ge(freed, t - 1)
                        for c in range(HC):
                            last = pe.matmul(k.ps[:, 4 + t % 2, 0:D], hT[:, c, t * P:(t + 1) * P], w2[:, c, :],
                                             start=c == 0, stop=c == HC - 1)
                        last.then_inc(down, 1)


BIG = 3.0e38


def l0_attn(k):
    nc = k.nc
    HC = 1024 // P
    TWO_PI_HI = 6.28125
    TWO_PI_LO = 2 * np.pi - TWO_PI_HI
    MAGIC = 12582912.0
    with ExitStack() as st:
        w_in = k.weight("L0_in", st)
        w_out = k.weight("L0_attn_out_proj_w", st)
        coup = k.weight("L0_coupling", st)
        gate = k.weight("L0_attn_gate_w", st)
        w1 = k.weight("L0_attn_mlp_w1", st)
        w2 = k.weight("L0_attn_mlp_w2", st)
        count = k.const("counting", st)
        once = k.sb("batches_normed_once", [P, NT, D], st)
        xT = norm_all(k, st, gain=k.vec("L0_attn_n1_g"), offset=k.vec("L0_attn_n1_b"), once=once,
                      load=(w_in, w_out, coup, gate, w1, w2, count))
        mag = k.sb("magnitude", [P, T], st)
        cos = k.sb("cosine", [P, T], st)
        sin = k.sb("signed_sine", [P, T], st)
        m = k.sb("out_weights", [P, 2, D], st)
        with signals(nc, "rot_order", "reduced", "angles", "magged", "coupled", "out_ready") as \
                (order, reduced, angles, magged, coupled, out_ready), ExitStack() as ts, nc.Block() as block:
            ph = k.sb("phase", [P, T], ts)
            turns = k.sb("turns", [P, T], ts)
            mcol = k.sb("mag_col", [P, 1], ts)

            @block.vector
            def _(dve):
                o = Order(dve, order)
                o.do(dve.tensor_scalar(ph[:, :], count[:, :], k.vec("L0_freq")[:, 0:1], None, ALU.mult))
                o.do(dve.tensor_scalar(turns[:, :], ph[:, :], 1 / (2 * np.pi), MAGIC, ALU.mult, ALU.add))
                o.do(dve.tensor_scalar(turns[:, :], turns[:, :], -MAGIC, None, ALU.add))
                o.do(dve.scalar_tensor_tensor(out=ph[:, :], in0=turns[:, :], scalar=-TWO_PI_HI, in1=ph[:, :],
                                              op0=ALU.mult, op1=ALU.add))
                o.do(dve.scalar_tensor_tensor(out=ph[:, :], in0=turns[:, :], scalar=-TWO_PI_LO, in1=ph[:, :],
                                              op0=ALU.mult, op1=ALU.add))
                dve.tensor_scalar(ph[:, :], ph[:, :], 3.141592, -3.141592, ALU.min, ALU.max).then_inc(reduced, 1)
                dve.wait_ge(magged, 1)
                o.mark(dve.tensor_scalar(mag[:, :], k.ones[:, 0:1].to_broadcast([P, T]), mcol[:, 0:1], None,
                                         ALU.mult))
                dve.wait_ge(angles, 2)
                o.mark(dve.tensor_scalar(sin[:, :], sin[:, :], k.vec("re_im_sign")[:, 0:1], None, ALU.mult))
                for i in range(2):
                    dve.wait_ge(coupled, i + 1)
                    dve.tensor_copy(m[:, i, :], k.ps[:, i, 0:D]).then_inc(out_ready, 1)

            @block.scalar
            def _(act):
                act.activation(mcol[:, :], k.vec("L0_decay")[:, 0:1], ACT.Sigmoid).then_inc(magged, 1)
                act.wait_ge(reduced, 1)
                act.activation(sin[:, :], ph[:, :], ACT.Sin).then_inc(angles, 1)
                act.activation(turns[:, :], ph[:, :], ACT.Abs).then_inc(angles, 1)
                act.wait_ge(angles, 2)
                act.activation(cos[:, :], turns[:, :], ACT.Sin, bias=k.vec("half_pi")[:, 0:1],
                               scale=-1.0).then_inc(angles, 1)

            @block.tensor
            def _(pe):
                for i in range(2):
                    pe.matmul(k.ps[:, i, 0:D], coup[:, 0, i * P:(i + 1) * P], w_out[:, 0, :], start=True,
                              stop=True).then_inc(coupled, 1)

        xin = k.sb("x_in", [P, TT, D], st)
        x2 = k.sb("x_mid_normed", [P, TT, D], st)
        x2T = k.sb("x_mid_T", [P, KC, T], st)
        beta = k.sb("beta_turned", [P, 4, T], st)
        gt = k.sb("gate_value", [P, TT, D], st)
        hT = k.sb("hidden_T", [P, HC, T], st)
        with nc.Fori(0, B) as b, signals(
                nc, *norm_names("m_"), "batch_picked", "beta_made", "rot_order", "scanned", "gate_made",
                "gate_biased", "gate_open", "outed", "midded", "up", "silued", "down", "biased", "added") as (
                *sems, batch_picked, beta_made, order, scanned, gate_made, gate_biased, gate_open, outed, midded, up,
                silued, down, biased, added), ExitStack() as bs:
            n2 = Norm(k, bs, sems, "m", twice=False, gain=k.vec("L0_attn_n2_g"), offset=k.vec("L0_attn_n2_b"))
            b1, b2r, gbr = k.vec("L0_attn_mlp_b1"), k.row("L0_attn_mlp_b2"), k.row("L0_attn_gate_b")
            x, x_once = batch_tiles(k, b), batch_tiles(k, b, once)
            with nc.Block() as block:
                @block.vector
                def _(dve):
                    pick_batch(dve, xT, b, k.xnT, batch_picked)
                    o = Order(dve, order)
                    dve.wait_ge(beta_made, 2)
                    o.mark(dve.tensor_tensor(beta[:, 0, :], k.ps[:, 0, :], cos[:, :], ALU.mult))
                    o.do(dve.tensor_tensor(beta[:, 1, :], k.ps[:, 1, :], sin[:, :], ALU.mult))
                    o.do(dve.tensor_tensor(beta[:, 0, :], beta[:, 0, :], beta[:, 1, :], ALU.add))
                    o.do(dve.tensor_tensor_scan(beta[:, 1, :], mag[:, :], beta[:, 0, :], 0.0, ALU.mult, ALU.add))
                    dve.tensor_tensor(beta[:, 2, :], beta[:, 1, :], cos[:, :], ALU.mult).then_inc(scanned, 1)
                    dve.tensor_tensor(beta[:, 3, :], beta[:, 1, :], sin[:, :], ALU.mult).then_inc(scanned, 1)
                    for t in range(TT):
                        dve.wait_ge(gate_made, 2 * (t // 2) + 2)
                        dve.tensor_tensor(gt[:, t, :], k.ps[:, 2 + t // 2, (t % 2) * D:(t % 2 + 1) * D], gbr,
                                          ALU.add).then_inc(gate_biased, 1)
                    for t in range(TT):
                        dve.wait_ge(gate_open, t + 1)
                        dve.wait_ge(outed, 2 * (t // 2) + 2)
                        o.do(dve.tensor_tensor(gt[:, t, :], gt[:, t, :],
                                               k.ps[:, 4 + t // 2, (t % 2) * D:(t % 2 + 1) * D], ALU.mult))
                        o.mark(dve.tensor_tensor(xin[:, t, :], x_once(t), gt[:, t, :], ALU.add))
                    o.wait()
                    n2.dve(dve, lambda t: xin[:, t, :], x2)
                    for t in range(TT):
                        dve.tensor_tensor(xin[:, t, :], xin[:, t, :], b2r, ALU.add).then_inc(biased, 1)
                    dve.wait_ge(biased, TT)
                    for t in range(TT):
                        dve.tensor_tensor(x(t), x(t), xin[:, t, :], ALU.add).then_inc(biased, 1)
                    for t in range(TT):
                        dve.wait_ge(down, 2 * (t // 2) + 2)
                        dve.wait_ge(biased, TT + t + 1)
                        dve.tensor_tensor(x(t), x(t), k.ps[:, t // 2, (t % 2) * D:(t % 2 + 1) * D],
                                          ALU.add).then_inc(added, 1)

                @block.gpsimd
                def _(pool):
                    n2.pool(pool)

                @block.scalar
                def _(act):
                    for t in range(TT):
                        act.wait_ge(gate_biased, t + 1)
                        act.activation(gt[:, t, :], gt[:, t, :], ACT.Sigmoid).then_inc(gate_open, 1)
                    n2.act(act, x2T, (6, 7))
                    for c in range(HC):
                        act.wait_ge(up, c + 1)
                        act.activation(hT[:, c, :], k.ps[:, 2 + c % 4, :], ACT.Silu,
                                       bias=b1[:, c:c + 1]).then_inc(silued, 1)

                @block.tensor
                def _(pe):
                    pe.wait_ge(batch_picked, KC)
                    for i in range(2):
                        for c in range(KC):
                            last = pe.matmul(k.ps[:, i, :], w_in[:, c, i * P:(i + 1) * P], k.xnT[:, c, :],
                                             start=c == 0, stop=c == KC - 1)
                        last.then_inc(beta_made, 1)
                    for t in range(TT):
                        for c in range(KC):
                            last = pe.matmul(k.ps[:, 2 + t // 2, (t % 2) * D:(t % 2 + 1) * D],
                                             k.xnT[:, c, t * P:(t + 1) * P], gate[:, c, :],
                                             start=c == 0, stop=c == KC - 1)
                        last.then_inc(gate_made, 1)
                    pe.wait_ge(scanned, 2)
                    for t in range(TT):
                        for i in range(2):
                            last = pe.matmul(k.ps[:, 4 + t // 2, (t % 2) * D:(t % 2 + 1) * D],
                                             beta[:, 2 + i, t * P:(t + 1) * P], m[:, i, :],
                                             start=i == 0, stop=i == 1)
                        last.then_inc(outed, 1)
                    n2.pe(pe, x2, (6, 7))
                    pe.wait_ge(n2.s_ready, KC)
                    for n in range(HC):
                        if n >= 4:
                            pe.wait_ge(silued, n - 3)
                        for c in range(KC):
                            last = pe.matmul(k.ps[:, 2 + n % 4, :], w1[:, c, n * P:(n + 1) * P], x2T[:, c, :],
                                             start=c == 0, stop=c == KC - 1)
                        last.then_inc(up, 1)
                    pe.wait_ge(silued, HC)
                    for t in range(TT):
                        for n in range(HC):
                            last = pe.matmul(k.ps[:, t // 2, (t % 2) * D:(t % 2 + 1) * D],
                                             hT[:, n, t * P:(t + 1) * P], w2[:, n, :],
                                             start=n == 0, stop=n == HC - 1)
                        last.then_inc(down, 1)



class Product:

    def __init__(self, dst, pairs, rows, n, add=None, mult=None, row=None, stats=None):
        self.dst, self.pairs, self.rows, self.n, self.stats = dst, pairs, rows, n, stats
        self.add, self.mult, self.row = add, mult, row


def project(k, products, batch=None):
    on_act = [i for i, p in enumerate(products) if i % 2 and p.add is None and p.row is None]
    on_dve = [i for i in range(len(products)) if i not in on_act]
    rank = {i: n for lst in (on_act, on_dve) for n, i in enumerate(lst)}
    with signals(k.nc, "made", "act_moved", "dve_moved", "batch_picked", "stats_made") as (
            made, act_moved, dve_moved, batch_picked, stats_made), k.nc.Block() as block:
        @block.tensor
        def _(pe):
            if batch is not None:
                pe.wait_ge(batch_picked, KC)
            for i, p in enumerate(products):
                if i >= 8:
                    pe.wait_ge(act_moved if i - 8 in on_act else dve_moved, rank[i - 8] + 1)
                for j, (lhsT, rhs) in enumerate(p.pairs):
                    last = pe.matmul(k.ps[0:p.rows, i % 8, 0:p.n], lhsT, rhs, start=j == 0,
                                     stop=j == len(p.pairs) - 1)
                last.then_inc(made, 1)

        @block.scalar
        def _(act):
            for i in on_act:
                p = products[i]
                act.wait_ge(made, i + 1)
                out = k.ps[0:p.rows, i % 8, 0:p.n]
                if p.mult is None:
                    act.copy(p.dst, out).then_inc(act_moved, 1)
                else:
                    act.mul(p.dst, out, p.mult).then_inc(act_moved, 1)

        @block.vector
        def _(dve):
            if batch is not None:
                pick_batch(dve, *batch, k.xnT, batch_picked)
            for i in on_dve:
                p = products[i]
                dve.wait_ge(made, i + 1)
                out = k.ps[0:p.rows, i % 8, 0:p.n]
                if p.row is not None:
                    dve.tensor_tensor(p.dst, out, p.row, ALU.add).then_inc(dve_moved, 1)
                elif p.add is not None:
                    dve.tensor_scalar(p.dst, out, p.add, p.mult, ALU.add,
                                      ALU.bypass if p.mult is None else ALU.mult).then_inc(dve_moved, 1)
                elif p.mult is not None:
                    dve.tensor_scalar(p.dst, out, p.mult, None, ALU.mult).then_inc(dve_moved, 1)
                else:
                    dve.tensor_copy(p.dst, out).then_inc(dve_moved, 1)
                if p.stats is not None:
                    dve.wait_ge(dve_moved, rank[i] + 1)
                    dve.bn_stats(p.stats, p.dst).then_inc(stats_made, 1)


class Item:

    def __init__(self, halves, scores, chunks, mask=None):
        self.halves = halves
        self.scores = scores
        self.chunks = chunks
        self.mask = mask


class Head:

    def __init__(self, rows, parts, store=None):
        self.rows, self.parts = rows, parts
        self.store = store


def attend(k, items, heads, ahead=()):
    nc, N = k.nc, len(items)
    wide = len(items[0].halves) == 2
    wmax = max(sum(it.halves) for it in items)
    cmax = (wmax + P - 1) // P
    SB = 2 if wide else 3
    LAG = 3
    PB = LAG + 1
    stores = [h for h in range(len(heads)) if heads[h].store is not None]
    with ExitStack() as st, signals(nc, "scored", "maxed", "exped", "inverted", "shared", "turned", "copied",
                                    "copied_fifth", "valued", "stored", "mask_order",
                                    "ahead_made", "ahead_moved_act", "ahead_moved_dve") as (
            scored, maxed, exped, inverted, shared, turned, copied, copied_fifth, valued, stored, order,
            ahead_made, ahead_moved_act, ahead_moved_dve):
        prob = k.sb("probs", [P, PB, wmax], st)
        pT = k.sb("probs_T", [P, 2, cmax, T], st)
        nmax = k.sb("neg_max", [P, 4], st)
        tot = k.sb("exp_sum", [P, 4], st)
        inv = k.sb("inv_sum", [P, 4], st)

        def score_banks(i):
            h = items[i].halves
            if wide:
                return k.ps[:, 2 * (i % 2):2 * (i % 2) + 2, 0:h[0]]
            return k.ps[:, i % 3, 0:h[0]]

        def probs(i):
            w = prob[:, i % PB, 0:sum(items[i].halves)]
            return w.rearrange("p (a n) -> p a n", a=2) if wide else w

        def turned_place(i, c):
            return k.ps[:, 4 + i % 2, c * P:(c + 1) * P] if c < 4 else k.ps[:, 7, 0:P]

        def ahead_bank(n):
            p = ahead[n]
            return k.ps[0:p.rows, 4 + n % 4, 0:p.n]

        with nc.Block() as block:
            @block.tensor
            def _(pe):
                for i in range(N + 4 + LAG):
                    if i < N:
                        if i >= SB:
                            pe.wait_ge(exped, i - SB + 1)
                        for lhsT, rhs, bank in items[i].scores:
                            out = score_banks(i)
                            last = pe.matmul(out[:, bank, :] if wide else out, lhsT, rhs, start=True, stop=True)
                        last.then_inc(scored, 1)
                    for n in range(4 * i, min(4 * i + 4, len(ahead))):
                        if n >= 4:
                            pe.wait_ge(ahead_moved_dve if n % 2 else ahead_moved_act, (n - 4) // 2 + 1)
                        pairs = ahead[n].pairs
                        for c, (lhsT, rhs) in enumerate(pairs):
                            last = pe.matmul(ahead_bank(n), lhsT, rhs, start=c == 0, stop=c == len(pairs) - 1)
                        last.then_inc(ahead_made, 1)
                    if i == LAG and ahead:
                        pe.wait_ge(ahead_moved_act, (len(ahead) + 1) // 2)
                        pe.wait_ge(ahead_moved_dve, len(ahead) // 2)
                    if LAG <= i < N + LAG:
                        j = i - LAG
                        pe.wait_ge(shared, j + 1)
                        if j >= 2:
                            pe.wait_ge(copied, j - 1)
                        if wide and j >= 1:
                            pe.wait_ge(copied_fifth, j)
                        at = 0
                        for c, n in items[j].chunks:
                            last = pe.transpose(turned_place(j, c)[0:n, :], prob[:, j % PB, at:at + n],
                                                k.ident[:, :])
                            at += n
                        last.then_inc(turned, 1)
                    if i >= 4 + LAG:
                        h, part = (i - 4 - LAG) // 4, (i - 4 - LAG) % 4
                        if part == 0:
                            pe.wait_ge(copied, 4 * h + 4)
                            if wide:
                                pe.wait_ge(copied_fifth, 4 * h + 4)
                            before = sum(1 for x in stores if x < h)
                            if before:
                                pe.wait_ge(stored, before)
                        for c, n, v, cols, start, stop in heads[h].parts[part]:
                            last = pe.matmul(k.ps[heads[h].rows, 6, 0:cols], v, pT[0:n, h % 2, c, 0:cols],
                                             start=start, stop=stop)
                        if part == 3:
                            last.then_inc(valued, 1)

            @block.vector
            def _(dve):
                o = Order(dve, order)
                for i in range(N + LAG):
                    if i < N:
                        it = items[i]
                        dve.wait_ge(scored, i + 1)
                        if it.mask is not None:
                            bank, c0, n, m = it.mask
                            place = (score_banks(i)[:, bank, :] if wide else score_banks(i))[:, c0:c0 + n]
                            o.do(dve.tensor_tensor(place, place, m, ALU.add))
                        dve.tensor_reduce(nmax[:, i % 4:i % 4 + 1], score_banks(i), AX.XY if wide else AX.X,
                                          ALU.max, negate=True).then_inc(maxed, 1)
                    if i >= LAG:
                        j = i - LAG
                        h, t = j // TT, j % TT
                        dve.wait_ge(turned, j + 1)
                        if h >= 2 and t == 0:
                            dve.wait_ge(valued, h - 1)
                        c0 = items[j].chunks[0][0]
                        c1 = min(4, items[j].chunks[-1][0] + 1)
                        dve.tensor_copy(pT[:, h % 2, c0:c1, t * P:(t + 1) * P],
                                        k.ps[:, 4 + j % 2, c0 * P:c1 * P]
                                        .rearrange("p (c q) -> p c q", q=P)).then_inc(copied, 1)
                    if 1 <= i < N + 1:
                        j = i - 1
                        dve.wait_ge(exped, j + 1)
                        dve.reciprocal(inv[:, j % 4:j % 4 + 1], tot[:, j % 4:j % 4 + 1]).then_inc(inverted, 1)
                    for n in range(4 * i + 1, min(4 * i + 4, len(ahead)), 2):
                        dve.wait_ge(ahead_made, n + 1)
                        dve.tensor_copy(ahead[n].dst, ahead_bank(n)).then_inc(ahead_moved_dve, 1)

            @block.gpsimd
            def _(pool):
                for j in range(N):
                    pool.wait_ge(inverted, j + 1)
                    w = prob[:, j % PB, 0:sum(items[j].halves)]
                    pool.tensor_scalar(w, w, inv[:, j % 4:j % 4 + 1], 1.0, ALU.mult, ALU.mult).then_inc(shared, 1)

            @block.scalar
            def _(act):
                for i in range(1, N + 4 + LAG):
                    if i <= N:
                        j = i - 1
                        act.wait_ge(maxed, j + 1)
                        if j >= PB:
                            act.wait_ge(turned, j - PB + 1)
                        if j >= 4:
                            act.wait_ge(inverted, j - 3)
                        act.activation(probs(j), score_banks(j), ACT.Exp, bias=nmax[:, j % 4:j % 4 + 1],
                                       accum_out=tot[:, j % 4:j % 4 + 1]).then_inc(exped, 1)
                    for n in range(4 * i - 4, min(4 * i, len(ahead)), 2):
                        act.wait_ge(ahead_made, n + 1)
                        act.copy(ahead[n].dst, ahead_bank(n)).then_inc(ahead_moved_act, 1)
                    if wide and LAG <= i < N + LAG:
                        j = i - LAG
                        h, t = j // TT, j % TT
                        n = items[j].chunks[4][1]
                        act.wait_ge(turned, j + 1)
                        if h >= 2 and t == 0:
                            act.wait_ge(valued, h - 1)
                        act.copy(pT[0:n, h % 2, 4, t * P:(t + 1) * P],
                                 turned_place(j, 4)[0:n, :]).then_inc(copied_fifth, 1)
                    if i >= 7 + LAG and (i - 4 - LAG) % 4 == 3:
                        h = (i - 4 - LAG) // 4
                        if heads[h].store is not None:
                            rows, dst = heads[h].store
                            act.wait_ge(valued, h + 1)
                            act.copy(dst, k.ps[rows, 6, :]).then_inc(stored, 1)




def output_projection(k, b, o, wo, width, bias_row=None, gain_row=None, offset_row=None, oT=None, before=None):
    given = oT is not None
    nc, C = k.nc, width // P
    with ExitStack() as st, signals(nc, "turned", "moved", "made", "summed", "stats", "aggr", "shifted", "rstd",
                                    "order") as (turned, moved, made, summed, stats, aggr, shifted, rstd, order):
        oT = oT if given else k.sb("attended_T", [P, C, T], st)
        y = k.sb("projected", [P, TT, D], st)
        stat = k.sb("out_stat", [P, TT, 6], st)
        mv = k.sb("out_mv", [P, TT, 2], st)
        rs = k.sb("out_rstd", [P, 2, TT], st)
        x = batch_tiles(k, b)

        def summand(t):
            return k.ps[:, 4 + t, 0:D] if before is None else y[:, t, :]

        with nc.Block() as block:
            @block.tensor
            def _(pe):
                for c in range(0 if given else C):
                    if c >= 4:
                        pe.wait_ge(moved, c - 3)
                    for t in range(TT):
                        last = pe.transpose(k.ps[:, c % 4, t * P:(t + 1) * P], o[:, t, c * P:(c + 1) * P],
                                            k.ident[:, :])
                    last.then_inc(turned, 1)
                if not given:
                    pe.wait_ge(moved, C)
                for t in range(TT):
                    for c in range(C):
                        last = pe.matmul(k.ps[:, 4 + t, 0:D], oT[:, c, t * P:(t + 1) * P], wo[:, c, :],
                                         start=c == 0, stop=c == C - 1)
                    last.then_inc(made, 1)

            @block.scalar
            def _(act):
                for c in range(0 if given else C):
                    act.wait_ge(turned, c + 1)
                    act.copy(oT[:, c, :], k.ps[:, c % 4, :]).then_inc(moved, 1)

            @block.vector
            def _(dve):
                o_ = Order(dve, order)
                if gain_row is None:
                    for t in range(TT):
                        if bias_row is not None:
                            o_.do(dve.tensor_tensor(x(t), x(t), bias_row, ALU.add))
                        dve.wait_ge(made, t + 1)
                        dve.tensor_tensor(x(t), x(t), k.ps[:, 4 + t, 0:D], ALU.add).then_inc(summed, 1)
                    return
                for t in range(TT):
                    o_.mark(dve.tensor_tensor(x(t), x(t), offset_row, ALU.add))
                    if before is not None:
                        o_.mark(dve.tensor_tensor(y[:, t, :], before[1](t), before[0], ALU.add))
                o_.wait()
                for t in range(TT):
                    if before is not None:
                        dve.wait_ge(made, t + 1)
                        o_.mark(dve.tensor_tensor(y[:, t, :], k.ps[:, 4 + t, 0:D], y[:, t, :], ALU.add))
                for t in range(TT):
                    dve.wait_ge(made, t + 1)
                    if before is not None:
                        dve.wait_ge(order, o_.n - TT + t + 1)
                    dve.bn_stats(stat[:, t, :], summand(t)).then_inc(stats, 1)
                for t in range(TT):
                    dve.wait_ge(stats, t + 1)
                    dve.bn_aggr(mv[:, t, :], stat[:, t, :]).then_inc(aggr, 1)
                dve.wait_ge(aggr, TT)
                for t in range(TT):
                    o_.mark(dve.scalar_tensor_tensor(out=y[:, t, :], in0=summand(t), scalar=mv[:, t, 0:1],
                                                     in1=gain_row, op0=ALU.subtract, op1=ALU.mult))
                dve.wait_ge(rstd, 1)
                o_.wait()
                for t in range(TT):
                    dve.scalar_tensor_tensor(out=x(t), in0=y[:, t, :], scalar=rs[:, 1, t:t + 1], in1=x(t),
                                             op0=ALU.mult, op1=ALU.add).then_inc(summed, 1)

            if gain_row is not None:
                @block.gpsimd
                def _(pool):
                    pool.wait_ge(aggr, TT)
                    pool.tensor_scalar(rs[:, 0, :], mv[:, :, 1], EPS, 1.0, ALU.add, ALU.mult).then_inc(shifted, 1)
                    pool.wait_ge(shifted, 1)
                    pool.tensor_tensor(rs[:, 1, :], rs[:, 0, :], k.half[:, 0:TT], ALU.pow).then_inc(rstd, 1)


def l0_xattn(k):
    nc = k.nc
    NK = 64
    with ExitStack() as st:
        wq, wk, wv, wo = (k.weight("L0_xattn_" + n, st) for n in ("wq", "wk", "wv", "wo"))
        ctxT = k.weight("ctx_T", st)
        mask8 = k.const("head_mask8", st)
        logw = k.weight("L0_side", st)
        xT = norm_all(k, st, twice=False,
                      load=(wq, wk, wv, wo, ctxT, mask8, logw))
        kT = k.sb("keys_T", [P, KC, B, NK], st)
        ctx2 = k.sb("ctx_T_twice", [P, KC, B, 2, NK], st)
        with signals(nc, "doubled") as (doubled,), nc.Block() as block:
            @block.vector
            def _(dve):
                for i in range(2):
                    dve.tensor_copy(ctx2[:, :, :, i, :], ctxT[:, :, :].rearrange("p c (b n) -> p c b n", b=B))\
                        .then_inc(doubled, 1)

        v = k.sb("values", [2 * NK, B, D], st)
        project(k, [Product(kT[:, c, :, :].rearrange("p b n -> p (b n)"),
                            [(wk[:, i, c * P:(c + 1) * P], ctxT[:, i, :]) for i in range(KC)], P, B * NK,
                            add=k.vec("L0_xattn_bk")[:, c:c + 1]) for c in range(KC)] +
                [Product(v[:, b, :], [(ctx2[:, i, b, :, :].rearrange("p s n -> p (s n)"), wv[:, i, :])
                                      for i in range(KC)], 2 * NK, D, row=k.row("L0_xattn_bv")) for b in range(B)])
        with signals(nc, "shifted", "logged") as (shifted, logged), nc.Block() as block:
            @block.vector
            def _(dve):
                dve.tensor_scalar(logw[:, 0, :], logw[:, 0, :], 1e-20, 2.0 ** 20, ALU.add,
                                  ALU.mult).then_inc(shifted, 1)
                dve.wait_ge(logged, 1)
                dve.tensor_scalar(logw[:, 0, :], logw[:, 0, :], -20 * float(np.log(2.0)), None,
                                  ALU.add).then_inc(shifted, 1)

            @block.scalar
            def _(act):
                act.wait_ge(shifted, 1)
                act.activation(logw[:, 0, :], logw[:, 0, :], ACT.Ln).then_inc(logged, 1)

        qT = k.sb("queries_T", [P, KC, T], st)
        km = k.sb("keys_by_head", [P, B, 16, NK], st)
        vb = k.sb("values_in_pairs", [P, B, 8, 32], st)
        o = k.sb("attended", [P, TT, D], st)
        prob = k.sb("probs", [P, 3, 8, NK], st)
        pT = k.sb("probs_T", [P, 2, 4, P], st)
        mx = k.sb("max", [P, 4, 8], st)
        tot = k.sb("exp_sum", [P, 4, 8], st)
        inv = k.sb("inv_sum", [P, 4, 8], st)
        with signals(nc, "zeroed", "spread") as (zeroed, spread), nc.Block() as block:
            @block.gpsimd
            def _(pool):
                pool.memset(vb[:, :, :, :], 0.0).then_inc(zeroed, 1)

            @block.vector
            def _(dve):
                for h in range(16):
                    dve.tensor_scalar(km[:, :, h, :], kT[:, h // 8, :, :], mask8[:, h % 8:h % 8 + 1], None,
                                      ALU.mult).then_inc(spread, 1)
                dve.wait_ge(zeroed, 1)
                for b in range(B):
                    for half in range(2):
                        r = slice(NK * half, NK * (half + 1))
                        dve.tensor_copy(vb[r, b, :, 16 * half:16 * half + 16],
                                        v[r, b, :].rearrange("p (i s d) -> p i s d", s=2, d=16)
                                        [:, :, half, :]).then_inc(spread, 1)
        with nc.Fori(0, B) as b:
            project(k, [Product(qT[:, c, :], [(wq[:, i, c * P:(c + 1) * P], k.xnT[:, i, :]) for i in range(KC)],
                                P, T, add=k.vec("L0_xattn_bq")[:, c:c + 1], mult=0.25) for c in range(KC)], batch=(xT, b))
            items = [(t, c) for t in range(TT) for c in range(KC)]
            N = len(items)
            with signals(nc, "scored", "weighted", "maxed", "below", "exped", "summed", "turned", "copied", "valued", "stored",
                         "order") as (scored, weighted, maxed, below, exped, summed, turned, copied, valued, stored,
                                      order), nc.Block() as block:
                @block.tensor
                def _(pe):
                    for i in range(N + 3):
                        if i < N:
                            t, c = items[i]
                            if i >= 3:
                                pe.wait_ge(weighted, i - 2)
                            pe.matmul(k.ps[:, i % 3, :], qT[:, c, t * P:(t + 1) * P],
                                      km[:, bass.ds(b, 1), 8 * c:8 * c + 8, :].rearrange("p o h n -> p (o h n)"),
                                      start=True, stop=True).then_inc(scored, 1)
                        if 2 <= i < N + 2:
                            j = i - 2
                            pe.wait_ge(exped, j + 1)
                            if j >= 2:
                                pe.wait_ge(copied, j - 1)
                            for a in range(4):
                                last = pe.transpose(k.ps[:, 4 + j % 2, a * P:(a + 1) * P],
                                                    prob[:, j % 3, 2 * a:2 * a + 2, :].rearrange(
                                                        "p h n -> p (h n)"), k.ident[:, :])
                            last.then_inc(turned, 1)
                        if i >= 3:
                            j = i - 3
                            t, c = items[j]
                            pe.wait_ge(copied, j + 1)
                            if j >= 2:
                                pe.wait_ge(stored, j - 1)
                            for a in range(4):
                                last = pe.matmul(k.ps[:, 6 + j % 2, 32 * a:32 * a + 32], pT[:, j % 2, a, :],
                                                 vb[:, bass.ds(b, 1), 4 * c + a, :].rearrange("p o d -> p (o d)"), start=True, stop=True)
                            last.then_inc(valued, 1)

                @block.scalar
                def _(act):
                    for i in range(N + 2):
                        if i < N:
                            act.wait_ge(below, i + 1)
                            act.activation(prob[:, i % 3, :, :], prob[:, i % 3, :, :],
                                           ACT.Exp).then_inc(exped, 1)
                        if i >= 2:
                            j = i - 2
                            act.wait_ge(turned, j + 1)
                            if j >= 2:
                                act.wait_ge(valued, j - 1)
                            act.copy(pT[:, j % 2, :, :], k.ps[:, 4 + j % 2, :].rearrange(
                                "p (c q) -> p c q", c=4)).then_inc(copied, 1)

                @block.gpsimd
                def _(pool):
                    for i in range(N):
                        pool.wait_ge(maxed, i + 1)
                        pool.tensor_tensor(prob[:, i % 3, :, :], prob[:, i % 3, :, :],
                                           mx[:, i % 4, :].unsqueeze(2).to_broadcast([P, 8, NK]),
                                           ALU.subtract).then_inc(below, 1)

                @block.vector
                def _(dve):
                    ord_ = Order(dve, order)
                    for i in range(N + 3):
                        if i < N:
                            dve.wait_ge(scored, i + 1)
                            if i >= 3:
                                dve.wait_ge(turned, i - 2)
                                dve.wait_ge(summed, i - 2)
                            lw = logw[:, 0, bass.ds(b * NK, NK)].unsqueeze(1).to_broadcast([P, 8, NK])
                            dve.tensor_tensor(prob[:, i % 3, :, :],
                                              k.ps[:, i % 3, :].rearrange("p (h n) -> p h n", h=8), lw,
                                              ALU.add).then_inc(weighted, 1)
                            dve.wait_ge(weighted, i + 1)
                            dve.reduce_max(mx[:, i % 4, :], prob[:, i % 3, :, :], AX.X).then_inc(maxed, 1)
                        if 2 <= i < N + 2:
                            j = i - 2
                            dve.wait_ge(exped, j + 1)
                            dve.reduce_sum(tot[:, j % 4, :], prob[:, j % 3, :, :], AX.X).then_inc(summed, 1)
                            dve.wait_ge(summed, j + 1)
                            ord_.mark(dve.reciprocal(inv[:, j % 4, :], tot[:, j % 4, :]))
                        if i >= 3:
                            j = i - 3
                            t, c = items[j]
                            dve.wait_ge(valued, j + 1)
                            dve.wait_ge(order, j + 1)
                            dve.tensor_tensor(o[:, t, c * P:(c + 1) * P].rearrange("p (h d) -> p h d", h=8),
                                              k.ps[:, 6 + j % 2, 0:P].rearrange("p (h d) -> p h d", h=8),
                                              inv[:, j % 4, :].unsqueeze(2).to_broadcast([P, 8, 16]),
                                              ALU.mult).then_inc(stored, 1)
            output_projection(k, b, o, wo, D, bias_row=k.row("L0_xattn_bo"))


def l2_attn(k):
    nc = k.nc
    with ExitStack() as st:
        wq, wk, wv, wo = (k.weight("L2_attn_" + n, st) for n in ("Wq", "Wk", "Wv", "Wo"))
        mask8 = k.const("head_mask8", st)
        block_mask = k.const("block_mask", st)
        xT = norm_all(k, st, twice=False,
                      load=(wq, wk, wv, wo, mask8, block_mask))
        qT = k.sb("queries_T", [P, KC, T], st)
        kT = k.sb("keys_T", [P, KC, T], st)
        km = k.sb("keys_by_head", [P, 16, T], st)
        v = k.sb("values", [P, TT, D], st)
        vh = k.sb("values_by_head", [P, TT, 16, P], st)
        o = k.sb("attended_T", [P, KC, T], st)
        with signals(nc, "zeroed") as (zeroed,), nc.Block() as block:
            @block.gpsimd
            def _(pool):
                pool.memset(vh[:, :, :, :], 0.0).then_inc(zeroed, 1)
        with nc.Fori(0, B) as b:
            project(k, [Product(qT[:, c, :], [(wq[:, i, c * P:(c + 1) * P], k.xnT[:, i, :]) for i in range(KC)],
                                P, T, add=k.vec("L2_attn_bq")[:, c:c + 1], mult=k.vec("L2_scale")[:, 0:1])
                        for c in range(KC)] +
                    [Product(kT[:, c, :], [(wk[:, i, c * P:(c + 1) * P], k.xnT[:, i, :]) for i in range(KC)],
                             P, T, add=k.vec("L2_attn_bk")[:, c:c + 1]) for c in range(KC)] +
                    [Product(v[:, t, :], [(k.xnT[:, i, t * P:(t + 1) * P], wv[:, i, :]) for i in range(KC)],
                             P, D, row=k.row("L2_attn_bv")) for t in range(TT)], batch=(xT, b))
            with signals(nc, "dve_masked", "act_masked", "spread") as (dve_masked, act_masked, spread), \
                    nc.Block() as block:
                @block.vector
                def _(dve):
                    for h in range(10):
                        dve.tensor_scalar(km[:, h, :], kT[:, h // 8, :], mask8[:, h % 8:h % 8 + 1], None,
                                          ALU.mult).then_inc(dve_masked, 1)

                @block.scalar
                def _(act):
                    for h in range(10, 16):
                        act.mul(km[:, h, :], kT[:, h // 8, :], mask8[:, h % 8:h % 8 + 1]).then_inc(act_masked, 1)

                @block.gpsimd
                def _(pool):
                    for c in range(TT):
                        for g in range(KC):
                            pool.tensor_copy(vh[:, c, 8 * g:8 * g + 8, :].rearrange(
                                "p h (a d) -> p (h a) d", d=16)[:, 0:64:9, :],
                                v[:, c, g * P:(g + 1) * P].rearrange("p (h d) -> p h d", d=16)).then_inc(spread, 1)

            def parts(h):
                return [[(c, P, vh[:, c, h, :], (c + 1) * P, h % 8 == 0 and c == TT - 1, h % 8 == 7 and c == 0)]
                        for c in reversed(range(TT))]

            attend(k, [Item([T - t * P], [(qT[:, h // 8, t * P:(t + 1) * P], km[:, h, t * P:T], 0)],
                            [(c, P) for c in range(t, TT)], mask=(0, 0, P, block_mask[:, :]))
                       for h in range(16) for t in range(TT)],
                   [Head(slice(0, P), parts(h), store=(slice(0, P), o[:, h // 8, :]) if h % 8 == 7 else None)
                    for h in range(16)])
            output_projection(k, b, None, wo, D, oT=o, bias_row=k.row("L2_attn_bo"))


def unit_heads(k, units, src, inv_width, floor):
    nc, N = k.nc, len(units)
    with ExitStack() as st, signals(nc, "made", "squared", "summed", "floored", "inverted", "scaled", "turned",
                                    "moved") as (made, squared, summed, floored, inverted, scaled, turned, moved):
        sq = k.sb("squares", [P, 2, 512], st)
        un = k.sb("unit_rows", [P, 2, 512], st)
        ss = k.sb("square_sum", [P, 4, 3, 8], st)
        with nc.Block() as block:
            @block.tensor
            def _(pe):
                for i in range(N + 3):
                    if i < N:
                        t0, n, w, c0, _, _ = units[i]
                        if i >= 4:
                            pe.wait_ge(scaled, i - 3)
                        for c in range(KC):
                            last = pe.matmul(k.ps[0:n, i % 4, :], src[:, c, t0:t0 + n], w[:, c, c0:c0 + 512],
                                             start=c == 0, stop=c == KC - 1)
                        last.then_inc(made, 1)
                    if i >= 3:
                        j = i - 3
                        n = units[j][1]
                        pe.wait_ge(scaled, j + 1)
                        if j >= 4:
                            pe.wait_ge(moved, j - 3)
                        for c in range(4):
                            last = pe.transpose(k.ps[:, 4 + j % 4, c * n:(c + 1) * n],
                                                un[0:n, j % 2, c * P:(c + 1) * P], k.ident[0:n, 0:n])
                        last.then_inc(turned, 1)

            @block.scalar
            def _(act):
                for i in range(N + 3):
                    if i < N:
                        n = units[i][1]
                        act.wait_ge(made, i + 1)
                        if i >= 2:
                            act.wait_ge(summed, i - 1)
                        act.activation(sq[0:n, i % 2, :], k.ps[0:n, i % 4, :], ACT.Square).then_inc(squared, 1)
                    if i >= 3:
                        _, n, _, _, dst, gain = units[i - 3]
                        act.wait_ge(turned, i - 2)
                        act.mul(dst, k.ps[:, 4 + (i - 3) % 4, 0:4 * n].rearrange("p (c n) -> p c n", c=4),
                                gain).then_inc(moved, 1)

            @block.vector
            def _(dve):
                for i in range(N + 1):
                    if i < N:
                        n = units[i][1]
                        dve.wait_ge(squared, i + 1)
                        if i >= 4:
                            dve.wait_ge(floored, i - 3)
                        dve.reduce_sum(ss[0:n, i % 4, 0, :], sq[0:n, i % 2, :].rearrange("p (h d) -> p h d", h=8),
                                       AX.X).then_inc(summed, 1)
                    if i >= 1:
                        j = i - 1
                        n = units[j][1]
                        dve.wait_ge(inverted, j + 1)
                        if j >= 2:
                            dve.wait_ge(turned, j - 1)
                        dve.tensor_tensor(un[0:n, j % 2, :].rearrange("p (h d) -> p h d", h=8),
                                          k.ps[0:n, j % 4, :].rearrange("p (h d) -> p h d", h=8),
                                          ss[0:n, j % 4, 2, :].unsqueeze(2).to_broadcast([n, 8, 64]),
                                          ALU.mult).then_inc(scaled, 1)

            @block.gpsimd
            def _(pool):
                for i in range(N):
                    n = units[i][1]
                    pool.wait_ge(summed, i + 1)
                    pool.tensor_scalar(ss[0:n, i % 4, 1, :], ss[0:n, i % 4, 0, :], inv_width, floor, ALU.mult,
                                       ALU.max).then_inc(floored, 1)
                    pool.wait_ge(floored, i + 1)
                    if i >= 4:
                        pool.wait_ge(scaled, i - 3)
                    pool.tensor_tensor(ss[0:n, i % 4, 2, :], ss[0:n, i % 4, 1, :], k.half[0:n, 0:8],
                                       ALU.pow).then_inc(inverted, 1)


def latent_attention(k, pre, H, names, unit=None, mask=None, **out_rows):
    nc = k.nc
    NC = 64
    W = H * 64
    NK = T + NC
    PAIRS = W // P
    lg, lb, cg, cb, w_out = names
    with ExitStack() as st:
        wq, wkv, wo = (k.weight(pre + n, st) for n in ("Wq", "Wkv", w_out))
        ctx = k.const("ctx_rows", st)
        kmask = k.weight(mask, st) if mask else None
        xT = norm_all(k, st, gain=k.vec(pre + lg), offset=k.vec(pre + lb),
                      load=[wq, wkv, wo, ctx, *([kmask] if mask else [])])
        ctxT = k.sb("context_T", [P, KC, B * NC], st)
        cn = k.sb("context_normed", [P, B, D], st)
        with signals(nc, *norm_names("c_")) as sems, ExitStack() as cs:
            n = Norm(k, cs, sems, "c", twice=False, gain=k.vec(pre + cg), offset=k.vec(pre + cb), tiles=B, rows=NC)
            with nc.Block() as block:
                @block.vector
                def _(dve):
                    n.dve(dve, lambda t: ctx[:, t, :], cn)

                @block.gpsimd
                def _(pool):
                    n.pool(pool)

                @block.tensor
                def _(pe):
                    n.pe(pe, cn, (6, 7))

                @block.scalar
                def _(act):
                    n.act(act, ctxT, (6, 7))
        kvT = k.sb("kv_input_T", [P, KC, NK], st)
        qT = k.sb("queries_T", [P, PAIRS, T], st)
        kT = k.sb("keys_T", [P, PAIRS, NK], st)
        v = k.sb("values", [P, TT + 1, W], st)
        km = k.sb("key_mask", [P, NC], st) if mask else None
        o = k.sb("attended_T", [P, PAIRS, T], st)
        with nc.Fori(0, B) as b:
            with signals(nc, "picked", "batch_picked") as (picked, batch_picked), nc.Block() as block:
                @block.vector
                def _(dve):
                    pick_batch(dve, xT, b, kvT, batch_picked)
                    dve.tensor_copy(kvT[:, :, T:NK], ctxT[:, :, bass.ds(b * NC, NC)]).then_inc(picked, 1)
                    if mask:
                        dve.tensor_scalar(km[:, :], kmask[:, 0, bass.ds(b * NC, NC)], 1.0, -1.0, ALU.min,
                                          ALU.add).then_inc(picked, 1)
                        dve.wait_ge(picked, 2)
                        dve.tensor_scalar(km[:, :], km[:, :], 1e30, None, ALU.mult).then_inc(picked, 1)
            values = [Product(v[0:n, t, a * 512:(a + 1) * 512],
                              [(kvT[:, i, t * P:t * P + n], wkv[:, i, W + a * 512:W + (a + 1) * 512])
                               for i in range(KC)], n, 512)
                      for t, n in enumerate([P] * TT + [NC]) for a in range(W // 512)]
            if unit is None:
                project(k, [Product(qT[:, j, :], [(wq[:, i, j * P:(j + 1) * P], kvT[:, i, 0:T])
                                                  for i in range(KC)], P, T, mult=0.125) for j in range(PAIRS)] +
                        [Product(kT[:, j, c0:c1], [(wkv[:, i, j * P:(j + 1) * P], kvT[:, i, c0:c1])
                                                   for i in range(KC)], P, c1 - c0)
                         for j in range(PAIRS) for c0, c1 in ((0, T), (T, NK))])
            else:
                inv_width, floor, qg, kg = unit
                unit_heads(k, [(t * P, P if t < TT else NC, w, a * 512,
                                dst[:, 4 * a:4 * a + 4, t * P:t * P + (P if t < TT else NC)], gain)
                               for w, dst, gain, last in ((wq, qT, qg, TT), (wkv, kT, kg, TT + 1))
                               for t in range(last) for a in range(W // 512)], kvT, inv_width, floor)
            items, heads = [], []
            half = NK // 2
            for h in range(H):
                r = slice(64 * (h % 2), 64 * (h % 2) + 64)
                for t in range(TT):
                    q = qT[r, h // 2, t * P:(t + 1) * P]
                    items.append(Item([half, half], [(q, kT[r, h // 2, a * half:(a + 1) * half], a)
                                                     for a in range(2)],
                                      list(enumerate([P] * TT + [NC])),
                                      mask=(1, half - NC, NC, km[:, :]) if mask else None))
                pieces = [(c, n, v[0:n, c, h * 64:(h + 1) * 64], T, c == 0, c == TT)
                          for c, n in enumerate([P] * TT + [NC])]
                heads.append(Head(r, [pieces[0:2], pieces[2:3], pieces[3:4], pieces[4:5]],
                                  store=(r, o[r, h // 2, :])))
            attend(k, items, heads, ahead=values)
            output_projection(k, b, None, wo, W, oT=o, **out_rows)


def l1_xattn(k):
    latent_attention(k, "L1_xattn_", 16, ("ln_l_g", "ln_l_b", "ln_m_g", "ln_m_b", "Wout"))


def l2_xattn(k):
    latent_attention(k, "L2_xattn_", 16, ("ln_l_g", "ln_l_b", "ln_x_g", "ln_x_b", "Wout"),
                     unit=(1.0 / 64, 1e-16, k.vec("L2_query_gain")[:, 0:1], k.vec("L2_xattn_kn_g2")[:, 0:1]),
                     mask="mask_bf1", bias_row=k.row("L2_xattn_bout"))


def l3_xattn(k):
    latent_attention(k, "L3_xattn_", 8, ("ln_l_w", "ln_l_b", "ln_x_w", "ln_x_b", "Wo"),
                     unit=(1.0, 1e-24, k.vec("L3_query_gain")[:, 0:1], k.vec("L3_xattn_k_scale2")[:, 0:1]),
                     mask="mask_bk0", gain_row=k.row("L3_xattn_ln_o_w"), offset_row=k.row("L3_xattn_ln_o_b"))



def l1_attn(k):
    nc = k.nc
    C = 16
    NCH = T // C
    PER = P // C
    KV = C // 2 + 1
    with ExitStack() as st:
        ws = {n: k.weight("L1_attn_" + n, st) for n in ("Wq", "Wk", "Wv", "Wg", "Wo")}
        mask8 = k.const("head_mask8", st)
        diag = k.const("chunk_diagonal", st)
        rows = k.sb("batches_normed", [P, NT, D], st)
        xT = norm_all(k, st, twice=False, rows=rows,
                      load=[*ws.values(), mask8, diag])
        q = k.sb("queries_decayed", [P, 2, NCH, C], st)
        kT = k.sb("keys_T", [P, NCH, C], st)
        g = k.sb("gates_T", [P, NCH, C], st)
        v = k.sb("values", [P, TT, P], st)
        vj = k.sb("values_by_position", [NCH, C, P], st)
        kd = k.sb("keys_decayed", [P, NCH, C], st)
        kdt = k.sb("keys_decayed_rows", [P, TT, P], st)
        r = k.sb("suffix_gates", [P, NCH], st)
        a = k.sb("scores_diagonal", [NCH, 2, NCH * C], st)
        vm = k.sb("values_by_chunk", [P, TT, PER, P], st)
        state = k.sb("states", [P, NCH + 1, P], st)
        zero = k.sb("zeros", [P, T], st)
        oT = k.sb("attended_T", [P, 1, T], st)
        with signals(nc, "zeroed") as (zeroed,), nc.Block() as block:
            @block.gpsimd
            def _(pool):
                pool.memset(zero[:, :], 0.0).then_inc(zeroed, 1)
                pool.memset(state[:, 0, :], 0.0).then_inc(zeroed, 1)
        with nc.Fori(0, B) as b:
            flat = lambda w: w.rearrange("p c j -> p (c j)")
            positions = k.xnT[:, :, :].rearrange("p i (c j) -> p i c j", j=C)
            project(k, [Product(flat(dst), [(ws[n][:, i, :], k.xnT[:, i, :]) for i in range(KC)], P, T,
                                add=k.vec("L1_attn_b" + n[1])[:, 0:1])
                        for n, dst in (("Wg", g[:, :, :]), ("Wq", q[:, 0, :, :]), ("Wq", q[:, 1, :, :]),
                                       ("Wk", kT[:, :, :]))] +
                    [Product(v[:, t, :], [(k.xnT[:, i, t * P:(t + 1) * P], ws["Wv"][:, i, :]) for i in range(KC)],
                             P, P, row=k.row("L1_attn_bv")) for t in range(TT)] +
                    [Product(vj[:, j, :], [(positions[:, i, :, j], ws["Wv"][:, i, :]) for i in range(KC)],
                             NCH, P, row=k.row("L1_attn_bv")[0:NCH, :]) for j in range(C)], batch=(xT, b))
            with signals(nc, "gated", "scored", "scored_diag", "decayed", "order", "within", "spread", "turned",
                         "moved", "kv_made", "carried", "outed") as (
                    gated, scored, scored_diag, decayed, order, within, spread, turned, moved, kv_made, carried,
                    outed), nc.Block() as block:
                @block.scalar
                def _(act):
                    act.activation(g[:, :, :], g[:, :, :], ACT.Sigmoid).then_inc(gated, 1)
                    act.wait_ge(turned, 1)
                    act.copy(kdt[:, :, :], k.ps[:, 3, :].rearrange("p (t s) -> p t s", t=TT)).then_inc(moved, 1)
                    act.wait_ge(outed, 1)
                    act.copy(oT[:, 0, :], k.ps[:, 2, :]).then_inc(moved, 1)

                @block.gpsimd
                def _(pool):
                    for t in range(TT):
                        pool.tensor_tensor(vm[:, t, :, :], v[:, t, :].unsqueeze(1).to_broadcast([P, PER, P]),
                                           mask8[:, :].unsqueeze(2).to_broadcast([P, PER, P]),
                                           ALU.mult).then_inc(spread, 1)

                @block.vector
                def _(dve):
                    o = Order(dve, order)
                    o.mark(dve.memset(r[:, :], 1.0))
                    dve.wait_ge(gated, 1)

                    def decay_keys(j):
                        o.wait()
                        o.mark(dve.tensor_tensor(kd[:, :, j], kT[:, :, j], r[:, :], ALU.mult))
                        o.mark(dve.tensor_tensor(r[:, :], r[:, :], g[:, :, j], ALU.mult))

                    def carry(c):
                        dve.wait_ge(kv_made, c // 4 + 1)
                        if c:
                            dve.wait_ge(carried, c)
                        dve.scalar_tensor_tensor(out=state[:, c + 1, :], in0=state[:, c, :], scalar=r[:, c:c + 1],
                                                 in1=k.ps[:, 4 + (c // 4) % 4, (c % 4) * P:(c % 4 + 1) * P],
                                                 op0=ALU.mult, op1=ALU.add).then_inc(carried, 1)

                    for n in range(C):
                        j = C - 1 - n
                        w = C - j
                        src, dst = q[:, n % 2, :, j:C], q[:, (n + 1) % 2, :, j:C]
                        if 2 * n < C:
                            decay_keys(C - 1 - 2 * n)
                            decay_keys(C - 2 - 2 * n)
                        if n >= 1:
                            dve.wait_ge(scored, n)
                            dve.wait_ge(decayed, n)
                        dve.tensor_tensor(dst, src, g[:, :, j:j + 1].to_broadcast([P, NCH, w]),
                                          ALU.mult).then_inc(decayed, 1)
                        dve.wait_ge(scored, n + 1)
                        if n >= 2:
                            dve.wait_ge(within, n - 1)
                        dve.tensor_tensor(a[:, n % 2, 0:NCH * w].rearrange("p (c i) -> p c i", i=w),
                                          k.ps[0:NCH, n % 2, 0:NCH * w].rearrange("p (c i) -> p c i", i=w),
                                          diag[:, :].unsqueeze(2).to_broadcast([NCH, NCH, w]),
                                          ALU.mult).then_inc(scored_diag, 1)
                        if n >= KV + 1:
                            if n == KV + 1:
                                o.wait()
                            for c in range(4 * (n - KV - 1), 4 * (n - KV)):
                                carry(c)
                    for c in range(4 * (C - KV - 1), NCH):
                        carry(c)

                @block.tensor
                def _(pe):
                    pe.matmul(k.ps[:, 2, :], zero[0:1, 0:P], zero[0:1, :], start=True, stop=False,
                              skip_group_check=True)
                    out = k.ps[:, 2, :].rearrange("p (c i) -> p c i", i=C)

                    def add_within(n):
                        j = C - 1 - n
                        w = C - j
                        pe.wait_ge(scored_diag, n + 1)
                        pe.matmul(out[:, :, j:C], vj[:, j, :],
                                  a[:, n % 2, 0:NCH * w].rearrange("p (c i) -> p c i", i=w), start=False,
                                  stop=False, skip_group_check=True).then_inc(within, 1)

                    def keys_times_values(u):
                        if u == 0:
                            pe.wait_ge(moved, 1)
                        pe.wait_ge(spread, u // 2 + 1)
                        if u >= 4:
                            pe.wait_ge(carried, 4 * (u - 3))
                        pe.matmul(k.ps[:, 4 + u % 4, :], kdt[:, u // 2, :],
                                  vm[:, u // 2, 4 * (u % 2):4 * (u % 2) + 4, :].rearrange("p c v -> p (c v)"),
                                  start=True, stop=True).then_inc(kv_made, 1)

                    for n in range(C):
                        j = C - 1 - n
                        w = C - j
                        if n >= 1:
                            pe.wait_ge(decayed, n)
                        if n >= 2:
                            pe.wait_ge(scored_diag, n - 1)
                        pe.matmul(k.ps[0:NCH, n % 2, 0:NCH * w].rearrange("p (c i) -> p c i", i=w), kT[:, :, j],
                                  q[:, n % 2, :, j:C], start=True, stop=True).then_inc(scored, 1)
                        if n >= 1:
                            add_within(n - 1)
                        if n == C // 2:
                            pe.wait_ge(order, 2 * C + 1)
                            flat_kd = flat(kd[:, :, :])
                            for t in range(TT):
                                last = pe.transpose(k.ps[:, 3, t * P:(t + 1) * P], flat_kd[:, t * P:(t + 1) * P],
                                                    k.ident[:, :])
                            last.then_inc(turned, 1)
                        if n >= KV:
                            keys_times_values(n - KV)
                    add_within(C - 1)
                    for u in range(C - KV, 2 * TT):
                        keys_times_values(u)
                    pe.wait_ge(decayed, C)
                    for c in range(NCH):
                        if c % 4 == 0:
                            pe.wait_ge(carried, min(c + 4, NCH))
                        last = pe.matmul(out[:, c, :], state[:, c, :], q[:, C % 2, c, :], start=False,
                                         stop=c == NCH - 1, skip_group_check=True)
                    last.then_inc(outed, 1)
            output_projection(k, b, None, ws["Wo"], P, oT=oT, gain_row=k.row("L1_attn_gamma"),
                              offset_row=k.row("L1_attn_beta"),
                              before=(k.row("L1_attn_bo"), batch_tiles(k, b, rows)))



def l1_ffn(k):
    nc = k.nc
    NG = 16
    KEYS = 32
    QC = 4
    with ExitStack() as st:
        wq, down, up = (k.weight(n, st) for n in ("L1_ffn_Wq", "L1_ffn_expert_down", "L1_ffn_expert_up"))
        keys = k.weight("L1_sub_keys", st)
        pair_mean = k.const("pair_mean", st)
        group4 = k.const("group_of_32", st)
        xT = norm_all(k, st, twice=False,
                      load=(wq, down, up, keys, pair_mean, group4))
        q = k.sb("queries_T", [P, QC, B * T], st)
        stat = k.sb("query_stat", [P, B * QC, 6], st)
        mv = k.sb("query_mv", [P, 2], st)
        col = k.sb("query_columns", [P, 8], st)
        with signals(nc, "squared", "summed", "floored", "inverted", "unit") as (
                squared, summed, floored, inverted, unit), ExitStack() as ks, nc.Block() as block:
            k2 = k.sb("keys_squared", [P, 3, P], ks)

            @block.vector
            def _(dve):
                dve.tensor_tensor(k2[:, 0, :], keys[:, 0, :], keys[:, 0, :], ALU.mult).then_inc(squared, 1)
                dve.wait_ge(summed, 1)
                dve.tensor_scalar(k2[:, 1, :], k.ps[:, 0, 0:P], 1e-24, None, ALU.max).then_inc(floored, 1)
                dve.wait_ge(inverted, 1)
                dve.tensor_tensor(keys[:, 0, :], keys[:, 0, :], k2[:, 2, :], ALU.mult).then_inc(unit, 1)

            @block.tensor
            def _(pe):
                pe.wait_ge(squared, 1)
                pe.matmul(k.ps[:, 0, 0:P], k.ones[:, :], k2[:, 0, :], start=True, stop=True).then_inc(summed, 1)

            @block.gpsimd
            def _(pool):
                pool.wait_ge(floored, 1)
                pool.tensor_tensor(k2[:, 2, :], k2[:, 1, :], k.half[:, 0:1].to_broadcast([P, P]),
                                   ALU.pow).then_inc(inverted, 1)

        with nc.Fori(0, B) as b:
            project(k, [Product(q[:, c, bass.ds(b * T, T)],
                                [(wq[:, i, c * P:(c + 1) * P], xT[:, i, bass.ds(b * T, T)]) for i in range(KC)],
                                P, T, add=k.vec("L1_ffn_bq")[:, c:c + 1],
                                stats=stat[:, bass.ds(b * QC + c, 1), :].rearrange("p o s -> p (o s)"))
                        for c in range(QC)])

        with signals(nc, "order", "aggregated", "averaged", "deviated", "spread", "shifted", "inverted") as (
                order, aggregated, averaged, deviated, spread, shifted, inverted), nc.Block() as block:
            @block.vector
            def _(dve):
                o = Order(dve, order)
                dve.bn_aggr(mv[:, :], stat[:, :, :].rearrange("p a s -> p (a s)")).then_inc(aggregated, 1)
                dve.wait_ge(averaged, 1)
                o.do(dve.tensor_copy(col[:, 0:2], k.ps[:, 0, 0:2]))
                dve.wait_ge(aggregated, 1)
                o.do(dve.tensor_tensor(col[:, 2:3], mv[:, 0:1], col[:, 0:1], ALU.subtract))
                o.do(dve.tensor_tensor(col[:, 3:4], col[:, 2:3], col[:, 2:3], ALU.mult))
                dve.tensor_copy(col[:, 2:3], col[:, 3:4]).then_inc(deviated, 1)
                dve.wait_ge(spread, 1)
                dve.tensor_tensor(col[:, 4:5], k.ps[:, 1, 0:1], col[:, 1:2], ALU.add).then_inc(deviated, 1)
                dve.wait_ge(inverted, 1)
                o.do(dve.tensor_tensor(col[:, 6:7], col[:, 5:6], k.vec("L1_bn_gamma2"), ALU.mult))
                o.do(dve.tensor_tensor(col[:, 7:8], col[:, 0:1], col[:, 6:7], ALU.mult))
                o.do(dve.tensor_tensor(col[:, 7:8], k.vec("L1_bn_beta2"), col[:, 7:8], ALU.subtract))

            @block.tensor
            def _(pe):
                pe.wait_ge(aggregated, 1)
                pe.matmul(k.ps[:, 0, 0:2], pair_mean[:, :], mv[:, :], start=True, stop=True).then_inc(averaged, 1)
                pe.wait_ge(deviated, 1)
                pe.matmul(k.ps[:, 1, 0:2], pair_mean[:, :], col[:, 2:4], start=True, stop=True).then_inc(spread, 1)

            @block.gpsimd
            def _(pool):
                pool.wait_ge(deviated, 2)
                pool.tensor_scalar(col[:, 5:6], col[:, 4:5], EPS, 1.0, ALU.add, ALU.mult).then_inc(shifted, 1)
                pool.wait_ge(shifted, 1)
                pool.tensor_tensor(col[:, 5:6], col[:, 5:6], k.half[:, 0:1], ALU.pow).then_inc(inverted, 1)

        qn = k.sb("queries_normed", [P, QC, T], st)
        sq = k.sb("queries_squared", [P, QC, T], st)
        gel = k.sb("expert_hidden", [P, TT, D], st)
        s = k.sb("key_scores", [P, TT, NG, KEYS + 4], st)
        marked = k.sb("key_marked", [P, 2, NG, KEYS + 4], st)
        top = k.sb("key_top", [P, TT, NG, 8], st)
        e = k.sb("key_exp", [P, TT, NG, KEYS], st)
        m = k.sb("key_mask", [P, TT, NG, KEYS], st)
        nrm = k.sb("query_norms", [P, TT, 2, NG], st)
        tot = k.sb("key_sums", [P, TT, 2, NG], st)
        pairs = k.sb("pair_weights", [P, 2, 8, D], st)
        w = k.sb("expert_weights", [P, TT, D], st)
        wt = k.sb("expert_weights_T", [P, KC, T], st)
        far = k.sb("far_weight", [P, TT], st)
        x_ = None
        with signals(nc, "sentinels") as (sentinels,), nc.Block() as block:
            @block.vector
            def _(dve):
                dve.memset(s[:, :, :, KEYS:KEYS + 4], BIG).then_inc(sentinels, 1)
        with nc.Fori(0, B) as b:
            x_ = batch_tiles(k, b)
            with signals(nc, "batch_picked", "q_normed", "dve_q_normed", "q_squared", "squares_summed", "hid_made", "gelued", "scored", "floored", "inverted",
                         "scaled", "topped", "marked", "masked", "below", "exped", "order", "shared", "paired",
                         "summed", "weighted", "turned", "moved", "made", "added") as (
                    batch_picked, q_normed, dve_q_normed, q_squared, squares_summed, hid_made, gelued, scored, floored, inverted, scaled, topped, marked_s,
                    masked, below, exped, order, shared, paired, summed, weighted, turned, moved, made,
                    added), nc.Block() as block:
                score_bank = lambda t: (0, 1, 3, 0)[t]

                @block.scalar
                def _(act):
                    for c in (1, 3):
                        act.activation(qn[:, c, :], q[:, c, bass.ds(b * T, T)], ACT.Identity, bias=col[:, 7:8],
                                       scale=col[:, 6:7]).then_inc(q_normed, 1)
                    for t in range(TT):
                        act.wait_ge(hid_made, t + 1)
                        act.activation(gel[:, t, :], k.ps[:, 4 + t, 0:D], ACT.Gelu).then_inc(gelued, 1)
                    for t in range(TT):
                        act.wait_ge(below, t + 1)
                        act.activation(e[:, t, :, :], e[:, t, :, :], ACT.Exp).then_inc(exped, 1)
                    for c in range(KC):
                        act.wait_ge(turned, c + 1)
                        act.copy(wt[:, c, :], k.ps[:, c, :]).then_inc(moved, 1)

                @block.tensor
                def _(pe):
                    def scores(t):
                        if t >= 3:
                            pe.wait_ge(scaled, t - 2)
                        for c in range(QC):
                            last = pe.matmul(k.ps[:, score_bank(t), c * P:(c + 1) * P],
                                             qn[:, c, t * P:(t + 1) * P], keys[:, 0, :], start=True, stop=True)
                        last.then_inc(scored, 1)

                    pe.wait_ge(q_squared, QC)
                    for t in range(TT):
                        for c in range(QC):
                            last = pe.matmul(k.ps[:, 2, NG * t + 4 * c:NG * t + 4 * c + 4],
                                             sq[:, c, t * P:(t + 1) * P], group4[:, :], start=True, stop=True)
                    last.then_inc(squares_summed, 1)
                    pe.wait_ge(q_normed, 2)
                    pe.wait_ge(dve_q_normed, 2)
                    for t in range(3):
                        scores(t)
                    pe.wait_ge(batch_picked, KC)
                    for t in range(TT):
                        for c in range(KC):
                            last = pe.matmul(k.ps[:, 4 + t, 0:D], k.xnT[:, c, t * P:(t + 1) * P], down[:, c, :],
                                             start=c == 0, stop=c == KC - 1)
                        last.then_inc(hid_made, 1)
                    scores(3)
                    pe.wait_ge(weighted, TT)
                    for c in range(KC):
                        for t in range(TT):
                            last = pe.transpose(k.ps[:, c, t * P:(t + 1) * P], w[:, t, c * P:(c + 1) * P],
                                                k.ident[:, :])
                        last.then_inc(turned, 1)
                    pe.wait_ge(moved, KC)
                    for t in range(TT):
                        for c in range(KC):
                            last = pe.matmul(k.ps[:, 4 + t, 0:D], wt[:, c, t * P:(t + 1) * P], up[:, c, :],
                                             start=c == 0, stop=c == KC - 1)
                        last.then_inc(made, 1)

                @block.gpsimd
                def _(pool):
                    pool.wait_ge(floored, 1)
                    for t in range(TT):
                        pool.tensor_tensor(nrm[:, t, 1, :], nrm[:, t, 0, :], k.half[:, 0:NG],
                                           ALU.pow).then_inc(inverted, 1)
                    for t in range(TT):
                        pool.wait_ge(shared, t + 1)
                        if t >= 2:
                            pool.wait_ge(summed, t - 1)
                        halves = e[:, t, :, :].rearrange("p (h s) n -> p h s n", s=2)
                        for h in range(8):
                            last = pool.tensor_tensor(
                                pairs[:, t % 2, h, :].rearrange("p (a c) -> p a c", a=8),
                                halves[:, h, 0, 0:8].unsqueeze(2).to_broadcast([P, 8, KEYS]),
                                halves[:, h, 1, :].unsqueeze(1).to_broadcast([P, 8, KEYS]), ALU.mult)
                            last.then_inc(paired, 1)

                @block.vector
                def _(dve):
                    o = Order(dve, order)
                    for c in (0, 2):
                        dve.tensor_scalar(qn[:, c, :], q[:, c, bass.ds(b * T, T)], col[:, 6:7], col[:, 7:8],
                                          ALU.mult, ALU.add).then_inc(dve_q_normed, 1)
                    dve.wait_ge(dve_q_normed, 2)
                    for c in (0, 2, 1, 3):
                        if c == 1:
                            dve.wait_ge(q_normed, 2)
                        dve.tensor_tensor(sq[:, c, :], qn[:, c, :], qn[:, c, :], ALU.mult).then_inc(q_squared, 1)
                    pick_batch(dve, xT, b, k.xnT, batch_picked)
                    dve.wait_ge(squares_summed, 1)
                    dve.tensor_scalar(nrm[:, :, 0, :], k.ps[:, 2, 0:TT * NG].rearrange("p (t g) -> p t g", t=TT),
                                      1e-24, None, ALU.max).then_inc(floored, 1)

                    def best_four(t):
                        dve.wait_ge(scored, t + 1)
                        dve.wait_ge(inverted, t + 1)
                        dve.tensor_tensor(s[:, t, :, 0:KEYS],
                                          k.ps[:, score_bank(t), :].rearrange("p (g n) -> p g n", g=NG),
                                          nrm[:, t, 1, :].unsqueeze(2).to_broadcast([P, NG, KEYS]),
                                          ALU.mult).then_inc(scaled, 1)
                        dve.wait_ge(scaled, t + 1)
                        for g in range(NG):
                            dve.max(top[:, t, g, :], s[:, t, g, :]).then_inc(topped, 1)
                        dve.wait_ge(topped, NG * (t + 1))
                        o.do(dve.tensor_tensor(e[:, t, :, :], s[:, t, :, 0:KEYS],
                                               top[:, t, :, 4:5].to_broadcast([P, NG, KEYS]), ALU.subtract))
                        dve.tensor_scalar(e[:, t, :, :], e[:, t, :, :], 0.0, None, ALU.min).then_inc(below, 1)
                        if t >= 2:
                            dve.wait_ge(masked, t - 1)
                        for g in range(NG):
                            dve.match_replace(marked[:, t % 2, g, :], top[:, t, g, :], s[:, t, g, :],
                                              -BIG).then_inc(marked_s, 1)
                        dve.wait_ge(marked_s, NG * (t + 1))
                        dve.tensor_scalar(m[:, t, :, :], marked[:, t % 2, :, 0:KEYS], -BIG, None,
                                          ALU.is_equal).then_inc(masked, 1)

                    def share(t):
                        dve.wait_ge(exped, t + 1)
                        dve.wait_ge(masked, t + 1)
                        o.do(dve.tensor_tensor(e[:, t, :, :], e[:, t, :, :], m[:, t, :, :], ALU.mult))
                        o.do(dve.reduce_sum(tot[:, t, 0, :], e[:, t, :, :], AX.X))
                        o.do(dve.reciprocal(tot[:, t, 1, :], tot[:, t, 0, :]))
                        dve.tensor_tensor(e[:, t, :, :], e[:, t, :, :],
                                          tot[:, t, 1, :].unsqueeze(2).to_broadcast([P, NG, KEYS]),
                                          ALU.mult).then_inc(shared, 1)
                        dve.wait_ge(shared, t + 1)
                        o.mark(dve.tensor_reduce(far[:, t:t + 1], e[:, t, :, :].rearrange(
                            "p (h s) n -> p h s n", s=2)[:, :, 0, 8:KEYS], AX.XY, ALU.add))

                    def weigh(t):
                        dve.wait_ge(paired, 8 * (t + 1))
                        dve.tensor_reduce(w[:, t, :], pairs[:, t % 2, :, :].rearrange("p h n -> p n h"), AX.X,
                                          ALU.add).then_inc(summed, 1)
                        dve.wait_ge(summed, t + 1)
                        o.wait()
                        o.do(dve.tensor_tensor(w[:, t, D - 1:D], w[:, t, D - 1:D], far[:, t:t + 1], ALU.add))
                        dve.wait_ge(gelued, t + 1)
                        dve.tensor_tensor(w[:, t, :], w[:, t, :], gel[:, t, :], ALU.mult).then_inc(weighted, 1)

                    best_four(0)
                    for t in range(TT):
                        share(t)
                        if t + 1 < TT:
                            best_four(t + 1)
                        if t >= 1:
                            weigh(t - 1)
                    weigh(TT - 1)
                    for t in range(TT):
                        dve.wait_ge(made, t + 1)
                        dve.tensor_tensor(x_(t), x_(t), k.ps[:, 4 + t, 0:D], ALU.add).then_inc(added, 1)



def l3_attn(k):
    nc = k.nc
    S = B
    with ExitStack() as st:
        ws = {n: k.weight("L3_attn_" + n, st) for n in ("w_q", "w_k", "w_v", "w_o")}
        rk, rv = k.const("rel_k_rows", st), k.const("rel_v_rows", st)
        xT = norm_all(k, st, twice=False,
                      load=[*ws.values(), rk, rv])
        qkv = [k.sb(n, [P, S, TT, D], st) for n in ("queries", "keys", "values")]
        out = k.sb("attended", [P, S, TT, D], st)
        with nc.Fori(0, B) as b:
            project(k, [Product(dst[:, bass.ds(b, 1), t, :].rearrange("p o d -> p (o d)"),
                                [(k.xnT[:, i, t * P:(t + 1) * P], ws[n][:, i, :]) for i in range(KC)], P, D)
                        for n, dst in zip(("w_q", "w_k", "w_v"), qkv) for t in range(TT)], batch=(xT, b))
        qq = k.sb("queries_tile", [P, S, D], st)
        kk = k.sb("keys_relative", [P, 2, S, D], st)
        vv = k.sb("values_relative", [P, 2, S, D], st)
        prod = k.sb("products", [P, 2, S, D], st)
        sc = k.sb("scores", [P, S * S, 16], st)
        red = k.sb("reduced", [P, 3, S * S], st)
        with nc.Fori(0, TT) as j, signals(nc, "keyed", "valued", "multiplied", "weighted", "order", "exped",
                                          "below", "stored") as (
                keyed, valued, multiplied, weighted, order, exped, below, stored), nc.Block() as block:
            q, kt, v = (w[:, :, bass.ds(j, 1), :].rearrange("p s o d -> p s (o d)") for w in qkv)

            @block.gpsimd
            def _(pool):
                for s in range(S):
                    if s >= 2:
                        pool.wait_ge(multiplied, s - 1)
                    pool.tensor_tensor(kk[:, s % 2, :, :], kt, rk[:, S - 1 - s:2 * S - 1 - s, :],
                                       ALU.add).then_inc(keyed, 1)
                for s in range(S):
                    if s >= 2:
                        pool.wait_ge(weighted, s - 1)
                    pool.tensor_tensor(vv[:, s % 2, :, :], v, rv[:, S - 1 - s:2 * S - 1 - s, :],
                                       ALU.add).then_inc(valued, 1)

            @block.scalar
            def _(act):
                act.wait_ge(below, 1)
                act.activation(sc[:, :, :], sc[:, :, :], ACT.Exp, scale=0.25).then_inc(exped, 1)

            @block.vector
            def _(dve):
                o = Order(dve, order)
                o.do(dve.tensor_copy(qq[:, :, :], q))
                for s in range(S):
                    dve.wait_ge(keyed, s + 1)
                    dve.tensor_tensor(prod[:, s % 2, :, :], kk[:, s % 2, :, :],
                                      qq[:, s, :].unsqueeze(1).to_broadcast([P, S, D]),
                                      ALU.mult).then_inc(multiplied, 1)
                    dve.wait_ge(multiplied, s + 1)
                    o.do(dve.reduce_sum(sc[:, S * s:S * s + S, :], prod[:, s % 2, :, :].rearrange(
                        "p t (h d) -> p t h d", d=16), AX.X))
                o.do(dve.tensor_reduce(red[:, 0, :], sc[:, :, :], AX.X, ALU.max))
                dve.tensor_tensor(sc[:, :, :], sc[:, :, :],
                                  red[:, 0, :].unsqueeze(2).to_broadcast([P, S * S, 16]),
                                  ALU.subtract).then_inc(below, 1)
                dve.wait_ge(exped, 1)
                o.do(dve.reduce_sum(red[:, 1, :], sc[:, :, :], AX.X))
                o.do(dve.reciprocal(red[:, 2, :], red[:, 1, :]))
                o.do(dve.tensor_tensor(sc[:, :, :], sc[:, :, :],
                                       red[:, 2, :].unsqueeze(2).to_broadcast([P, S * S, 16]), ALU.mult))
                for s in range(S):
                    dve.wait_ge(valued, s + 1)
                    dve.tensor_tensor(prod[:, s % 2, :, :].rearrange("p t (h d) -> p (t h) d", d=16),
                                      vv[:, s % 2, :, :].rearrange("p t (h d) -> p (t h) d", d=16),
                                      sc[:, S * s:S * s + S, :].rearrange("p t h -> p (t h)").unsqueeze(2)
                                      .to_broadcast([P, S * 16, 16]), ALU.mult).then_inc(weighted, 1)
                    dve.wait_ge(weighted, s + 1)
                    dve.reduce_sum(out[:, s, bass.ds(j, 1), :].rearrange("p o d -> p (o d)"),
                                   prod[:, s % 2, :, :].rearrange("p t d -> p d t"), AX.X).then_inc(stored, 1)
        with nc.Fori(0, B) as b:
            with signals(nc, "picked") as (picked,), nc.Block() as block:
                @block.vector
                def _(dve):
                    dve.tensor_copy(k.xn[:, :, :], out[:, bass.ds(b, 1), :, :].rearrange("p o t d -> p (o t) d"))\
                        .then_inc(picked, 1)
            output_projection(k, b, k.xn, ws["w_o"], D, bias_row=k.row("L3_attn_b_o"))



E = 8


def top_two_gate(k, st, xT, router, from_sigmoid):
    nc = k.nc
    combT = k.sb("combine_T", [E, B * T], st)
    with ExitStack() as ts, signals(nc, "scored", "rowed", "picked", "exped", "combined", "turned", "ready",
                                    "order") as (
            scored, rowed, picked, exped, combined, turned, ready, order):
        row = k.sb("gate_row", [P, NT, 14], ts)
        marked = k.sb("gate_marked", [P, NT, 14], ts)
        top = k.sb("gate_top", [P, NT, 8], ts)
        mask = k.sb("gate_mask", [P, NT, E], ts)
        e = k.sb("gate_exp", [P, NT, E], ts)
        tot = k.sb("gate_total", [P, NT, 2], ts)
        comb = k.sb("gate_combine", [P, NT, E], ts)
        scores = k.ps[:, 7, 0:NT * E].rearrange("p (t e) -> p t e", t=NT)
        with nc.Block() as block:
            @block.sync
            def _(sp):
                k.wait_weights(sp, late=True)

            @block.vector
            def _(dve):
                o = Order(dve, order)
                o.do(dve.memset(row[:, :, E:14], BIG))
                dve.wait_ge(scored, 1)
                if not from_sigmoid:
                    dve.tensor_copy(row[:, :, 0:E], scores).then_inc(rowed, 1)
                dve.wait_ge(rowed, 1)
                for t in range(NT):
                    o.mark(dve.max(top[:, t, :], row[:, t, :]))
                o.wait()
                for t in range(NT):
                    o.mark(dve.match_replace(marked[:, t, :], top[:, t, :], row[:, t, :], -BIG))
                o.wait()
                o.do(dve.tensor_scalar(mask[:, :, :], marked[:, :, 0:E], -BIG, None, ALU.is_equal))
                if from_sigmoid:
                    o.do(dve.tensor_tensor(e[:, :, :], row[:, :, 0:E], mask[:, :, :], ALU.mult))
                else:
                    o.do(dve.tensor_tensor(e[:, :, :], row[:, :, 0:E], top[:, :, 6:7].to_broadcast([P, NT, E]),
                                           ALU.subtract))
                    dve.tensor_scalar(e[:, :, :], e[:, :, :], 0.0, None, ALU.min).then_inc(picked, 1)
                    dve.wait_ge(exped, 1)
                    o.do(dve.tensor_tensor(e[:, :, :], e[:, :, :], mask[:, :, :], ALU.mult))
                o.do(dve.reduce_sum(tot[:, :, 0], e[:, :, :], AX.X))
                if from_sigmoid:
                    o.do(dve.tensor_scalar(tot[:, :, 0], tot[:, :, 0], 1e-20, None, ALU.add))
                o.do(dve.reciprocal(tot[:, :, 1], tot[:, :, 0]))
                dve.tensor_tensor(comb[:, :, :], e[:, :, :], tot[:, :, 1:2].to_broadcast([P, NT, E]),
                                  ALU.mult).then_inc(combined, 1)

            @block.scalar
            def _(act):
                if from_sigmoid:
                    act.wait_ge(scored, 1)
                    act.activation(row[:, :, 0:E], scores, ACT.Sigmoid).then_inc(rowed, 1)
                else:
                    act.wait_ge(picked, 1)
                    act.activation(e[:, :, :], e[:, :, :], ACT.Exp).then_inc(exped, 1)
                for b in range(B):
                    act.wait_ge(turned, b + 1)
                    act.copy(combT[:, b * T:(b + 1) * T], k.ps[0:E, b, :]).then_inc(ready, 1)

            @block.tensor
            def _(pe):
                for t in range(NT):
                    for c in range(KC):
                        last = pe.matmul(scores[:, t, :], xT[:, c, t * P:(t + 1) * P], router[:, c, :],
                                         start=c == 0, stop=c == KC - 1)
                last.then_inc(scored, 1)
                pe.wait_ge(combined, 1)
                for t in range(NT):
                    last = pe.transpose(k.ps[0:E, t // TT, (t % TT) * P:(t % TT + 1) * P], comb[:, t, :],
                                        k.ident[:, :])
                    if t % TT == TT - 1:
                        last.then_inc(turned, 1)
    return combT


def l2_ffn(k):
    nc = k.nc
    HC = 3072 // P
    expert_of = [n // 2 if n < 8 else 4 + (n - 8) // 4 for n in range(HC)]
    R = 4
    with ExitStack() as st:
        router = k.weight("L2_ffn_router_w", st)
        w1 = k.weight("L2_ffn_w1", st)
        w2 = k.weight("L2_ffn_w2", st)
        sel = k.const("select8", st)
        xT = norm_all(k, st, twice=False,
                      load=(router,), later=(sel, w1, w2))
        relu = k.sb("relu", [P, R, T], st)
        rw = k.sb("relu_weighted", [P, R, T], st)
        hT = k.sb("hidden_T", [P, R, T], st)
        wb = k.sb("expert_weight", [P, E, T], st)
        combT = top_two_gate(k, st, xT, router, True)
        with nc.Fori(0, B) as b, signals(
                nc, "batch_picked", "spread", "spread_copied", "up", "relued", "weighted", "squared",
                "consumed", "added") as (batch_picked, spread, spread_copied, up, relued, weighted, squared,
                                         consumed, added):
            x = batch_tiles(k, b)
            with nc.Block() as block:
                @block.vector
                def _(dve):
                    pick_batch(dve, xT, b, k.xnT, batch_picked)
                    for n in range(HC):
                        dve.wait_ge(weighted, n + 1)
                        if n >= R:
                            dve.wait_ge(consumed, n - R + 1)
                        dve.tensor_tensor(hT[:, n % R, :], relu[:, n % R, :], rw[:, n % R, :],
                                          ALU.mult).then_inc(squared, 1)
                    dve.wait_ge(consumed, HC)
                    for t in range(TT):
                        dve.tensor_tensor(x(t), x(t), k.ps[:, t, 0:D], ALU.add).then_inc(added, 1)

                @block.gpsimd
                def _(pool):
                    for n in range(HC):
                        pool.wait_ge(relued, n + 1)
                        pool.wait_ge(spread_copied, expert_of[n] + 1)
                        if n >= R:
                            pool.wait_ge(squared, n - R + 1)
                        pool.tensor_tensor(rw[:, n % R, :], relu[:, n % R, :], wb[:, expert_of[n], :],
                                           ALU.mult).then_inc(weighted, 1)

                @block.scalar
                def _(act):
                    for e in range(E):
                        act.wait_ge(spread, e + 1)
                        act.copy(wb[:, e, :], k.ps[:, 4 + e % 2, :]).then_inc(spread_copied, 1)
                    for n in range(HC):
                        act.wait_ge(up, n + 1)
                        if n >= R:
                            act.wait_ge(squared, n - R + 1)
                        act.activation(relu[:, n % R, :], k.ps[:, 4 + n % 4, :], ACT.Relu).then_inc(relued, 1)

                @block.tensor
                def _(pe):
                    for e in range(E):
                        if e >= 2:
                            pe.wait_ge(spread_copied, e - 1)
                        pe.matmul(k.ps[:, 4 + e % 2, :], sel[:, e, :], combT[:, bass.ds(b * T, T)], start=True,
                                  stop=True).then_inc(spread, 1)
                    pe.wait_ge(spread_copied, E)
                    pe.wait_ge(batch_picked, KC)

                    def product_down(n):
                        pe.wait_ge(squared, n + 1)
                        for t in range(TT):
                            last = pe.matmul(k.ps[:, t, 0:D], hT[:, n % R, t * P:(t + 1) * P], w2[:, n, :],
                                             start=n == 0, stop=n == HC - 1)
                        last.then_inc(consumed, 1)
                        return last

                    for n in range(HC):
                        if n >= 4:
                            pe.wait_ge(relued, n - 3)
                        for c in range(KC):
                            last = pe.matmul(k.ps[:, 4 + n % 4, :], w1[:, c, n * P:(n + 1) * P], k.xnT[:, c, :],
                                             start=c == 0, stop=c == KC - 1)
                        last.then_inc(up, 1)
                        if n >= 2:
                            product_down(n - 2)
                    product_down(HC - 2)
                    product_down(HC - 1)
                    

def l3_ffn(k):
    nc = k.nc
    HC = E * 512 // P
    R = 4
    with ExitStack() as st:
        router = k.weight("L3_ffn_Wg", st)
        w1 = k.weight("L3_ffn_W1", st)
        w2 = k.weight("L3_ffn_W2", st)
        w3 = k.weight("L3_ffn_W3", st)
        b3 = k.const("L3_ffn_b3", st)
        sel = k.const("select8", st)
        xT = norm_all(k, st, twice=False,
                      load=(router,), later=(b3, sel, w1, w2, w3))
        b1, b2 = k.vec("L3_ffn_b1"), k.vec("L3_ffn_b2")
        silu = k.sb("silu", [P, R, T], st)
        gv = k.sb("gated", [P, R, T], st)
        hT = k.sb("hidden_T", [P, R, T], st)
        wb = k.sb("expert_weight", [P, 2, T], st)
        combT = top_two_gate(k, st, xT, router, False)
        combTb = k.sb("combine_T_batch", [E, T], st)
        with nc.Fori(0, B) as b, signals(
                nc, "batch_picked", "comb_picked", "spread", "spread_copied", "up_g", "up_v", "silued", "gated",
                "weighted", "consumed", "added") as (batch_picked, comb_picked, spread, spread_copied, up_g, up_v,
                                                     silued, gated, weighted, consumed, added):
            x = batch_tiles(k, b)
            with nc.Block() as block:
                @block.vector
                def _(dve):
                    dve.tensor_copy(combTb[:, :], combT[:, bass.ds(b * T, T)]).then_inc(comb_picked, 1)
                    pick_batch(dve, xT, b, k.xnT, batch_picked)
                    for n in range(HC):
                        dve.wait_ge(up_v, n + 1)
                        dve.wait_ge(silued, n + 1)
                        if n >= R:
                            dve.wait_ge(weighted, n - R + 1)
                        dve.scalar_tensor_tensor(out=gv[:, n % R, :], in0=k.ps[:, 5 + 2 * (n % 2), :],
                                                 scalar=b2[:, n:n + 1], in1=silu[:, n % R, :], op0=ALU.add,
                                                 op1=ALU.mult).then_inc(gated, 1)
                    dve.wait_ge(consumed, HC)
                    for t in range(TT):
                        dve.tensor_tensor(x(t), x(t), k.ps[:, t, 0:D], ALU.add).then_inc(added, 1)

                @block.gpsimd
                def _(pool):
                    for n in range(HC):
                        pool.wait_ge(gated, n + 1)
                        pool.wait_ge(spread_copied, n // 4 + 1)
                        if n >= R:
                            pool.wait_ge(consumed, n - R + 1)
                        pool.tensor_tensor(hT[:, n % R, :], gv[:, n % R, :], wb[:, (n // 4) % 2, :],
                                           ALU.mult).then_inc(weighted, 1)

                @block.scalar
                def _(act):
                    for n in range(HC):
                        if n % 4 == 0:
                            e = n // 4
                            act.wait_ge(spread, e + 1)
                            if e >= 2:
                                act.wait_ge(weighted, 4 * (e - 1))
                            act.copy(wb[:, e % 2, :], k.ps[:, 7, :]).then_inc(spread_copied, 1)
                        act.wait_ge(up_g, n + 1)
                        if n >= R:
                            act.wait_ge(gated, n - R + 1)
                        act.activation(silu[:, n % R, :], k.ps[:, 4 + 2 * (n % 2), :], ACT.Silu,
                                       bias=b1[:, n:n + 1]).then_inc(silued, 1)

                @block.tensor
                def _(pe):
                    pe.wait_ge(comb_picked, 1)
                    for t in range(TT):
                        pe.matmul(k.ps[:, t, 0:D], combTb[:, t * P:(t + 1) * P], b3[:, :], start=True, stop=False)

                    def product_down(n):
                        pe.wait_ge(weighted, n + 1)
                        for t in range(TT):
                            last = pe.matmul(k.ps[:, t, 0:D], hT[:, n % R, t * P:(t + 1) * P], w3[:, n, :],
                                             start=False, stop=n == HC - 1)
                        last.then_inc(consumed, 1)

                    for n in range(HC):
                        if n >= 2:
                            pe.wait_ge(silued, n - 1)
                            pe.wait_ge(gated, n - 1)
                        if n % 4 == 0:
                            if n:
                                pe.wait_ge(gated, n)
                            pe.matmul(k.ps[:, 7, :], sel[:, n // 4, :], combTb[:, :], start=True,
                                      stop=True).then_inc(spread, 1)
                        if n == 0:
                            pe.wait_ge(batch_picked, KC)
                        for bank, w, sem in ((4, w1, up_g), (5, w2, up_v)):
                            bank += 2 * (n % 2)
                            if bank == 7:
                                pe.wait_ge(spread_copied, n // 4 + 1)
                            for c in range(KC):
                                last = pe.matmul(k.ps[:, bank, :], w[:, c, n * P:(n + 1) * P], k.xnT[:, c, :],
                                                 start=c == 0, stop=c == KC - 1)
                            last.then_inc(sem, 1)
                        if n >= 2:
                            product_down(n - 2)
                    product_down(HC - 2)
                    product_down(HC - 1)



STAGES = [None] * 12
STAGES[0] = l0_attn
STAGES[1] = l0_xattn
STAGES[2] = l0_ffn
STAGES[3] = l1_attn
STAGES[5] = l1_ffn
STAGES[9] = l3_attn
STAGES[4] = l1_xattn
STAGES[6] = l2_attn
STAGES[7] = l2_xattn
STAGES[10] = l3_xattn
STAGES[8] = l2_ffn
STAGES[11] = l3_ffn

VECS = ["L1_attn_bq", "L1_attn_bk", "L1_attn_bg", "L1_ffn_bq", "L1_bn_gamma2", "L1_bn_beta2", "L0_xattn_bq", "L0_xattn_bk", "L2_attn_bq", "L2_attn_bk", "L2_scale", "L2_query_gain", "L2_xattn_kn_g2",
        "L3_query_gain", "L3_xattn_k_scale2"] + [
    p + n for p, ns in (("L1_xattn_", ("ln_l_g", "ln_l_b", "ln_m_g", "ln_m_b")),
                        ("L2_xattn_", ("ln_l_g", "ln_l_b", "ln_x_g", "ln_x_b")),
                        ("L3_xattn_", ("ln_l_w", "ln_l_b", "ln_x_w", "ln_x_b"))) for n in ns] + [
        "L0_freq", "L0_decay", "re_im_sign", "half_pi", "L0_attn_n1_g", "L0_attn_n1_b", "L0_attn_n2_g",
        "L0_attn_n2_b", "L0_attn_mlp_b1", "L3_ffn_b1", "L3_ffn_b2",
        "L0_ffn_ln1_g", "L0_ffn_ln1_b", "L0_ffn_ln2_g", "L0_ffn_ln2_b"]
ROWS = ["L1_attn_bv", "L1_attn_bo", "L1_attn_gamma", "L1_attn_beta", "L3_attn_b_o", "L0_xattn_bv", "L0_xattn_bo", "L2_attn_bv", "L2_attn_bo", "L2_xattn_bout", "L3_xattn_ln_o_w",
        "L3_xattn_ln_o_b", "L0_attn_gate_b", "L0_attn_mlp_b2", "L0_ffn_b1", "L0_ffn_b2"]
WEIGHTS = {"L0_ffn_w1": "T", "L0_ffn_w2": "T", "L2_ffn_router_w": "T", "L2_ffn_w1": "", "L2_ffn_w2": "",
           "L0_in": "", "L0_attn_out_proj_w": "T", "L0_coupling": "", "L0_attn_gate_w": "T",
           "L0_attn_mlp_w1": "T", "L0_attn_mlp_w2": "T", "L3_ffn_Wg": "T", "L3_ffn_W1": "T", "L3_ffn_W2": "T",
           "L3_ffn_W3": "", "L1_ffn_Wq": "", "L1_ffn_expert_down": "T", "L1_ffn_expert_up": "", "L1_sub_keys": "",
           **{"L1_attn_" + n: "" for n in ("Wq", "Wk", "Wv", "Wg", "Wo")},
           **{"L3_attn_" + n: "T" for n in ("w_q", "w_k", "w_v", "w_o")},
           "ctx_T": "", "L0_side": "", "mask_bf1": "", "mask_bk0": "",
           **{"L0_xattn_" + n: "" for n in ("wq", "wk", "wv", "wo")},
           **{"L2_attn_" + n: "T" for n in ("Wq", "Wk", "Wv", "Wo")},
           **{p + n: "" for p, o in (("L1_xattn_", "Wout"), ("L2_xattn_", "Wout"), ("L3_xattn_", "Wo"))
              for n in ("Wq", "Wkv", o)}}


def program(nc, dram, slots_v, slots_r):
    with ExitStack() as ctx:
        k = Core(nc, ctx, dram)
        k.slots_v, k.slots_r = slots_v, slots_r
        with signals(nc, "in_loaded", "consts_set") as (loaded, consts), nc.Block() as block:
            @block.sync
            def _(sp):
                sp.dma_start(k.x[:, :, :], dram["x"]).then_inc(loaded, 16)
                sp.dma_start(k.vecs[:, :], dram["vecs"]).then_inc(loaded, 16)
                sp.dma_start(k.rows[:, :], dram["rows"]).then_inc(loaded, 16)
                sp.dma_start(k.ident[:, :], dram["ident"]).then_inc(loaded, 16)
                sp.wait_ge(loaded, 64)

            @block.gpsimd
            def _(pool):
                pool.memset(k.ones[:, :], 1.0).then_inc(consts, 1)
                pool.memset(k.half[:, :], -0.5).then_inc(consts, 1)
                pool.wait_ge(consts, 2)

        with signals(nc, "folded") as (folded,), nc.Block() as block:
            @block.vector
            def _(dve):
                for name, c in (("L2_query_gain", 64 ** -0.5), ("L3_query_gain", 8.0)):
                    dve.tensor_scalar(k.vec(name), k.vec(name), c, None, ALU.mult).then_inc(folded, 1)

        for stage in STAGES[FIRST:LAST]:
            stage(k)

        with signals(nc, "out_stored") as (stored,), nc.Block() as block:
            @block.sync
            def _(sp):
                sp.dma_start(dram["out"], k.x[:, :, :]).then_inc(stored, 16)
                sp.wait_ge(stored, 16)


def words_of_bools(m):
    return np.broadcast_to(np.repeat(m.view(np.uint8).reshape(1, -1), 4, axis=1).view(np.int32), (P, m.size))


def lay_out(a, arrays):
    f = np.float32
    w = a["L0_attn_in_proj_w"].T
    a["L0_in"] = np.concatenate([w, w[:, 64:], w[:, :64]], axis=1)
    a["L0_freq"] = np.concatenate([a["L0_attn_frequency"]] * 2)
    a["L0_decay"] = np.concatenate([a["L0_attn_log_decay"]] * 2)
    a["re_im_sign"] = np.repeat(np.array([1, -1], f), 64)
    a["half_pi"] = np.full((P,), np.pi / 2, f)
    cp = np.zeros((P, 2 * P), f)
    for ri in range(2):
        for h in range(4):
            i = 64 * ri + 16 * h
            cp[i:i + 16, i:i + 16] = a["L0_attn_coupling"][h]
            j = P + 64 * (1 - ri) + 16 * h
            cp[i:i + 16, j:j + 16] = a["L0_attn_coupling"][h]
    a["L0_coupling"] = cp
    ctx = a["ctx_1024"]
    a["ctx_T"] = ctx.reshape(-1, D).T
    arrays["ctx_rows"] = np.ascontiguousarray(ctx.transpose(1, 0, 2))
    a["L0_side"] = np.broadcast_to(a["fside_BxS2_0"].reshape(1, -1), (P, B * 64))
    a["mask_bf1"] = words_of_bools(a["mask_BxS2_bf1"])
    a["mask_bk0"] = words_of_bools(a["mask_BxS2_bk0"])
    arrays["head_mask8"] = np.repeat(np.eye(8, dtype=f), 16, axis=0)
    q, c = np.arange(P)[:, None], np.arange(P)[None, :]
    hidden = (q // 64 > c // 64) | ((q // 64 == c // 64) & (c > q))
    arrays["block_mask"] = np.where(hidden, f(-1e30), f(0))
    a["L2_scale"] = np.broadcast_to(a["L2_attn_attn_scale"], (P,))
    a["L2_query_gain"] = np.tile(a["L2_xattn_qn_g"], 2)
    a["L2_xattn_kn_g2"] = np.tile(a["L2_xattn_kn_g"], 2)
    a["L3_query_gain"] = np.tile(a["L3_xattn_q_scale"], 2)
    a["L3_xattn_k_scale2"] = np.tile(a["L3_xattn_k_scale"], 2)
    arrays["chunk_diagonal"] = np.eye(T // 16, dtype=f)
    arrays["pair_mean"] = np.tile(np.eye(64, dtype=f) * f(0.5), (2, 2))
    arrays["group_of_32"] = np.repeat(np.eye(4, dtype=f), 32, axis=0)
    sk = np.zeros((P, P), f)
    for i in range(4):
        sk[32 * i:32 * i + 32, 32 * i:32 * i + 32] = a["L1_ffn_sub_key%d" % (i % 2)].T
    a["L1_sub_keys"] = sk
    a["L1_bn_gamma2"] = np.tile(a["L1_ffn_bn_gamma"], 2)
    a["L1_bn_beta2"] = np.tile(a["L1_ffn_bn_beta"], 2)
    for n in ("rel_k", "rel_v"):
        rel = np.tile(a["L3_attn_" + n][128 - 3:128 + 4][::-1], (1, 16))
        arrays[n + "_rows"] = np.ascontiguousarray(np.broadcast_to(rel[None], (P, 7, D)))
    arrays["counting"] = np.ascontiguousarray(np.broadcast_to(np.arange(T, dtype=f)[None], (P, T)))
    arrays["select8"] = np.ascontiguousarray(np.repeat(np.eye(E, dtype=f)[:, :, None], P, axis=2))
    for n in ("L3_ffn_W1", "L3_ffn_W2"):
        a[n] = a[n].reshape(-1, D)
    a["L3_ffn_W3"] = a["L3_ffn_W3"].transpose(0, 2, 1).reshape(-1, D)
    arrays["L3_ffn_b3"] = a["L3_ffn_b3"]


def kernel(**inputs):
    import concourse.bacc as _bacc
    from concourse.bass_utils import run_bass_kernel_spmd as _run

    nc = _bacc.Bacc("TRN2", target_bir_lowering=False, num_devices=1)
    a = {n: np.asarray(v) for n, v in inputs.items()}
    arrays = {"x": np.ascontiguousarray(a["x"].reshape(NT, P, D).transpose(1, 0, 2))}
    lay_out(a, arrays)
    slots_v, slots_r, at = {}, {}, 0
    for n in VECS:
        slots_v[n] = (at, at + a[n].size // P)
        at += a[n].size // P
    arrays["vecs"] = np.ascontiguousarray(np.concatenate([a[n].reshape(-1, P).T for n in VECS], axis=1))
    at = 0
    for n in ROWS:
        slots_r[n] = (at, at + a[n].size)
        at += a[n].size
    arrays["rows"] = np.ascontiguousarray(
        np.broadcast_to(np.concatenate([a[n].reshape(-1) for n in ROWS])[None, :], (P, at)))
    arrays["ident"] = np.eye(P, dtype=np.float32)
    for n, how in WEIGHTS.items():
        w = a[n].T if how == "T" else a[n]
        arrays[n] = np.ascontiguousarray(w.reshape(w.shape[0] // P, P, w.shape[1]).transpose(1, 0, 2))
    dram = {n: nc.dram_tensor("in_" + n, v.shape, mybir.dt.from_np(v.dtype), kind="ExternalInput").ap()
            for n, v in arrays.items()}
    dram["out"] = nc.dram_tensor("out_x", (P, NT, D), F32, kind="ExternalOutput").ap()
    program(nc, dram, slots_v, slots_r)
    r = _run(nc, [{"in_" + n: v for n, v in arrays.items()}], core_ids=[0])
    out = np.asarray(r.results[0]["out_x"])
    return out.transpose(1, 0, 2).reshape(B, T, D)
```
